# Optimizing a Trainium2 kernel written in Bass

```python
import numpy as np
import jax
import jax.numpy as jnp

def _softmax(x, axis=-1):
    return jax.nn.softmax(x, axis=axis)

def _gelu(x):
    return jax.nn.gelu(x, approximate=True)

def _silu(x):
    return jax.nn.silu(x)

def _sigmoid(x):
    return jax.nn.sigmoid(x)

def _layernorm(x, axis=-1, eps=1e-05):
    m = jnp.mean(x, axis=axis, keepdims=True)
    v = jnp.var(x, axis=axis, keepdims=True)
    return (x - m) / jnp.sqrt(v + eps)

def _scatter_add(tgt, idx, src, axis=0):
    return tgt.at[idx].add(src)

def _segment_sum(src, seg, n):
    return jax.ops.segment_sum(src, seg, n)
kernel_name = 'mk_xattn_seq_d4_seqx_r8_57d083'

def setup_inputs(seed: int=0):
    np.random.seed(seed)
    _w = jnp.asarray

    def _rec_inputs():
        import jax
        import jax.numpy as jnp
        _rk = jax.random.key(seed)
        x = -0.0005207 + 1.001 * jax.random.normal(jax.random.fold_in(_rk, 1), (4, 256, 256), jnp.float32)
        _lenS = 256 - jax.random.randint(jax.random.fold_in(_rk, 7), (4,), 0, max(1, 256 // 4) + 1, jnp.int32)
        _lenS2 = 256 - jax.random.randint(jax.random.fold_in(_rk, 8), (4,), 0, max(1, 256 // 4) + 1, jnp.int32)
        _ctx_2048P = jax.random.normal(jax.random.fold_in(_rk, 11), (4, 16, 256), jnp.float32)
        _ctx_2048c = jax.random.dirichlet(jax.random.fold_in(_rk, 511), 0.3 * jnp.ones((16,), jnp.float32), (4, 256))
        _ctx_2048t = jnp.einsum('bsk,bkd->bsd', _ctx_2048c, _ctx_2048P)
        _ctx_2048t = _ctx_2048t * jax.lax.rsqrt(jnp.mean(jnp.square(_ctx_2048t)) + 1e-12) * 0.953939
        ctx_2048 = 2.81802e-05 + 1.00001 * (_ctx_2048t + 0.3 * jax.random.normal(jax.random.fold_in(_rk, 611), (4, 256, 256), jnp.float32))
        _validS = jnp.arange(256)[None, :] < _lenS[:, None]
        _validS2 = jnp.arange(256)[None, :] < _lenS2[:, None]
        _causal = jnp.tril(jnp.ones((256, 256), dtype=bool))
        mask_BxS2_bf1 = jnp.ones((4, 256), dtype=bool)
        mask_Bx1xSxS2_ff0 = jnp.where(jnp.ones((4, 1, 256, 256), dtype=bool), 0.0, -1000000000.0).astype(jnp.float32)
        return (x, ctx_2048, mask_BxS2_bf1, mask_Bx1xSxS2_ff0)
    x, ctx_2048, mask_BxS2_bf1, mask_Bx1xSxS2_ff0 = _rec_inputs()

    def _L0_xattn_setup():
        import jax, jax.numpy as jnp
        import numpy as np
        B, Q, S1, S2 = (4, 32, 256, 256)
        D, H, K, F = (256, 16, 128, 1024)
        LN_EPS = 1e-05

        def _layer_norm(x, scale, offset):
            mu = jnp.mean(x, axis=-1, keepdims=True)
            var = jnp.var(x, axis=-1, keepdims=True)
            return (x - mu) * jax.lax.rsqrt(var + LN_EPS) * scale + offset

        def _cross_attention(q_in, kv_in, wq, bq, wk, bk, wv, bv, wo, bo, bias_k, bias_v):
            b, q_len, _ = q_in.shape
            t = kv_in.shape[1]
            qh = (q_in @ wq + bq).reshape(b, q_len, H, K)
            kh = (kv_in @ wk + bk).reshape(b, t, H, K)
            vh = (kv_in @ wv + bv).reshape(b, t, H, K)
            kh = jnp.concatenate([kh, jnp.broadcast_to(bias_k, (b, 1, H, K))], axis=1)
            vh = jnp.concatenate([vh, jnp.broadcast_to(bias_v, (b, 1, H, K))], axis=1)
            scale = jnp.sqrt(jnp.asarray(K, q_in.dtype))
            logits = jnp.einsum('bqhk,bthk->bhqt', qh, kh) / scale
            weights = jax.nn.softmax(logits, axis=-1)
            ctx = jnp.einsum('bhqt,bthk->bqhk', weights, vh).reshape(b, q_len, H * K)
            return ctx @ wo + bo

        def _forward(x, xf_1, xf_2, ln1_scale, ln1_offset, wq1, bq1, wk1, bk1, wv1, bv1, wo1, bo1, bias_k1, bias_v1, ln2_scale, ln2_offset, wq2, bq2, wk2, bk2, wv2, bv2, wo2, bo2, bias_k2, bias_v2, ln_mlp_scale, ln_mlp_offset, w_fc1, b_fc1, w_fc2, b_fc2):
            res = x
            h = _layer_norm(x, ln1_scale, ln1_offset)
            x = res + _cross_attention(h, xf_1, wq1, bq1, wk1, bk1, wv1, bv1, wo1, bo1, bias_k1, bias_v1)
            res = x
            h = _layer_norm(x, ln2_scale, ln2_offset)
            x = res + _cross_attention(h, xf_2, wq2, bq2, wk2, bk2, wv2, bv2, wo2, bo2, bias_k2, bias_v2)
            h = _layer_norm(x, ln_mlp_scale, ln_mlp_offset)
            h = jax.nn.gelu(h @ w_fc1 + b_fc1, approximate=False) @ w_fc2 + b_fc2
            return x + h
        key = jax.random.key(seed)
        ks = iter(jax.random.split(key, 64))

        def rn(shape, s=0.02):
            return jax.random.normal(next(ks), shape, jnp.float32) * s
        inp = {'x': rn((B, Q, D), 1.0), 'xf_1': rn((B, S1, D), 1.0), 'xf_2': rn((B, S2, D), 1.0)}
        for i in (1, 2):
            inp[f'ln{i}_scale'] = jnp.ones((D,), jnp.float32)
            inp[f'ln{i}_offset'] = jnp.zeros((D,), jnp.float32)
            inp[f'wq{i}'] = rn((D, H * K))
            inp[f'bq{i}'] = jnp.zeros((H * K,), jnp.float32)
            inp[f'wk{i}'] = rn((D, H * K))
            inp[f'bk{i}'] = jnp.zeros((H * K,), jnp.float32)
            inp[f'wv{i}'] = rn((D, H * K))
            inp[f'bv{i}'] = jnp.zeros((H * K,), jnp.float32)
            inp[f'wo{i}'] = rn((H * K, D))
            inp[f'bo{i}'] = jnp.zeros((D,), jnp.float32)
            inp[f'bias_k{i}'] = rn((1, 1, H, K))
            inp[f'bias_v{i}'] = rn((1, 1, H, K))
        inp['ln_mlp_scale'] = jnp.ones((D,), jnp.float32)
        inp['ln_mlp_offset'] = jnp.zeros((D,), jnp.float32)
        inp['w_fc1'] = rn((D, F))
        inp['b_fc1'] = jnp.zeros((F,), jnp.float32)
        inp['w_fc2'] = rn((F, D))
        inp['b_fc2'] = jnp.zeros((D,), jnp.float32)
        return inp
    _L0_xattn_all = _L0_xattn_setup()
    _L0_xattn_in = {k: v for k, v in _L0_xattn_all.items() if k in ('ln1_scale', 'ln1_offset', 'wq1', 'bq1', 'wk1', 'bk1', 'wv1', 'bv1', 'wo1', 'bo1', 'bias_k1', 'bias_v1', 'ln2_scale', 'ln2_offset', 'wq2', 'bq2', 'wk2', 'bk2', 'wv2', 'bv2', 'wo2', 'bo2', 'bias_k2', 'bias_v2', 'ln_mlp_scale', 'ln_mlp_offset', 'w_fc1', 'b_fc1', 'w_fc2', 'b_fc2')}
    del _L0_xattn_all

    def _L1_xattn_setup():
        import jax, jax.numpy as jnp
        import numpy as np
        B, L, E, H = (4, 64, 256, 32)
        S = E // H
        EXTRA_MAA, EXTRA_DECAY = (32, 64)
        EPS = 1e-05

        def _ln(x, w, b):
            m = jnp.mean(x, axis=-1, keepdims=True)
            v = jnp.mean((x - m) ** 2, axis=-1, keepdims=True)
            return (x - m) * jax.lax.rsqrt(v + EPS) * w + b

        def _token_shift(xn, prev_row):
            first = (prev_row - xn[:, 0])[:, None]
            rest = xn[:, :-1] - xn[:, 1:]
            return jnp.concatenate([first, rest], axis=1)
        key = jax.random.key(seed)
        ks = jax.random.split(key, 24)
        rn = lambda k, shp, s=1.0: jax.random.normal(k, shp, dtype=jnp.float32) * s
        return dict(x=rn(ks[0], (B, L, E)), state=rn(ks[1], (B, 2 + S, E), 0.1), ln1_w=jnp.ones((E,), jnp.float32), ln1_b=jnp.zeros((E,), jnp.float32), ln2_w=jnp.ones((E,), jnp.float32), ln2_b=jnp.zeros((E,), jnp.float32), maa_x=rn(ks[2], (E,), 0.02), maa_w1=rn(ks[3], (E, 5 * EXTRA_MAA), 0.02), maa_w2=rn(ks[4], (5, EXTRA_MAA, E), 0.02), maa_stack=rn(ks[5], (5, E), 0.02), time_decay=rn(ks[6], (E,), 0.5), decay_w1=rn(ks[7], (E, EXTRA_DECAY), 0.02), decay_w2=rn(ks[8], (EXTRA_DECAY, E), 0.02), faaaa=rn(ks[9], (H, S), 0.1), Wr=rn(ks[10], (E, E), 0.02), Wk=rn(ks[11], (E, E), 0.02), Wv=rn(ks[12], (E, E), 0.02), Wg=rn(ks[13], (E, E), 0.02), Wo=rn(ks[14], (E, E), 0.02), gn_w=jnp.ones((E,), jnp.float32), gn_b=jnp.zeros((E,), jnp.float32), ffn_maa_k=rn(ks[15], (E,), 0.02), ffn_maa_r=rn(ks[16], (E,), 0.02), ffn_Wk=rn(ks[17], (E, E), 0.02), ffn_Wr=rn(ks[18], (E, E), 0.02), ffn_Wv=rn(ks[19], (E, E), 0.02), i=0)
    _L1_xattn_all = _L1_xattn_setup()
    _L1_xattn_in = {k: v for k, v in _L1_xattn_all.items() if k in ('ln1_w', 'ln1_b', 'ln2_w', 'ln2_b', 'maa_x', 'maa_w1', 'maa_w2', 'maa_stack', 'time_decay', 'decay_w1', 'decay_w2', 'faaaa', 'Wr', 'Wk', 'Wv', 'Wg', 'Wo', 'gn_w', 'gn_b', 'ffn_maa_k', 'ffn_maa_r', 'ffn_Wk', 'ffn_Wr', 'ffn_Wv')}
    del _L1_xattn_all

    def _L2_xattn_setup():
        import jax, jax.numpy as jnp
        import numpy as np
        HIDDEN = 256
        HEADS = 16
        HEAD_DIM = HIDDEN // HEADS
        LN_EPS = 1e-05
        GATE_INIT = 0.5

        def _layer_norm(x, gamma, beta):
            mu = jnp.mean(x, axis=-1, keepdims=True)
            var = jnp.mean(jnp.square(x - mu), axis=-1, keepdims=True)
            return (x - mu) * jax.lax.rsqrt(var + LN_EPS) * gamma + beta
        key = jax.random.key(seed)
        ks = jax.random.split(key, 8)
        B, T_TEXT, T_AUDIO = (4, 256, 1500)
        s = 0.02
        return {'hidden_states': jax.random.normal(ks[0], (B, T_TEXT, HIDDEN), jnp.float32), 'audio_kv': jax.random.normal(ks[1], (B, T_AUDIO, HIDDEN), jnp.float32), 'audio_attention_mask': jnp.ones((B, T_AUDIO), dtype=bool), 'Wq': jax.random.normal(ks[2], (HIDDEN, HIDDEN), jnp.float32) * s, 'Wk': jax.random.normal(ks[3], (HIDDEN, HIDDEN), jnp.float32) * s, 'Wv': jax.random.normal(ks[4], (HIDDEN, HIDDEN), jnp.float32) * s, 'Wo': jax.random.normal(ks[5], (HIDDEN, HIDDEN), jnp.float32) * s, 'ln_gamma': jnp.ones((HIDDEN,), jnp.float32), 'ln_beta': jnp.zeros((HIDDEN,), jnp.float32), 'gate': jnp.array([GATE_INIT], jnp.float32)}
    _L2_xattn_all = _L2_xattn_setup()
    _L2_xattn_in = {k: v for k, v in _L2_xattn_all.items() if k in ('Wq', 'Wk', 'Wv', 'Wo', 'ln_gamma', 'ln_beta', 'gate')}
    del _L2_xattn_all

    def _L3_xattn_setup():
        import jax, jax.numpy as jnp
        import numpy as np
        H = 256
        NH = 32
        KVH = 8
        HD = H // NH
        GROUPS = NH // KVH
        EPS = 1e-06
        B, L, S = (4, 128, 128)

        def _gqa_forward(hidden_state, encoder_hidden_state, encoder_attention_mask, Wq, bq, Wk, bk, Wv, bv, Wo, bo, gamma, beta):
            b, l, _ = hidden_state.shape
            s = encoder_hidden_state.shape[1]
            q = hidden_state @ Wq + bq
            k = encoder_hidden_state @ Wk + bk
            v = encoder_hidden_state @ Wv + bv
            q = q.reshape(b, l, KVH, GROUPS, HD).transpose(0, 2, 3, 1, 4)
            k = k.reshape(b, s, KVH, HD).transpose(0, 2, 1, 3)
            v = v.reshape(b, s, KVH, HD).transpose(0, 2, 1, 3)
            scale = 1.0 / jnp.sqrt(jnp.asarray(HD, q.dtype))
            scores = jnp.einsum('bkgld,bksd->bkgls', q, k) * scale
            scores = scores + encoder_attention_mask[:, :, None, :, :]
            attn = jax.nn.softmax(scores, axis=-1)
            out = jnp.einsum('bkgls,bksd->bkgld', attn, v)
            out = out.transpose(0, 3, 1, 2, 4).reshape(b, l, H)
            out = out @ Wo + bo
            x = out + hidden_state
            mu = jnp.mean(x, axis=-1, keepdims=True)
            var = jnp.var(x, axis=-1, keepdims=True)
            return (x - mu) * jax.lax.rsqrt(var + EPS) * gamma + beta
        key = jax.random.key(seed)
        ks = jax.random.split(key, 12)
        sd = 0.02
        return {'hidden_state': jax.random.normal(ks[0], (B, L, H), jnp.float32), 'encoder_hidden_state': jax.random.normal(ks[1], (B, S, H), jnp.float32), 'encoder_attention_mask': jnp.zeros((B, 1, L, S), jnp.float32), 'Wq': jax.random.normal(ks[2], (H, H), jnp.float32) * sd, 'bq': jnp.zeros((H,), jnp.float32), 'Wk': jax.random.normal(ks[3], (H, KVH * HD), jnp.float32) * sd, 'bk': jnp.zeros((KVH * HD,), jnp.float32), 'Wv': jax.random.normal(ks[4], (H, KVH * HD), jnp.float32) * sd, 'bv': jnp.zeros((KVH * HD,), jnp.float32), 'Wo': jax.random.normal(ks[5], (H, H), jnp.float32) * sd, 'bo': jnp.zeros((H,), jnp.float32), 'gamma': jnp.ones((H,), jnp.float32), 'beta': jnp.zeros((H,), jnp.float32)}
    _L3_xattn_all = _L3_xattn_setup()
    _L3_xattn_in = {k: v for k, v in _L3_xattn_all.items() if k in ('Wq', 'bq', 'Wk', 'bk', 'Wv', 'bv', 'Wo', 'bo', 'gamma', 'beta')}
    del _L3_xattn_all
    return {'x': x, 'ctx_2048': ctx_2048, 'mask_BxS2_bf1': mask_BxS2_bf1, 'mask_Bx1xSxS2_ff0': mask_Bx1xSxS2_ff0, 'L0_xattn_ln1_scale': _L0_xattn_in['ln1_scale'], 'L0_xattn_ln1_offset': _L0_xattn_in['ln1_offset'], 'L0_xattn_wq1': _L0_xattn_in['wq1'], 'L0_xattn_bq1': _L0_xattn_in['bq1'], 'L0_xattn_wk1': _L0_xattn_in['wk1'], 'L0_xattn_bk1': _L0_xattn_in['bk1'], 'L0_xattn_wv1': _L0_xattn_in['wv1'], 'L0_xattn_bv1': _L0_xattn_in['bv1'], 'L0_xattn_wo1': _L0_xattn_in['wo1'], 'L0_xattn_bo1': _L0_xattn_in['bo1'], 'L0_xattn_bias_k1': _L0_xattn_in['bias_k1'], 'L0_xattn_bias_v1': _L0_xattn_in['bias_v1'], 'L0_xattn_ln2_scale': _L0_xattn_in['ln2_scale'], 'L0_xattn_ln2_offset': _L0_xattn_in['ln2_offset'], 'L0_xattn_wq2': _L0_xattn_in['wq2'], 'L0_xattn_bq2': _L0_xattn_in['bq2'], 'L0_xattn_wk2': _L0_xattn_in['wk2'], 'L0_xattn_bk2': _L0_xattn_in['bk2'], 'L0_xattn_wv2': _L0_xattn_in['wv2'], 'L0_xattn_bv2': _L0_xattn_in['bv2'], 'L0_xattn_wo2': _L0_xattn_in['wo2'], 'L0_xattn_bo2': _L0_xattn_in['bo2'], 'L0_xattn_bias_k2': _L0_xattn_in['bias_k2'], 'L0_xattn_bias_v2': _L0_xattn_in['bias_v2'], 'L0_xattn_ln_mlp_scale': _L0_xattn_in['ln_mlp_scale'], 'L0_xattn_ln_mlp_offset': _L0_xattn_in['ln_mlp_offset'], 'L0_xattn_w_fc1': _L0_xattn_in['w_fc1'], 'L0_xattn_b_fc1': _L0_xattn_in['b_fc1'], 'L0_xattn_w_fc2': _L0_xattn_in['w_fc2'], 'L0_xattn_b_fc2': _L0_xattn_in['b_fc2'], 'L1_xattn_ln1_w': _L1_xattn_in['ln1_w'], 'L1_xattn_ln1_b': _L1_xattn_in['ln1_b'], 'L1_xattn_ln2_w': _L1_xattn_in['ln2_w'], 'L1_xattn_ln2_b': _L1_xattn_in['ln2_b'], 'L1_xattn_maa_x': _L1_xattn_in['maa_x'], 'L1_xattn_maa_w1': _L1_xattn_in['maa_w1'], 'L1_xattn_maa_w2': _L1_xattn_in['maa_w2'], 'L1_xattn_maa_stack': _L1_xattn_in['maa_stack'], 'L1_xattn_time_decay': _L1_xattn_in['time_decay'], 'L1_xattn_decay_w1': _L1_xattn_in['decay_w1'], 'L1_xattn_decay_w2': _L1_xattn_in['decay_w2'], 'L1_xattn_faaaa': _L1_xattn_in['faaaa'], 'L1_xattn_Wr': _L1_xattn_in['Wr'], 'L1_xattn_Wk': _L1_xattn_in['Wk'], 'L1_xattn_Wv': _L1_xattn_in['Wv'], 'L1_xattn_Wg': _L1_xattn_in['Wg'], 'L1_xattn_Wo': _L1_xattn_in['Wo'], 'L1_xattn_gn_w': _L1_xattn_in['gn_w'], 'L1_xattn_gn_b': _L1_xattn_in['gn_b'], 'L1_xattn_ffn_maa_k': _L1_xattn_in['ffn_maa_k'], 'L1_xattn_ffn_maa_r': _L1_xattn_in['ffn_maa_r'], 'L1_xattn_ffn_Wk': _L1_xattn_in['ffn_Wk'], 'L1_xattn_ffn_Wr': _L1_xattn_in['ffn_Wr'], 'L1_xattn_ffn_Wv': _L1_xattn_in['ffn_Wv'], 'L2_xattn_Wq': _L2_xattn_in['Wq'], 'L2_xattn_Wk': _L2_xattn_in['Wk'], 'L2_xattn_Wv': _L2_xattn_in['Wv'], 'L2_xattn_Wo': _L2_xattn_in['Wo'], 'L2_xattn_ln_gamma': _L2_xattn_in['ln_gamma'], 'L2_xattn_ln_beta': _L2_xattn_in['ln_beta'], 'L2_xattn_gate': _L2_xattn_in['gate'], 'L3_xattn_Wq': _L3_xattn_in['Wq'], 'L3_xattn_bq': _L3_xattn_in['bq'], 'L3_xattn_Wk': _L3_xattn_in['Wk'], 'L3_xattn_bk': _L3_xattn_in['bk'], 'L3_xattn_Wv': _L3_xattn_in['Wv'], 'L3_xattn_bv': _L3_xattn_in['bv'], 'L3_xattn_Wo': _L3_xattn_in['Wo'], 'L3_xattn_bo': _L3_xattn_in['bo'], 'L3_xattn_gamma': _L3_xattn_in['gamma'], 'L3_xattn_beta': _L3_xattn_in['beta']}

def reference(x, ctx_2048, mask_BxS2_bf1, mask_Bx1xSxS2_ff0, L0_xattn_ln1_scale, L0_xattn_ln1_offset, L0_xattn_wq1, L0_xattn_bq1, L0_xattn_wk1, L0_xattn_bk1, L0_xattn_wv1, L0_xattn_bv1, L0_xattn_wo1, L0_xattn_bo1, L0_xattn_bias_k1, L0_xattn_bias_v1, L0_xattn_ln2_scale, L0_xattn_ln2_offset, L0_xattn_wq2, L0_xattn_bq2, L0_xattn_wk2, L0_xattn_bk2, L0_xattn_wv2, L0_xattn_bv2, L0_xattn_wo2, L0_xattn_bo2, L0_xattn_bias_k2, L0_xattn_bias_v2, L0_xattn_ln_mlp_scale, L0_xattn_ln_mlp_offset, L0_xattn_w_fc1, L0_xattn_b_fc1, L0_xattn_w_fc2, L0_xattn_b_fc2, L1_xattn_ln1_w, L1_xattn_ln1_b, L1_xattn_ln2_w, L1_xattn_ln2_b, L1_xattn_maa_x, L1_xattn_maa_w1, L1_xattn_maa_w2, L1_xattn_maa_stack, L1_xattn_time_decay, L1_xattn_decay_w1, L1_xattn_decay_w2, L1_xattn_faaaa, L1_xattn_Wr, L1_xattn_Wk, L1_xattn_Wv, L1_xattn_Wg, L1_xattn_Wo, L1_xattn_gn_w, L1_xattn_gn_b, L1_xattn_ffn_maa_k, L1_xattn_ffn_maa_r, L1_xattn_ffn_Wk, L1_xattn_ffn_Wr, L1_xattn_ffn_Wv, L2_xattn_Wq, L2_xattn_Wk, L2_xattn_Wv, L2_xattn_Wo, L2_xattn_ln_gamma, L2_xattn_ln_beta, L2_xattn_gate, L3_xattn_Wq, L3_xattn_bq, L3_xattn_Wk, L3_xattn_bk, L3_xattn_Wv, L3_xattn_bv, L3_xattn_Wo, L3_xattn_bo, L3_xattn_gamma, L3_xattn_beta):
    import jax
    import jax.numpy as jnp

    def _L0_xattn_ref(x, xf_1, xf_2, ln1_scale, ln1_offset, wq1, bq1, wk1, bk1, wv1, bv1, wo1, bo1, bias_k1, bias_v1, ln2_scale, ln2_offset, wq2, bq2, wk2, bk2, wv2, bv2, wo2, bo2, bias_k2, bias_v2, ln_mlp_scale, ln_mlp_offset, w_fc1, b_fc1, w_fc2, b_fc2):
        import jax, jax.numpy as jnp
        import numpy as np
        B, Q, S1, S2 = (4, 32, 256, 256)
        D, H, K, F = (256, 16, 128, 1024)
        LN_EPS = 1e-05

        def _layer_norm(x, scale, offset):
            mu = jnp.mean(x, axis=-1, keepdims=True)
            var = jnp.var(x, axis=-1, keepdims=True)
            return (x - mu) * jax.lax.rsqrt(var + LN_EPS) * scale + offset

        def _cross_attention(q_in, kv_in, wq, bq, wk, bk, wv, bv, wo, bo, bias_k, bias_v):
            b, q_len, _ = q_in.shape
            t = kv_in.shape[1]
            qh = (q_in @ wq + bq).reshape(b, q_len, H, K)
            kh = (kv_in @ wk + bk).reshape(b, t, H, K)
            vh = (kv_in @ wv + bv).reshape(b, t, H, K)
            kh = jnp.concatenate([kh, jnp.broadcast_to(bias_k, (b, 1, H, K))], axis=1)
            vh = jnp.concatenate([vh, jnp.broadcast_to(bias_v, (b, 1, H, K))], axis=1)
            scale = jnp.sqrt(jnp.asarray(K, q_in.dtype))
            logits = jnp.einsum('bqhk,bthk->bhqt', qh, kh) / scale
            weights = jax.nn.softmax(logits, axis=-1)
            ctx = jnp.einsum('bhqt,bthk->bqhk', weights, vh).reshape(b, q_len, H * K)
            return ctx @ wo + bo

        def _forward(x, xf_1, xf_2, ln1_scale, ln1_offset, wq1, bq1, wk1, bk1, wv1, bv1, wo1, bo1, bias_k1, bias_v1, ln2_scale, ln2_offset, wq2, bq2, wk2, bk2, wv2, bv2, wo2, bo2, bias_k2, bias_v2, ln_mlp_scale, ln_mlp_offset, w_fc1, b_fc1, w_fc2, b_fc2):
            res = x
            h = _layer_norm(x, ln1_scale, ln1_offset)
            x = res + _cross_attention(h, xf_1, wq1, bq1, wk1, bk1, wv1, bv1, wo1, bo1, bias_k1, bias_v1)
            res = x
            h = _layer_norm(x, ln2_scale, ln2_offset)
            x = res + _cross_attention(h, xf_2, wq2, bq2, wk2, bk2, wv2, bv2, wo2, bo2, bias_k2, bias_v2)
            h = _layer_norm(x, ln_mlp_scale, ln_mlp_offset)
            h = jax.nn.gelu(h @ w_fc1 + b_fc1, approximate=False) @ w_fc2 + b_fc2
            return x + h
        return _forward(x, xf_1, xf_2, ln1_scale, ln1_offset, wq1, bq1, wk1, bk1, wv1, bv1, wo1, bo1, bias_k1, bias_v1, ln2_scale, ln2_offset, wq2, bq2, wk2, bk2, wv2, bv2, wo2, bo2, bias_k2, bias_v2, ln_mlp_scale, ln_mlp_offset, w_fc1, b_fc1, w_fc2, b_fc2)

    def _L1_xattn_ref(x, state, ln1_w, ln1_b, ln2_w, ln2_b, maa_x, maa_w1, maa_w2, maa_stack, time_decay, decay_w1, decay_w2, faaaa, Wr, Wk, Wv, Wg, Wo, gn_w, gn_b, ffn_maa_k, ffn_maa_r, ffn_Wk, ffn_Wr, ffn_Wv, i):
        import jax, jax.numpy as jnp
        import numpy as np
        B, L, E, H = (4, 64, 256, 32)
        S = E // H
        EXTRA_MAA, EXTRA_DECAY = (32, 64)
        EPS = 1e-05

        def _ln(x, w, b):
            m = jnp.mean(x, axis=-1, keepdims=True)
            v = jnp.mean((x - m) ** 2, axis=-1, keepdims=True)
            return (x - m) * jax.lax.rsqrt(v + EPS) * w + b

        def _token_shift(xn, prev_row):
            first = (prev_row - xn[:, 0])[:, None]
            rest = xn[:, :-1] - xn[:, 1:]
            return jnp.concatenate([first, rest], axis=1)
        b, l = (x.shape[0], x.shape[1])
        i0 = (2 + S) * i + 0
        i1 = (2 + S) * i + 1
        xn = _ln(x, ln1_w, ln1_b)
        sx = _token_shift(xn, state[:, i1])
        xxx = jnp.tanh((xn + sx * maa_x) @ maa_w1).reshape(b, l, 5, 1, EXTRA_MAA)
        xxx = jnp.matmul(xxx, maa_w2).reshape(b, l, 5, E)
        x5 = xn[:, :, None] + sx[:, :, None] * (maa_stack + xxx)
        w = jnp.exp(-jnp.exp(time_decay + jnp.tanh(x5[:, :, 1] @ decay_w1) @ decay_w2))
        w = w.reshape(b, l, H, S)
        r = (x5[:, :, 3] @ Wr.T).reshape(b, l, H, S)
        k = (x5[:, :, 0] @ Wk.T).reshape(b, l, H, S)
        v = (x5[:, :, 2] @ Wv.T).reshape(b, l, H, S)
        g = jax.nn.silu(x5[:, :, 4] @ Wg.T)
        s0 = state[:, (2 + S) * i + 2:(2 + S) * (i + 1)].reshape(b, H, S, S)
        u = faaaa[None, :, :, None]

        def step(s, rkvw):
            r_t, k_t, v_t, w_t = rkvw
            a = k_t[:, :, :, None] * v_t[:, :, None, :]
            out = jnp.einsum('bhk,bhkd->bhd', r_t, u * a + s)
            return (a + w_t[:, :, :, None] * s, out)
        xs = tuple((jnp.moveaxis(t, 1, 0) for t in (r, k, v, w)))
        _, outs = jax.lax.scan(step, s0, xs)
        att = jnp.moveaxis(outs, 0, 1).reshape(b, l, E)
        a4 = att.reshape(b, l, H, S)
        m = jnp.mean(a4, axis=-1, keepdims=True)
        var = jnp.mean((a4 - m) ** 2, axis=-1, keepdims=True)
        att = ((a4 - m) * jax.lax.rsqrt(var + EPS)).reshape(b, l, E) * gn_w + gn_b
        x = x + att * g @ Wo.T
        xn2 = _ln(x, ln2_w, ln2_b)
        sx2 = _token_shift(xn2, state[:, i0])
        xk = xn2 + sx2 * ffn_maa_k
        xr = xn2 + sx2 * ffn_maa_r
        rr = jax.nn.sigmoid(xr @ ffn_Wr.T)
        kk = jnp.square(jax.nn.relu(xk @ ffn_Wk.T))
        x = x + rr * (kk @ ffn_Wv.T)
        return x

    def _L2_xattn_ref(hidden_states, audio_kv, audio_attention_mask, Wq, Wk, Wv, Wo, ln_gamma, ln_beta, gate):
        import jax, jax.numpy as jnp
        import numpy as np
        HIDDEN = 256
        HEADS = 16
        HEAD_DIM = HIDDEN // HEADS
        LN_EPS = 1e-05
        GATE_INIT = 0.5

        def _layer_norm(x, gamma, beta):
            mu = jnp.mean(x, axis=-1, keepdims=True)
            var = jnp.mean(jnp.square(x - mu), axis=-1, keepdims=True)
            return (x - mu) * jax.lax.rsqrt(var + LN_EPS) * gamma + beta
        B, Tt, D = hidden_states.shape
        Ta = audio_kv.shape[1]
        scale = HEAD_DIM ** (-0.5)
        a = _layer_norm(audio_kv, ln_gamma, ln_beta)
        Q = (hidden_states @ Wq.T).reshape(B, Tt, HEADS, HEAD_DIM).transpose(0, 2, 1, 3)
        K = (a @ Wk.T).reshape(B, Ta, HEADS, HEAD_DIM).transpose(0, 2, 1, 3)
        V = (a @ Wv.T).reshape(B, Ta, HEADS, HEAD_DIM).transpose(0, 2, 1, 3)
        scores = jnp.einsum('bhtd,bhsd->bhts', Q, K) * scale
        mask = audio_attention_mask[:, None, None, :]
        scores = jnp.where(mask, scores, jnp.float32(-jnp.inf))
        attn = jax.nn.softmax(scores, axis=-1)
        out = jnp.einsum('bhts,bhsd->bhtd', attn, V)
        out = out.transpose(0, 2, 1, 3).reshape(B, Tt, D)
        out = out @ Wo.T
        return hidden_states + jnp.tanh(gate) * out

    def _L3_xattn_ref(hidden_state, encoder_hidden_state, encoder_attention_mask, Wq, bq, Wk, bk, Wv, bv, Wo, bo, gamma, beta):
        import jax, jax.numpy as jnp
        import numpy as np
        H = 256
        NH = 32
        KVH = 8
        HD = H // NH
        GROUPS = NH // KVH
        EPS = 1e-06
        B, L, S = (4, 128, 128)

        def _gqa_forward(hidden_state, encoder_hidden_state, encoder_attention_mask, Wq, bq, Wk, bk, Wv, bv, Wo, bo, gamma, beta):
            b, l, _ = hidden_state.shape
            s = encoder_hidden_state.shape[1]
            q = hidden_state @ Wq + bq
            k = encoder_hidden_state @ Wk + bk
            v = encoder_hidden_state @ Wv + bv
            q = q.reshape(b, l, KVH, GROUPS, HD).transpose(0, 2, 3, 1, 4)
            k = k.reshape(b, s, KVH, HD).transpose(0, 2, 1, 3)
            v = v.reshape(b, s, KVH, HD).transpose(0, 2, 1, 3)
            scale = 1.0 / jnp.sqrt(jnp.asarray(HD, q.dtype))
            scores = jnp.einsum('bkgld,bksd->bkgls', q, k) * scale
            scores = scores + encoder_attention_mask[:, :, None, :, :]
            attn = jax.nn.softmax(scores, axis=-1)
            out = jnp.einsum('bkgls,bksd->bkgld', attn, v)
            out = out.transpose(0, 3, 1, 2, 4).reshape(b, l, H)
            out = out @ Wo + bo
            x = out + hidden_state
            mu = jnp.mean(x, axis=-1, keepdims=True)
            var = jnp.var(x, axis=-1, keepdims=True)
            return (x - mu) * jax.lax.rsqrt(var + EPS) * gamma + beta
        return _gqa_forward(hidden_state, encoder_hidden_state, encoder_attention_mask, Wq, bq, Wk, bk, Wv, bv, Wo, bo, gamma, beta)
    x = _L0_xattn_ref(x, ctx_2048, ctx_2048, L0_xattn_ln1_scale, L0_xattn_ln1_offset, L0_xattn_wq1, L0_xattn_bq1, L0_xattn_wk1, L0_xattn_bk1, L0_xattn_wv1, L0_xattn_bv1, L0_xattn_wo1, L0_xattn_bo1, L0_xattn_bias_k1, L0_xattn_bias_v1, L0_xattn_ln2_scale, L0_xattn_ln2_offset, L0_xattn_wq2, L0_xattn_bq2, L0_xattn_wk2, L0_xattn_bk2, L0_xattn_wv2, L0_xattn_bv2, L0_xattn_wo2, L0_xattn_bo2, L0_xattn_bias_k2, L0_xattn_bias_v2, L0_xattn_ln_mlp_scale, L0_xattn_ln_mlp_offset, L0_xattn_w_fc1, L0_xattn_b_fc1, L0_xattn_w_fc2, L0_xattn_b_fc2)
    x = _L1_xattn_ref(x, ctx_2048, L1_xattn_ln1_w, L1_xattn_ln1_b, L1_xattn_ln2_w, L1_xattn_ln2_b, L1_xattn_maa_x, L1_xattn_maa_w1, L1_xattn_maa_w2, L1_xattn_maa_stack, L1_xattn_time_decay, L1_xattn_decay_w1, L1_xattn_decay_w2, L1_xattn_faaaa, L1_xattn_Wr, L1_xattn_Wk, L1_xattn_Wv, L1_xattn_Wg, L1_xattn_Wo, L1_xattn_gn_w, L1_xattn_gn_b, L1_xattn_ffn_maa_k, L1_xattn_ffn_maa_r, L1_xattn_ffn_Wk, L1_xattn_ffn_Wr, L1_xattn_ffn_Wv, 0)
    x = _L2_xattn_ref(x, ctx_2048, mask_BxS2_bf1, L2_xattn_Wq, L2_xattn_Wk, L2_xattn_Wv, L2_xattn_Wo, L2_xattn_ln_gamma, L2_xattn_ln_beta, L2_xattn_gate)
    x = _L3_xattn_ref(x, ctx_2048, mask_Bx1xSxS2_ff0, L3_xattn_Wq, L3_xattn_bq, L3_xattn_Wk, L3_xattn_bk, L3_xattn_Wv, L3_xattn_bv, L3_xattn_Wo, L3_xattn_bo, L3_xattn_gamma, L3_xattn_beta)
    return x

_drawn_inputs = setup_inputs


def setup_inputs(seed=0):
    import zlib

    import numpy as np

    out = dict(_drawn_inputs(seed))
    spreads = {'L0_xattn_ln1_scale': (1.0, 0.6),
     'L0_xattn_ln1_offset': (0.0, 0.8),
     'L0_xattn_bq1': (0.0, 0.8),
     'L0_xattn_bk1': (0.0, 2.0),
     'L0_xattn_bv1': (0.0, 0.1),
     'L0_xattn_bo1': (0.0, 0.1),
     'L0_xattn_ln2_scale': (1.0, 0.6),
     'L0_xattn_ln2_offset': (0.0, 0.8),
     'L0_xattn_bq2': (0.0, 0.8),
     'L0_xattn_bk2': (0.0, 2.0),
     'L0_xattn_bv2': (0.0, 0.1),
     'L0_xattn_bo2': (0.0, 0.1),
     'L0_xattn_ln_mlp_scale': (1.0, 0.6),
     'L0_xattn_ln_mlp_offset': (0.0, 0.687),
     'L0_xattn_b_fc1': (0.0, 0.1),
     'L0_xattn_b_fc2': (0.0, 0.1),
     'L1_xattn_ln1_w': (1.0, 0.6),
     'L1_xattn_ln1_b': (0.0, 0.575),
     'L1_xattn_ln2_w': (1.0, 0.6),
     'L1_xattn_ln2_b': (0.0, 0.8),
     'L1_xattn_gn_w': (1.0, 0.6),
     'L1_xattn_gn_b': (0.0, 0.8),
     'L2_xattn_ln_gamma': (1.0, 0.6),
     'L2_xattn_ln_beta': (0.0, 2.0),
     'L3_xattn_bq': (0.0, 2.0),
     'L3_xattn_bk': (0.0, 2.0),
     'L3_xattn_bv': (0.0, 0.283),
     'L3_xattn_bo': (0.0, 0.1),
     'L3_xattn_gamma': (1.0, 0.2),
     'L3_xattn_beta': (0.0, 0.1)}
    factors = {'L0_xattn_wq1': 8.0,
     'L0_xattn_wk1': 8.0,
     'L0_xattn_bias_k1': 64.0,
     'L0_xattn_bias_v1': 64.0,
     'L0_xattn_wq2': 8.0,
     'L0_xattn_wk2': 8.0,
     'L0_xattn_bias_k2': 64.0,
     'L0_xattn_bias_v2': 64.0,
     'L1_xattn_maa_x': 8.0,
     'L1_xattn_maa_w1': 8.0,
     'L1_xattn_maa_w2': 8.0,
     'L1_xattn_maa_stack': 8.0,
     'L1_xattn_time_decay': 2.994,
     'L1_xattn_decay_w1': 8.0,
     'L1_xattn_decay_w2': 8.0,
     'L1_xattn_faaaa': 6.103,
     'L1_xattn_ffn_maa_k': 8.0,
     'L1_xattn_ffn_maa_r': 8.0,
     'L1_xattn_ffn_Wk': 3.071,
     'L1_xattn_ffn_Wr': 8.0,
     'L1_xattn_ffn_Wv': 2.888,
     'L2_xattn_Wq': 8.0,
     'L2_xattn_Wk': 8.0,
     'L3_xattn_Wq': 8.0,
     'L3_xattn_Wk': 8.0}
    for name, (base, spread) in spreads.items():
        noise = np.random.default_rng([zlib.crc32(name.encode()), seed]).standard_normal(out[name].shape)
        drawn = base * np.exp(spread * noise) if base else spread * noise
        out[name] = jnp.asarray(drawn.astype(out[name].dtype))
    for name, factor in factors.items():
        out[name] = (out[name] * factor).astype(out[name].dtype)
    return out
```

```python
from contextlib import ExitStack

import numpy as np

import concourse.bass as bass
from concourse import mybir

F32 = mybir.dt.float32
F32R = mybir.dt.float32r
U8 = mybir.dt.uint8
ALU = mybir.AluOpType
ACT = mybir.ActivationFunctionType
AX = mybir.AxisListType

P = 128
B, S, D = 4, 256, 256
TOK = B * S
NT = TOK // P
NC = D // P
H0, K0 = 16, 128
PAIR = 2
NPAIR = H0 // PAIR
HW = PAIR * K0
FF = 1024
NF = FF // P
EPS0 = 1e-5
HALF = TOK // 2
BANK = 512

VECS = ['L0_xattn_ln1_scale', 'L0_xattn_ln1_offset', 'L0_xattn_ln2_scale', 'L0_xattn_ln2_offset',
        'L0_xattn_ln_mlp_scale', 'L0_xattn_ln_mlp_offset', 'L1_xattn_ln1_w', 'L1_xattn_ln1_b',
        'L1_xattn_ln2_w', 'L1_xattn_ln2_b', 'L1_xattn_maa_x', 'L1_xattn_maa_stack', 'L1_xattn_time_decay',
        'L1_xattn_faaaa', 'L1_xattn_gn_w', 'L1_xattn_gn_b', 'L1_xattn_ffn_maa_k', 'L1_xattn_ffn_maa_r',
        'L2_xattn_ln_gamma', 'L2_xattn_ln_beta', 'L3_xattn_bq']
VROWS = {}
for _n in VECS:
    VROWS[_n] = sum(5 if m == 'L1_xattn_maa_stack' else 1 for m in VECS[:VECS.index(_n)])
PREV = len(VECS) + 4
NV = PREV + 2 * B
HVECS = [f'L0_xattn_{n}{a}' for a in (1, 2) for n in ('bq', 'bk', 'bias_k', 'bias_v', 'bv')]
NHV = len(HVECS) * H0 + NF
ROWS = ['L0_xattn_bo1', 'L0_xattn_bo2', 'L0_xattn_b_fc2', 'L3_xattn_bo', 'L3_xattn_gamma', 'L3_xattn_beta']


class Chip:

    def __init__(self, nc, stack):
        self.nc = nc

        def sb(name, shape, dt=F32):
            return stack.enter_context(nc.sbuf_tensor(name, shape, dt))

        self.x = sb("x_rows", [P, NT, D])
        self.ctx = sb("ctx_rows", [P, NT, D])
        self.ident = sb("ident", [P, P])
        self.vecs = sb("vecs_T", [P, NC, NV])
        self.hvecs = sb("hvecs_T", [P, NHV])
        self.rows = sb("rows_bc", [P, len(ROWS), D])
        self.expo = sb("minus_half", [P, NT])
        self.psum = stack.enter_context(nc.psum_tensor("psum", [P, 8, BANK], F32))

        self.semaphores = []

    def semaphore(self, name):
        self.semaphores.append(self.nc.alloc_semaphore(name))
        return self.semaphores[-1]

    def renew_semaphores(self):
        self.nc.all_engine_barrier()
        self.nc.clear_and_free_semaphores(self.semaphores)
        self.nc.all_engine_barrier()
        self.semaphores = []

    def vec(self, name, c, i=0):
        r = VROWS[name] + i
        return self.vecs[:, c, r:r + 1]


def tiles_of(dram):
    return dram.rearrange("b (u p) d -> p (b u) d", p=P)


def stage_setup(chip, d, ctx_hi, ctx_lo):
    nc, ps = chip.nc, chip.psum
    with ExitStack() as st:
        sb = lambda n, s, t=F32: st.enter_context(nc.sbuf_tensor(n, s, t))
        sem = lambda n: chip.semaphore(n)
        vraw = sb("vecs_raw", [NV, D])
        hraw = sb("hvecs_raw", [NHV // 2, 2, K0])
        ld_ctx, ld_vec, ld_x, ld_rows = sem("ld_ctx"), sem("ld_vec"), sem("ld_x"), sem("ld_rows")
        ident_zero, ident_ok, turned, hi_done, lo_done, vec_done = (
            sem("ident_zero"), sem("ident_ok"), sem("turned"), sem("ctx_hi_done"), sem("ctx_lo_done"), sem("vec_done"))
        with nc.Block() as block:
            @block.sync
            def _(sp):
                for j in range(2):
                    sp.dma_start(chip.ctx[:, j * 4:j * 4 + 4, :], tiles_of(d['ctx_2048'])[:, j * 4:j * 4 + 4, :]).then_inc(ld_ctx, 16)
                sp.dma_start(chip.x[:, :, :], tiles_of(d['x'])).then_inc(ld_x, 16)
                sp.wait_ge(ld_x, 16)

            @block.scalar
            def _(act):
                act.dma_start(vraw[:, :], d['vecs']).then_inc(ld_vec, 16)
                act.dma_start(hraw[:, :, :], d['hvecs'].rearrange("(t r) k -> r t k", t=2)).then_inc(ld_vec, 16)
                act.dma_start(chip.rows[:, :, :].rearrange("p r d -> p (r d)"),
                              d['rows'].rearrange("(a n) -> a n", a=1).to_broadcast([P, len(ROWS) * D])).then_inc(ld_rows, 16)
                for n in range(4):
                    act.wait_ge(turned, n + 1)
                    act.activation(ctx_hi[:, n // 2, (n % 2) * HALF:(n % 2 + 1) * HALF], ps[:, n, :], ACT.Copy).then_inc(hi_done, 1)
                act.wait_ge(ld_rows, 16)

            @block.gpsimd
            def _(pool):
                pool.memset(chip.expo[:, :], -0.5)
                pool.memset(chip.ident[:, :], 0.0).then_inc(ident_zero, 1)
                pool.wait_ge(ident_zero, 1)
                pool.affine_select(out=chip.ident[:, :], in_=chip.ident[:, :], compare_op=ALU.not_equal, fill=1.0,
                                   base=0, pattern=[[-1, P]], channel_multiplier=1).then_inc(ident_ok, 1)

            @block.tensor
            def _(pe):
                pe.wait_ge(ident_ok, 1)
                for n in range(4):
                    pe.wait_ge(ld_ctx, 32)
                    c, half = n // 2, n % 2
                    for t in range(4):
                        mm = pe.transpose(ps[:, n, t * P:(t + 1) * P], chip.ctx[:, half * 4 + t, c * P:(c + 1) * P], chip.ident[:, :])
                    mm.then_inc(turned, 1)
                pe.wait_ge(ld_vec, 32)
                for c in range(NC):
                    pe.transpose(ps[:, 4, c * NV:(c + 1) * NV], vraw[:, c * P:(c + 1) * P], chip.ident[0:NV, 0:NV])
                R = NHV // 2
                for t in range(2):
                    mm = pe.transpose(ps[:, 5, t * R:(t + 1) * R], hraw[:, t, :], chip.ident[0:R, 0:R])
                mm.then_inc(turned, 1)

            @block.vector
            def _(dve):
                for n in range(4):
                    dve.wait_ge(hi_done, n + 1)
                    sl = slice((n % 2) * HALF, (n % 2 + 1) * HALF)
                    dve.tensor_tensor(ctx_lo[:, n // 2, sl], ps[:, n, :], ctx_hi[:, n // 2, sl].bitcast(F32), ALU.subtract).then_inc(lo_done, 1)
                dve.wait_ge(turned, 5)
                dve.tensor_copy(chip.vecs[:, :, :], ps[:, 4, 0:NC * NV].rearrange("p (c v) -> p c v", c=NC))
                dve.tensor_copy(chip.hvecs[:, :], ps[:, 5, 0:NHV])


def stage_layernorm(chip, tag, rows, scale_of, offset_of, eps, hi=None, lo=None, plain=None, add=None, prefetch=None):
    nc, ps = chip.nc, chip.psum
    with ExitStack() as st:
        sb = lambda n, s, t=F32: st.enter_context(nc.sbuf_tensor(f"{tag}_{n}", s, t))
        sem = lambda n: chip.semaphore(f"{tag}_{n}")
        xn = sb("normed", [P, NT, D])
        bn = sb("bn", [P, NT, 6])
        mv = sb("mean_var", [P, NT, 2])
        ve = sb("var_eps", [P, NT])
        rstd = sb("rstd", [P, NT])
        full = sb("full", [P, 4, BANK]) if hi is not None else None
        stats, aggr, var_ok, rstd_ok, normed, turned, full_ok, hi_ok, lo_ok = (
            sem(n) for n in ("stats", "aggr", "var_ok", "rstd_ok", "normed", "turned", "full_ok", "hi_ok", "lo_ok"))
        with nc.Block() as block:
            if prefetch:
                block.sync(prefetch)

            @block.gpsimd
            def _(pool):
                pool.wait_ge(var_ok, 1)
                pool.tensor_tensor(rstd[:, :], ve[:, :], chip.expo[:, :], ALU.pow).then_inc(rstd_ok, 1)
                if hi is not None:
                    for n in range(4):
                        pool.wait_ge(hi_ok, n + 1)
                        sl = slice((n % 2) * HALF, (n % 2 + 1) * HALF)
                        pool.tensor_tensor(lo[:, n // 2, sl], full[:, n, :], hi[:, n // 2, sl].bitcast(F32), ALU.subtract).then_inc(lo_ok, 1)

            @block.vector
            def _(dve):
                for j in range(NT):
                    dve.bn_stats(bn[:, j, :], rows[:, j, :]).then_inc(stats, 1)
                for j in range(NT):
                    dve.wait_ge(stats, j + 1)
                    dve.bn_aggr(mv[:, j, :], bn[:, j, :]).then_inc(aggr, 1)
                dve.wait_ge(aggr, NT)
                dve.tensor_scalar(ve[:, :], mv[:, :, 1], float(eps), None, ALU.add).then_inc(var_ok, 1)
                dve.wait_ge(rstd_ok, 1)
                for j in range(NT):
                    dve.tensor_scalar(xn[:, j, :], rows[:, j, :], mv[:, j, 0:1], rstd[:, j:j + 1], ALU.subtract, ALU.mult).then_inc(normed, 1)
                if add is not None:
                    dve.wait_ge(normed, NT)
                    dve.tensor_tensor(rows[:, :, :], rows[:, :, :], chip.rows[:, add:add + 1, :].to_broadcast([P, NT, D]), ALU.add)
                if hi is not None:
                    for n in range(4):
                        dve.wait_ge(full_ok, n + 1)
                        dve.tensor_copy(hi[:, n // 2, (n % 2) * HALF:(n % 2 + 1) * HALF], full[:, n, :]).then_inc(hi_ok, 1)

            @block.tensor
            def _(pe):
                for n in range(4):
                    half, c = n % 2, n // 2
                    pe.wait_ge(normed, half * 4 + 4)
                    for t in range(4):
                        mm = pe.transpose(ps[:, n, t * P:(t + 1) * P], xn[:, half * 4 + t, c * P:(c + 1) * P], chip.ident[:, :])
                    mm.then_inc(turned, 1)

            @block.scalar
            def _(act):
                for n in range(4):
                    half, c = n % 2, n // 2
                    act.wait_ge(turned, n + 1)
                    if hi is not None:
                        act.activation(full[:, n, :], ps[:, n, :], ACT.Identity, scale=scale_of(c), bias=offset_of(c)).then_inc(full_ok, 1)
                    else:
                        act.activation(plain(c, half), ps[:, n, :].rearrange("p (b s) -> p b s", b=2), ACT.Identity,
                                       scale=scale_of(c), bias=offset_of(c)).then_inc(full_ok, 1)


def stage_cross_attention(chip, d, a, h_hi, h_lo, ctx_hi, ctx_lo):
    nc, ps = chip.nc, chip.psum
    C = float(K0) ** -0.5
    L = f"L0_xattn_"
    at = (a - 1) * 5 * H0
    W3 = {n: d[f"{L}w{n}{a}"].rearrange("(c p) n -> p c n", p=P) for n in 'qkv'}
    with ExitStack() as st:
        sb = lambda n, s, t=F32: st.enter_context(nc.sbuf_tensor(f"a{a}_{n}", s, t))
        sem = lambda n: chip.semaphore(f"a{a}_{n}")
        raw = {n: sb(f"w{n}_raw", [P, NC, HW]) for n in 'qkv'}
        wo_raw = sb("wo_raw", [P, H0, D])
        whi = {n: sb(f"w{n}_hi", [P, NC, HW], F32R) for n in 'qkvo'}
        wlo = {n: sb(f"w{n}_lo", [P, NC, HW], F32R) for n in 'qkvo'}
        qk_hi = {n: sb(f"{n}_hi", [P, PAIR, TOK], F32R) for n in 'qc'}
        qk_lo = {n: sb(f"{n}_lo", [P, PAIR, TOK], F32R) for n in 'qc'}
        E_LATE, M_LATE, I_LATE = 2, 1, 3
        KW = S + 2
        k_hi = sb("k_hi", [P, PAIR, B, KW], F32R)
        k_lo = sb("k_lo", [P, PAIR, B, KW], F32R)
        v_hi = sb("v_hi", [P, NT, HW], F32R)
        v_lo = sb("v_lo", [P, NT, HW], F32R)
        prob = sb("prob", [P, 4, 2, KW])
        negm = sb("neg_max", [P, 4, 2])
        tot = sb("total", [P, 4, 2])
        rtot = sb("inv_total", [P, 4, 2])
        pt_hi = sb("probT_hi", [P, 4, BANK], F32R)
        pt_lo = sb("probT_lo", [P, 4, BANK], F32R)
        one = sb("ones", [P, 2])
        pb = sb("prob_bias", [P, NT, NPAIR, PAIR])
        bcol = sb("bias_cols", [P, 3, NPAIR, PAIR])
        qk_cols = sb("qk_cols", [P, 2, PAIR])
        v_cols = sb("v_cols", [P, PAIR])
        wo_pair = sb("wo_pair", [P, PAIR, D])
        kb_hi = sb("bias_k_hi", [P, NPAIR, PAIR], F32R)
        kb_lo = sb("bias_k_lo", [P, NPAIR, PAIR], F32R)
        dv = sb("bias_v_less_bv", [P, H0])
        bvo_T = sb("bias_out_T", [P, NC, H0])
        bvo = sb("bias_out", [H0, D])
        pb_T = sb("prob_bias_T", [H0, TOK])

        (ld_q, ld_k, ld_v, ld_o, q_split, k_split, v_split, o_split, rounded, q_rounded, cols_ok, cols_cur, ld_op, kcols,
         acc_full, acc_hi, acc_free, s_done, s_max, s_exp, s_sum, s_norm, t_done, t_hi, t_free) = (
            sem(n) for n in ("ld_wq", "ld_wk", "ld_wv", "ld_wo", "wq_split", "wk_split", "wv_split", "wo_split",
                             "w_rounded", "wq_rounded", "cols_ok", "cols_cur", "ld_wo_pair", "bias_k_cols",
                             "acc_full", "acc_hi", "acc_free", "scores_done", "max_done", "exp_done", "inv_done",
                             "norm_done", "turned", "turned_hi", "turned_free"))
        ld = {'q': ld_q, 'k': ld_k, 'v': ld_v}
        split = {'q': q_split, 'k': k_split, 'v': v_split}
        hv = lambda k: chip.hvecs[:, at + k * H0:at + (k + 1) * H0]

        PRE = ['Q0', 'Q1', 'K0', 'K1', 'Q2', 'Q3', 'K2', 'K3']
        STEP = ("S0 O0 O1 S1 O2 O3 S2 V0 V1 T0 S3 V2 T1 S4 V3 Q0 T2 S5 A0 Q1 T3 S6 K0 T4 A1 S7 K1 T5 Q2 T6 "
                "A2 Q3 K2 T7 K3 A3").split()
        FIRST = [s for s in STEP if s[0] != 'O']
        LAST = [s for s in STEP if s[0] not in 'QK']
        TAIL = ['O0', 'O1', 'O2', 'O3']
        HIS = 16
        USES = HIS + 4
        base_of = lambda i: len(PRE) if isinstance(i, int) and i == 0 else i * USES + len(PRE) - 4
        END = base_of(NPAIR - 1) + 12 + 4
        use_of = lambda order, s: [x for x in order if x[0] in 'VAQKO'].index(s)
        acc = lambda n: ps[:, n % 2, :]
        s_bank = lambda u: ps[:, 2 + 2 * (u % 2):4 + 2 * (u % 2), 0:KW]
        t_bank = lambda u: ps[:, 6 + u % 2, :]
        U = 2 * B

        def three(pe, out, l_hi, l_lo, r_hi, r_lo, first, last):
            pe.matmul(out, l_hi, r_hi, start=first, stop=False)
            pe.matmul(out, l_hi, r_lo, start=False, stop=False)
            return pe.matmul(out, l_lo, r_hi, start=False, stop=last)

        def steps(eng, body):
            body(0, FIRST)
            with eng.Fori(1, NPAIR - 1) as i:
                body(i, STEP)
            body(NPAIR - 1, LAST)
            body(NPAIR, TAIL)

        def project_out(s, h_dst, half):
            if s[0] == 'Q':
                cols = slice(half * HALF, (half + 1) * HALF)
                return qk_hi['q'][:, h_dst, cols], qk_lo['q'][:, h_dst, cols]
            return k_hi[:, h_dst, 2 * half:2 * half + 2, 0:S], k_lo[:, h_dst, 2 * half:2 * half + 2, 0:S]

        def like(s, view):
            return view.rearrange("p (b s) -> p b s", b=2) if s[0] == 'K' else view

        def later(order, what, steps):
            out, held = [], []
            for s in order:
                out.append(s)
                held = [(t, n - 1) for t, n in held]
                out += [t for t, n in held if n == 0]
                held = [(t, n) for t, n in held if n > 0]
                if s[0] == 'S':
                    held.append((what + s[1], steps))
            return out + [t for t, n in held]

        def act_order(order):
            out = [s for s in later(order, 'E', E_LATE) if s[0] in 'EVATQK' or s == 'S2']
            return [('R0' if s == 'S2' else s) for s in out]

        def dve_order(order):
            out = []
            for s in later(later(order, 'M', M_LATE), 'I', I_LATE):
                if s == 'S2':
                    out.append('R0')
                elif s[0] != 'S':
                    out.append(s)
            return out

        with nc.Block() as block:
            @block.sync
            def _(sp):
                sp.dma_start(wo_raw[:, :, :], d[f"{L}wo{a}"].rearrange("(h k) n -> k h n", k=K0)).then_inc(ld_o, 16)
                for n in 'qkv':
                    sp.dma_start(raw[n][:, :, :], W3[n][:, :, 0:HW]).then_inc(ld[n], 16)
                sp.wait_ge(ld_o, 16)
                sp.dma_start(wo_pair[:, :, :], wo_raw[:, 0:PAIR, :]).then_inc(ld_op, 16)
                with sp.Fori(1, NPAIR) as i:
                    for n in 'qkv':
                        sp.wait_ge(split[n], i)
                        sp.dma_start(raw[n][:, :, :], W3[n][:, :, bass.ds(i * HW, HW)]).then_inc(ld[n], 16)
                    sp.wait_ge(o_split, i)
                    sp.dma_start(wo_pair[:, :, :], wo_raw[:, bass.ds(i * PAIR, PAIR), :]).then_inc(ld_op, 16)

            @block.gpsimd
            def _(pool):
                rounds = [0]
                ones = one[:, 0:1].to_broadcast([P, NC, HW])

                def cut(src, n, count, done):
                    pool.tensor_tensor(whi[n][:, :, :], src, ones, ALU.mult).then_inc(rounded, 1)
                    pool.wait_ge(rounded, count + 1)
                    pool.tensor_tensor(wlo[n][:, :, :], src, whi[n][:, :, :].bitcast(F32), ALU.subtract).then_inc(done, 1)

                pool.memset(one[:, :], 1.0).then_inc(rounded, 1)
                pool.wait_ge(rounded, 1)
                pool.wait_ge(ld_k, 16)
                cut(raw['k'][:, :, :], 'k', 1, k_split)
                pool.wait_ge(ld_v, 16)
                cut(raw['v'][:, :, :], 'v', 2, v_split)

                def body(i, order):
                    last = order is LAST

                    def norm(u):
                        h, b = u // B, u % B
                        pool.wait_ge(s_sum, i * U + u + 1)
                        pool.tensor_tensor(prob[:, u % 4, :, 0:S], prob[:, u % 4, :, 0:S],
                                           rtot[:, u % 4, :].unsqueeze(2).to_broadcast([P, 2, S]), ALU.mult)
                        pool.tensor_tensor(pb[:, 2 * b:2 * b + 2, i, h:h + 1], prob[:, u % 4, :, S:S + 1], rtot[:, u % 4, :].unsqueeze(2), ALU.mult).then_inc(s_norm, 1)

                    if order is TAIL:
                        return
                    norm(0)
                    norm(1)
                    if order is not FIRST:
                        pool.wait_ge(acc_full, base_of(i) + 4)
                    pool.wait_ge(ld_op, i * 16 + 16)
                    cut(wo_pair[:, :, :], 'o', i * 3 + 3, o_split)
                    norm(2)
                    if not last:
                        pool.wait_ge(ld_k, i * 16 + 32)
                        cut(raw['k'][:, :, :], 'k', i * 3 + 4, k_split)
                    for u in range(3, U):
                        norm(u)
                        if u == U - 2 and not last:
                            pool.wait_ge(ld_v, i * 16 + 32)
                            cut(raw['v'][:, :, :], 'v', i * 3 + 5, v_split)

                steps(pool, body)

            @block.tensor
            def _(pe):
                pe.sem_inc(t_done, 4)

                def project(s, i, n, total):
                    w, h, half = s[0].lower(), int(s[1]) // 2, int(s[1]) % 2
                    for c in range(NC):
                        cols = slice(half * HALF, (half + 1) * HALF)
                        rh, rl = (h_hi, h_lo) if w == 'q' else (ctx_hi, ctx_lo)
                        mm = three(pe, acc(n), whi[w][:, c, h * K0:(h + 1) * K0], wlo[w][:, c, h * K0:(h + 1) * K0],
                                   rh[:, c, cols], rl[:, c, cols], c == 0, c == NC - 1)
                    mm.then_inc(acc_full, 1)

                pe.wait_ge(q_split, 1)
                for n, s in enumerate(PRE):
                    if s == 'K0':
                        pe.wait_ge(k_split, 1)
                    if n >= 2:
                        pe.wait_ge(acc_free, n - 1)
                    project(s, 0, n, n)

                def body(i, order):
                    base = base_of(i) if order is not TAIL else END - 4
                    for s in order:
                        k, m = s[0], int(s[1])
                        if k in 'VAQKO':
                            n = use_of(order, s)
                            pe.wait_ge(acc_free, base + n - 1)
                        if k in 'QK':
                            if s in ('Q0', 'K0'):
                                pe.wait_ge(split[k.lower()], i + 2)
                            project(s, i, n, base + n)
                        if k == 'V':
                            if m == 0:
                                pe.wait_ge(v_split, i + 1)
                            for j in range(2):
                                t = 2 * m + j
                                for c in range(NC):
                                    mm = three(pe, acc(n)[:, j * HW:(j + 1) * HW], ctx_hi[:, c, t * P:(t + 1) * P], ctx_lo[:, c, t * P:(t + 1) * P],
                                               whi['v'][:, c, :], wlo['v'][:, c, :], c == 0, c == NC - 1)
                            mm.then_inc(acc_full, 1)
                        if k == 'S':
                            h, b = m // B, m % B
                            if m == 0:
                                if order is FIRST:
                                    pe.wait_ge(acc_free, PRE.index('K1') + 1)
                                else:
                                    pe.wait_ge(acc_free, base - USES + use_of(STEP, 'K1') + 1)
                                pe.wait_ge(kcols, i + 1)
                            pe.wait_ge(s_exp, 2 * (i * U + m) + 2)
                            for q in range(2):
                                cols = slice(b * S + q * P, b * S + (q + 1) * P)
                                mm = three(pe, s_bank(m)[:, q, :], qk_hi['q'][:, h, cols], qk_lo['q'][:, h, cols],
                                           k_hi[:, h, b, :], k_lo[:, h, b, :], True, True)
                            mm.then_inc(s_done, 1)
                        if k == 'T':
                            pe.wait_ge(s_norm, i * U + m + 1)
                            pe.wait_ge(t_free, i * U + m + 1)
                            for t in range(2):
                                for q in range(2):
                                    mm = pe.transpose(t_bank(m)[:, t * S + q * P:t * S + (q + 1) * P], prob[:, m % 4, q, t * P:(t + 1) * P], chip.ident[:, :])
                            mm.then_inc(t_done, 1)
                        if k == 'A':
                            pe.wait_ge(t_free, i * U + 2 * m + 4)
                            if m == 0:
                                pe.wait_ge(acc_free, base + use_of(order, 'V3') + 1)
                            for u in (2 * m, 2 * m + 1):
                                h, b = u // B, u % B
                                for t in range(2):
                                    mm = three(pe, acc(n)[:, (u % 2) * S:(u % 2 + 1) * S], v_hi[:, 2 * b + t, h * K0:(h + 1) * K0], v_lo[:, 2 * b + t, h * K0:(h + 1) * K0],
                                               pt_hi[:, u % 4, t * S:(t + 1) * S], pt_lo[:, u % 4, t * S:(t + 1) * S], t == 0, t == 1)
                            mm.then_inc(acc_full, 1)
                        if k == 'O':
                            if m == 0:
                                pe.wait_ge(o_split, i)
                                pe.wait_ge(acc_free, base)
                            for j in range(2):
                                t = 2 * m + j
                                for h in range(PAIR):
                                    mm = three(pe, acc(n)[:, j * D:(j + 1) * D], qk_hi['c'][:, h, t * P:(t + 1) * P], qk_lo['c'][:, h, t * P:(t + 1) * P],
                                               whi['o'][:, h, :], wlo['o'][:, h, :], h == 0, h == PAIR - 1)
                            mm.then_inc(acc_full, 1)

                steps(pe, body)
                last = END
                pe.wait_ge(acc_free, last)
                for h in range(H0):
                    for c in range(NC):
                        mm = pe.matmul(ps[:, 0, c * H0 + h:c * H0 + h + 1], wo_raw[:, h, c * P:(c + 1) * P], dv[:, h:h + 1], start=True, stop=True)
                mm.then_inc(acc_full, 1)
                for j in range(NT):
                    mm = pe.transpose(ps[0:H0, 2 + j // 4, (j % 4) * P:(j % 4 + 1) * P], pb[:, j, :, :].rearrange("p i h -> p (i h)"), chip.ident[:, :])
                mm.then_inc(acc_full, 1)
                pe.wait_ge(acc_free, last + 1)
                for c in range(NC):
                    mm = pe.transpose(ps[0:H0, 1, c * P:(c + 1) * P], bvo_T[:, c, :], chip.ident[:, :])
                mm.then_inc(acc_full, 1)
                pe.wait_ge(acc_free, last + 3)
                for j in range(NT):
                    mm = pe.matmul(ps[:, 4 + j // 2, (j % 2) * D:(j % 2 + 1) * D], pb_T[:, j * P:(j + 1) * P], bvo[:, :], start=True, stop=True)
                    if j % 2:
                        mm.then_inc(acc_full, 1)

            @block.scalar
            def _(act):
                act.sem_inc(s_exp, 4)
                act.wait_ge(ld_q, 16)
                act.activation(whi['q'][:, :, :], raw['q'][:, :, :], ACT.Copy, scale=C).then_inc(q_rounded, 1)
                act.wait_ge(cols_cur, 1)

                def qk(s, n, i, count):
                    h, half = int(s[1]) // 2, int(s[1]) % 2
                    act.wait_ge(acc_full, count + 1)
                    act.activation(project_out(s, h, half)[0], like(s, acc(n)), ACT.Identity,
                                   bias=qk_cols[:, 0 if s[0] == 'Q' else 1, h:h + 1]).then_inc(acc_hi, 1)

                for n, s in enumerate(PRE):
                    qk(s, n, 0, n)

                def body(i, order):
                    last = order is LAST
                    base = base_of(i) if order is not TAIL else END - 4
                    for s in act_order(order):
                        k, m = s[0], int(s[1])
                        if k == 'E':
                            act.wait_ge(s_max, i * U + m + 1)
                            act.wait_ge(t_done, i * U + m + 1)
                            for q in range(2):
                                act.activation(prob[:, m % 4, q, 0:S + 1], s_bank(m)[:, q, 0:S + 1], ACT.Exp,
                                               bias=negm[:, m % 4, q:q + 1], accum_out=tot[:, m % 4, q:q + 1]).then_inc(s_exp, 1)
                        elif k == 'T':
                            act.wait_ge(t_done, i * U + m + 5)
                            act.activation(pt_hi[:, m % 4, :], t_bank(m), ACT.Copy).then_inc(t_hi, 1)
                        elif k == 'R':
                            if not last:
                                act.wait_ge(ld_q, i * 16 + 32)
                                act.activation(whi['q'][:, :, :], raw['q'][:, :, :], ACT.Copy, scale=C).then_inc(q_rounded, 1)
                        elif k in 'QK':
                            if s == 'Q0':
                                act.wait_ge(cols_cur, 2 * i + 3)
                            qk(s, use_of(order, s), i + 1, base + use_of(order, s))
                        elif k in 'VA':
                            n = use_of(order, s)
                            act.wait_ge(acc_full, base + n + 1)
                            if s == 'A0':
                                act.wait_ge(cols_cur, 2 * i + 2)
                            if k == 'V':
                                act.activation(v_hi[:, 2 * m:2 * m + 2, :], acc(n).rearrange("p (j n) -> p j n", j=2), ACT.Copy).then_inc(acc_hi, 1)
                            else:
                                act.activation(qk_hi['c'][:, m // 2, (m % 2) * HALF:(m % 2 + 1) * HALF], acc(n), ACT.Identity,
                                               bias=v_cols[:, m // 2:m // 2 + 1]).then_inc(acc_hi, 1)

                steps(act, body)

            @block.vector
            def _(dve):
                dve.sem_inc(t_free, 2)
                dve.tensor_scalar(bcol[:, 0, :, :], hv(0).rearrange("p (i h) -> p i h", h=PAIR), C, None, ALU.mult)
                dve.tensor_copy(bcol[:, 1, :, :], hv(1).rearrange("p (i h) -> p i h", h=PAIR))
                dve.tensor_copy(bcol[:, 2, :, :], hv(4).rearrange("p (i h) -> p i h", h=PAIR))
                dve.memset(k_hi[:, :, :, S:KW].bitcast(F32), 0.0)
                dve.memset(k_lo[:, :, :, S:KW].bitcast(F32), 0.0)
                dve.tensor_tensor(dv[:, :], hv(3), hv(4), ALU.subtract)
                dve.tensor_copy(kb_hi[:, :, :], hv(2).rearrange("p (i h) -> p i h", h=PAIR)).then_inc(cols_ok, 1)
                dve.wait_ge(cols_ok, 1)
                dve.tensor_tensor(kb_lo[:, :, :], hv(2).rearrange("p (i h) -> p i h", h=PAIR), kb_hi[:, :, :].bitcast(F32), ALU.subtract).then_inc(cols_ok, 1)
                dve.wait_ge(q_rounded, 1)
                dve.scalar_tensor_tensor(wlo['q'][:, :, :], raw['q'][:, :, :], C, whi['q'][:, :, :].bitcast(F32), ALU.mult, ALU.subtract).then_inc(q_split, 1)
                dve.wait_ge(cols_ok, 2)
                dve.tensor_copy(qk_cols[:, :, :], bcol[:, 0:2, 0, :]).then_inc(cols_cur, 1)
                dve.wait_ge(cols_cur, 1)

                def qk(s, n, i, count):
                    h, half = int(s[1]) // 2, int(s[1]) % 2
                    hi, lo = project_out(s, h, half)
                    dve.wait_ge(acc_hi, count + 1)
                    dve.scalar_tensor_tensor(lo, like(s, acc(n)), qk_cols[:, 0 if s[0] == 'Q' else 1, h:h + 1],
                                             hi.bitcast(F32), ALU.add, ALU.subtract).then_inc(acc_free, 1)

                def key_cols(i):
                    for dst, src in ((k_hi, kb_hi), (k_lo, kb_lo)):
                        ins = dve.tensor_copy(dst[:, :, :, S:S + 1], src[:, i, :].bitcast(F32).unsqueeze(2).unsqueeze(3).to_broadcast([P, PAIR, B, 1]))
                    ins.then_inc(kcols, 1)

                for n, s in enumerate(PRE):
                    qk(s, n, 0, n)
                key_cols(0)

                def body(i, order):
                    last = order is LAST
                    base = base_of(i) if order is not TAIL else END - 4
                    hi_base = i * HIS + len(PRE)
                    his = [s for s in order if s[0] in 'VAQK']
                    for s in dve_order(order):
                        k, m = s[0], int(s[1])
                        if k == 'M':
                            dve.wait_ge(s_done, i * U + m + 1)
                            dve.tensor_reduce(negm[:, m % 4, :], s_bank(m)[:, :, 0:S + 1], AX.X, ALU.max, negate=True).then_inc(s_max, 1)
                        elif k == 'I':
                            dve.wait_ge(s_exp, 2 * (i * U + m) + 6)
                            dve.reciprocal(rtot[:, m % 4, :], tot[:, m % 4, :]).then_inc(s_sum, 1)
                        elif k == 'T':
                            dve.wait_ge(t_hi, i * U + m + 1)
                            dve.tensor_tensor(pt_lo[:, m % 4, :], t_bank(m), pt_hi[:, m % 4, :].bitcast(F32), ALU.subtract).then_inc(t_free, 1)
                        elif k == 'R':
                            dve.wait_ge(acc_free, base)
                            dve.tensor_copy(v_cols[:, :], bcol[:, 2, i, :]).then_inc(cols_cur, 1)
                            if not last:
                                dve.tensor_copy(qk_cols[:, :, :], bcol[:, 0:2, i + 1, :]).then_inc(cols_cur, 1)
                                dve.wait_ge(q_rounded, i + 2)
                                dve.scalar_tensor_tensor(wlo['q'][:, :, :], raw['q'][:, :, :], C, whi['q'][:, :, :].bitcast(F32),
                                                         ALU.mult, ALU.subtract).then_inc(q_split, 1)
                        elif k in 'QK':
                            if s == 'Q0':
                                dve.wait_ge(cols_cur, 2 * i + 3)
                            qk(s, use_of(order, s), i + 1, hi_base + his.index(s))
                            if s == 'K3':
                                key_cols(i + 1)
                        elif k == 'V':
                            dve.wait_ge(acc_hi, hi_base + his.index(s) + 1)
                            dve.tensor_tensor(v_lo[:, 2 * m:2 * m + 2, :], acc(use_of(order, s)).rearrange("p (j n) -> p j n", j=2),
                                              v_hi[:, 2 * m:2 * m + 2, :].bitcast(F32), ALU.subtract).then_inc(acc_free, 1)
                        elif k == 'A':
                            dve.wait_ge(acc_hi, hi_base + his.index(s) + 1)
                            cols = slice((m % 2) * HALF, (m % 2 + 1) * HALF)
                            dve.scalar_tensor_tensor(qk_lo['c'][:, m // 2, cols], acc(use_of(order, s)), v_cols[:, m // 2:m // 2 + 1],
                                                     qk_hi['c'][:, m // 2, cols].bitcast(F32), ALU.add, ALU.subtract).then_inc(acc_free, 1)
                        elif k == 'O':
                            n = use_of(order, s)
                            dve.wait_ge(acc_full, base + n + 1)
                            dve.tensor_tensor(chip.x[:, 2 * m:2 * m + 2, :], chip.x[:, 2 * m:2 * m + 2, :],
                                              acc(n).rearrange("p (j n) -> p j n", j=2), ALU.add).then_inc(acc_free, 1)

                steps(dve, body)
                last = END
                dve.wait_ge(acc_full, last + 1)
                dve.tensor_copy(bvo_T[:, :, :], ps[:, 0, 0:NC * H0].rearrange("p (c h) -> p c h", c=NC)).then_inc(acc_free, 1)
                dve.wait_ge(acc_full, last + 2)
                dve.tensor_copy(pb_T[:, :], ps[0:H0, 2:4, :].rearrange("p b n -> p (b n)")).then_inc(acc_free, 1)
                dve.wait_ge(acc_full, last + 3)
                dve.tensor_copy(bvo[:, :], ps[0:H0, 1, 0:D]).then_inc(acc_free, 1)
                for m in range(4):
                    dve.wait_ge(acc_full, last + 4 + m)
                    dve.tensor_tensor(chip.x[:, 2 * m:2 * m + 2, :], chip.x[:, 2 * m:2 * m + 2, :],
                                      ps[:, 4 + m, :].rearrange("p (j n) -> p j n", j=2), ALU.add)


def stage_mlp(chip, w1_raw, w2_raw, ld_w, h_hi, h_lo):
    nc, ps = chip.nc, chip.psum
    bias1 = lambda f: chip.hvecs[:, len(HVECS) * H0 + f:len(HVECS) * H0 + f + 1]
    with ExitStack() as st:
        sb = lambda n, s, t=F32R: st.enter_context(nc.sbuf_tensor(f"mlp_{n}", s, t))
        sem = lambda n: chip.semaphore(f"mlp_{n}")
        w1_hi, w1_lo = sb("w1_hi", [P, NC, FF]), sb("w1_lo", [P, NC, FF])
        w2_hi, w2_lo = sb("w2_hi", [P, NF, D]), sb("w2_lo", [P, NF, D])
        u = sb("u", [P, 4, BANK], F32)
        u_hi, u_lo = sb("u_hi", [P, NF, TOK]), sb("u_lo", [P, NF, TOK])
        w_hi_ok, w1_ok, w2_hi_ok, w2_ok, full, gelu, u_hi_ok, u_ok, out_full, out_free = (
            sem(n) for n in ("w1_hi_ok", "w1_ok", "w2_hi_ok", "w2_ok", "full", "gelu", "u_hi_ok", "u_ok", "out_full", "out_free"))
        part = lambda f: slice(f * P, (f + 1) * P)
        half = lambda n: slice((n % 2) * HALF, (n % 2 + 1) * HALF)
        NU = 2 * NF
        with nc.Block() as block:
            @block.scalar
            def _(act):
                act.wait_ge(ld_w, 32)
                for q in range(4):
                    act.activation(w1_hi[:, :, q * 256:(q + 1) * 256], w1_raw[:, :, q * 256:(q + 1) * 256], ACT.Copy).then_inc(w_hi_ok, 1)
                for n in range(NU):
                    act.wait_ge(full, n + 1)
                    if n >= 4:
                        act.wait_ge(u_ok, n - 3)
                    act.activation(u[:, n % 4, :], ps[:, n % 4, :], ACT.Gelu, bias=bias1(n // 2)).then_inc(gelu, 1)

            @block.gpsimd
            def _(pool):
                pool.wait_ge(ld_w, 32)
                for q in range(4):
                    pool.wait_ge(w2_hi_ok, q + 1)
                    pool.tensor_tensor(w2_lo[:, 2 * q:2 * q + 2, :], w2_raw[:, 2 * q:2 * q + 2, :],
                                       w2_hi[:, 2 * q:2 * q + 2, :].bitcast(F32), ALU.subtract).then_inc(w2_ok, 1)

            @block.vector
            def _(dve):
                dve.wait_ge(ld_w, 32)
                for q in range(4):
                    dve.wait_ge(w_hi_ok, q + 1)
                    cols = slice(q * 256, (q + 1) * 256)
                    dve.tensor_tensor(w1_lo[:, :, cols], w1_raw[:, :, cols], w1_hi[:, :, cols].bitcast(F32), ALU.subtract).then_inc(w1_ok, 1)
                for q in range(4):
                    dve.tensor_copy(w2_hi[:, 2 * q:2 * q + 2, :], w2_raw[:, 2 * q:2 * q + 2, :]).then_inc(w2_hi_ok, 1)
                for n in range(NU):
                    dve.wait_ge(gelu, n + 1)
                    dve.tensor_copy(u_hi[:, n // 2, half(n)], u[:, n % 4, :]).then_inc(u_hi_ok, 1)
                    dve.wait_ge(u_hi_ok, n + 1)
                    dve.tensor_tensor(u_lo[:, n // 2, half(n)], u[:, n % 4, :], u_hi[:, n // 2, half(n)].bitcast(F32), ALU.subtract).then_inc(u_ok, 1)
                for m in range(4):
                    dve.wait_ge(out_full, m + 1)
                    dve.tensor_tensor(chip.x[:, 2 * m:2 * m + 2, :], chip.x[:, 2 * m:2 * m + 2, :],
                                      ps[:, 4 + m, :].rearrange("p (j n) -> p j n", j=2), ALU.add).then_inc(out_free, 1)

            @block.tensor
            def _(pe):
                def three(out, l_hi, l_lo, r_hi, r_lo, first, last):
                    pe.matmul(out, l_hi, r_hi, start=first, stop=False)
                    pe.matmul(out, l_hi, r_lo, start=False, stop=False)
                    return pe.matmul(out, l_lo, r_hi, start=False, stop=last)

                for n in range(NU):
                    f = n // 2
                    pe.wait_ge(w1_ok, f // 2 + 1)
                    if n >= 4:
                        pe.wait_ge(gelu, n - 3)
                    for c in range(NC):
                        mm = three(ps[:, n % 4, :], w1_hi[:, c, part(f)], w1_lo[:, c, part(f)], h_hi[:, c, half(n)], h_lo[:, c, half(n)], c == 0, c == NC - 1)
                    mm.then_inc(full, 1)
                pe.wait_ge(u_ok, NU)
                pe.wait_ge(w2_ok, 4)
                for t in range(NT):
                    for f in range(NF):
                        mm = three(ps[:, 4 + t // 2, (t % 2) * D:(t % 2 + 1) * D], u_hi[:, f, part(t)], u_lo[:, f, part(t)], w2_hi[:, f, :], w2_lo[:, f, :], f == 0, f == NF - 1)
                    if t % 2:
                        mm.then_inc(out_full, 1)


E1 = 256
H1, S1 = 32, 8
KM = 32
NMIX = 5
KD = 64
L1_WEIGHTS = ['Wr', 'Wk', 'Wv', 'Wg', 'Wo', 'ffn_Wk', 'ffn_Wr', 'ffn_Wv']
R1 = S + 1


def layer1_memory(chip, st, d):
    nc = chip.nc
    """Weights and start values of layer 1, and the function that loads them."""
    sb = lambda n, s: st.enter_context(nc.sbuf_tensor(f"r_{n}", s, F32))
    w = {n: sb(n, [P, NC, E1]) for n in L1_WEIGHTS}
    m = {'w': w, 'maa_w1': sb("maa_w1", [P, NC, NMIX * KM]), 'maa_w2': sb("maa_w2", [P, E1]), 'maa_w2e': sb("maa_w2e", [KM, E1]),
         'decay_w1': sb("decay_w1", [P, NC, KD]), 'decay_w2': sb("decay_w2", [KD, E1]),
         's0': sb("s0", [P, NC, B, S1]), 'ld': chip.semaphore("ld_layer1")}
    ld = m['ld']
    count = [0]

    def load(sp):
        def go(dst, src):
            sp.dma_start(dst, src).then_inc(ld, 16)
            count[0] += 16

        for b in range(B):
            go(m['s0'][:, :, b, :], d['ctx_2048'][b, 2:2 + S1, :].rearrange("r (q e) -> (r q) e", e=S1).rearrange("(c p) e -> p c e", p=P))
        go(m['maa_w1'][:, :, :], d['L1_xattn_maa_w1'].rearrange("(c p) n -> p c n", p=P))
        go(m['maa_w2'][:, :], d['L1_xattn_maa_w2'][0:4].rearrange("i k n -> (i k) n"))
        go(m['maa_w2e'][:, :], d['L1_xattn_maa_w2'][4])
        go(m['decay_w1'][:, :, :], d['L1_xattn_decay_w1'].rearrange("(c p) n -> p c n", p=P))
        go(m['decay_w2'][:, :], d['L1_xattn_decay_w2'])
        for n in L1_WEIGHTS:
            go(w[n][:, :, :], d[f'L1_xattn_{n}_T'].rearrange("(c p) n -> p c n", p=P))
        sp.wait_ge(ld, count[0])

    return m, load


def stage_rwkv_mix(chip, m, xe, kT, vT, rT, wT, gT):
    nc, ps = chip.nc, chip.psum
    w = m['w']
    with ExitStack() as st:
        sb = lambda n, s, t=F32: st.enter_context(nc.sbuf_tensor(f"mix_{n}", s, t))
        sem = lambda n: chip.semaphore(f"mix_{n}")
        sx = sb("shift", [P, NC, B, S])
        first = sb("first", [P, NC, B, S])
        lowA, lowB = sb("lowA", [P, TOK]), sb("lowB", [KM, TOK])
        scaled = sb("scaled", [P, 2, NC, TOK])
        mixed = sb("mixed", [P, 2, NC, TOK])
        dec = sb("dec", [KD, TOK])
        e1 = sb("e1", [P, 2, BANK])
        th = sb("th", [P, 2, BANK])
        cur = lambda c: xe[:, c, :, 1:R1]
        flat = lambda ap: ap.rearrange("p b s -> p (b s)")
        batches = lambda ap: ap.rearrange("p (b s) -> p b s", s=S)
        MIX = {'w': 1, 'k': 0, 'v': 2, 'r': 3, 'g': 4}
        ORDER = 'wkvrg'
        uses = [('low', n, 'act') for n in range(4)]
        uses += [('mw', n, 'dve') for n in range(4)] + [('mk', n, 'dve') for n in range(4)] + [('d1', n, 'act') for n in range(2)]
        uses += [('mv', n, 'dve') for n in range(4)] + [('pk', n, 'act') for n in range(4)] + [('d2', n, 'act') for n in range(4)]
        uses += [('mr', n, 'dve') for n in range(4)] + [('pv', n, 'act') for n in range(4)] + [('mg', n, 'dve') for n in range(4)]
        uses += [('pr', n, 'act') for n in range(4)] + [('pg', n, 'dve') for n in range(4)]
        num = {u[:2]: i for i, u in enumerate(uses)}
        nth = lambda i: sum(u[2] == uses[i][2] for u in uses[:i + 1])
        full, act_free, dve_free, shifted, first_ok, low_ok, scaled_ok, mix_dve, mix_pool, dec_ok, e_ok, th_ok = (
            sem(n) for n in ("full", "act_read", "dve_read", "shifted", "first_ok", "low_ok", "scaled_ok", "mixed_dve",
                             "mixed_pool", "dec_ok", "e_ok", "th_ok"))
        ch = lambda n: (n // 2, n % 2)
        half = lambda n: slice((n % 2) * HALF, (n % 2 + 1) * HALF)
        bh = lambda n: slice(2 * (n % 2), 2 * (n % 2) + 2)

        with nc.Block() as block:
            @block.tensor
            def _(pe):
                def begin(key):
                    n = num[key]
                    if n >= 8:
                        pe.wait_ge(act_free if uses[n - 8][2] == 'act' else dve_free, nth(n - 8))
                    return ps[:, n % 8, :]

                def product(key, weight, cols, src, rows=P):
                    out = begin(key)[0:rows, :]
                    for c in range(NC):
                        mm = pe.matmul(out, weight[:, c, cols], src(c), start=c == 0, stop=c == NC - 1)
                    mm.then_inc(full, 1)

                for key in [u[:2] for u in uses]:
                    what, n = key
                    if what == 'low':
                        pe.wait_ge(first_ok, 2)
                        src = lambda c: flat(first[:, c, bh(n), :])
                        product(key, m['maa_w1'], slice(0, P) if n < 2 else slice(P, NMIX * KM), src, P if n < 2 else KM)
                    elif what[0] == 'm':
                        i, (c, _h) = MIX[what[1]], ch(n)
                        pe.wait_ge(low_ok, 4)
                        out = begin(key)
                        if i < 4:
                            lhs, rhs = m['maa_w2'][KM * i:KM * i + KM, c * P:(c + 1) * P], lowA[KM * i:KM * i + KM, half(n)]
                        else:
                            lhs, rhs = m['maa_w2e'][:, c * P:(c + 1) * P], lowB[:, half(n)]
                        tile = (KM * i, 0) if i < 4 else (0, 0)
                        pe.matmul(out, lhs, rhs, start=True, stop=True, tile_position=tile).then_inc(full, 1)
                    elif what == 'd1':
                        if n == 0:
                            pe.wait_ge(mix_dve, 1)
                            pe.wait_ge(mix_pool, 1)
                        product(key, m['decay_w1'], slice(0, KD), lambda c: mixed[:, 0, c, half(n)], KD)
                    elif what == 'd2':
                        pe.wait_ge(dec_ok, 2)
                        out = begin(key)
                        pe.matmul(out, m['decay_w2'][:, (n // 2) * P:(n // 2 + 1) * P], dec[:, half(n)], start=True, stop=True).then_inc(full, 1)
                    else:
                        i = ORDER.index(what[1])
                        if n == 0:
                            pe.wait_ge(mix_dve, i + 1)
                            pe.wait_ge(mix_pool, i + 1)
                        product(key, w['W' + what[1]], slice((n // 2) * P, (n // 2 + 1) * P), lambda c: mixed[:, i % 2, c, half(n)])

            @block.vector
            def _(dve):
                dve.tensor_copy(xe[:, :, :, 0:1], chip.vecs[:, :, PREV + B:PREV + 2 * B].unsqueeze(3)).then_inc(shifted, 1)
                dve.wait_ge(shifted, 1)
                for c in range(NC):
                    dve.tensor_tensor(sx[:, c, :, :], xe[:, c, :, 0:S], cur(c), ALU.subtract).then_inc(shifted, 1)
                for c in range(NC):
                    dve.wait_ge(shifted, c + 2)
                    dve.scalar_tensor_tensor(first[:, c, :, :], sx[:, c, :, :], chip.vec('L1_xattn_maa_x', c), cur(c), ALU.mult, ALU.add).then_inc(first_ok, 1)
                for i, x in enumerate(ORDER):
                    if i >= 2:
                        prior = ORDER[i - 2]
                        dve.wait_ge(full, num[('d1', 1) if prior == 'w' else ('p' + prior, 3)] + 1)
                        dve.wait_ge(mix_pool, i - 1)
                    for n in range(4):
                        c, h = ch(n)
                        dve.wait_ge(full, num[('m' + x, n)] + 1)
                        dve.scalar_tensor_tensor(batches(scaled[:, i % 2, c, half(n)]), batches(ps[:, num[('m' + x, n)] % 8, :]),
                                                 chip.vec('L1_xattn_maa_stack', c, MIX[x]), sx[:, c, bh(n), :], ALU.add, ALU.mult).then_inc(dve_free, 1)
                    dve.wait_ge(dve_free, nth(num[('m' + x, 3)]))
                    dve.tensor_tensor(batches(mixed[:, i % 2, 0, :]), batches(scaled[:, i % 2, 0, :]), cur(0), ALU.add).then_inc(mix_dve, 1)
                for n in range(4):
                    c, h = ch(n)
                    dve.wait_ge(th_ok, n + 1)
                    dve.scalar_tensor_tensor(gT[:, c, half(n)], th[:, n % 2, :], 1.0, ps[:, num[('pg', n)] % 8, :], ALU.add, ALU.mult).then_inc(dve_free, 1)

            @block.gpsimd
            def _(pool):
                for t in (kT, vT, wT):
                    pool.memset(t[:, :, :, 0:1], 0.0)
                for i, x in enumerate(ORDER):
                    pool.wait_ge(dve_free, nth(num[('m' + x, 3)]))
                    pool.tensor_tensor(batches(mixed[:, i % 2, 1, :]), batches(scaled[:, i % 2, 1, :]), cur(1), ALU.add).then_inc(mix_pool, 1)

            @block.scalar
            def _(act):
                for i, (what, n, reader) in enumerate(uses):
                    c, h = ch(n)
                    src = ps[:, i % 8, :]
                    if what == 'pg':
                        act.wait_ge(full, i + 1)
                        if n >= 2:
                            act.wait_ge(dve_free, nth(num[('pg', n - 2)]))
                        act.activation(th[:, n % 2, :], src, ACT.Tanh, scale=0.5).then_inc(th_ok, 1)
                        continue
                    if reader != 'act':
                        continue
                    act.wait_ge(full, i + 1)
                    if what == 'low':
                        dst, src = (lowA[:, half(n)], src) if n < 2 else (lowB[:, half(n)], src[0:KM, :])
                        act.activation(dst, src, ACT.Tanh).then_inc(act_free, 1)
                        if n == 3:
                            act.wait_ge(act_free, nth(i))
                            act.sem_inc(low_ok, 4)
                    elif what == 'd1':
                        act.activation(dec[:, half(n)], src[0:KD, :], ACT.Tanh).then_inc(act_free, 1)
                        if n == 1:
                            act.wait_ge(act_free, nth(i))
                            act.sem_inc(dec_ok, 2)
                    elif what == 'd2':
                        act.activation(e1[:, n % 2, :], src, ACT.Exp, bias=chip.vec('L1_xattn_time_decay', c)).then_inc(act_free, 1)
                        act.wait_ge(act_free, nth(i))
                        act.activation(wT[:, c, bh(n), 1:S], batches(e1[:, n % 2, :])[:, :, 0:S - 1], ACT.Exp, scale=-1.0).then_inc(e_ok, 1)
                        act.wait_ge(e_ok, n + 1)
                    elif what in ('pk', 'pv'):
                        act.activation((kT if what == 'pk' else vT)[:, c, bh(n), 1:R1], batches(src), ACT.Copy).then_inc(act_free, 1)
                    elif what == 'pr':
                        act.activation(rT[:, c, half(n)], src, ACT.Copy).then_inc(act_free, 1)


def stage_rwkv_scan(chip, m, kT, vT, rT, wT, gT):
    nc, ps = chip.nc, chip.psum
    HP = P // S1
    with ExitStack() as st:
        sb = lambda n, s, t=F32: st.enter_context(nc.sbuf_tensor(f"scan_{n}", s, t))
        sem = lambda n: chip.semaphore(f"scan_{n}")
        same = sb("same_head", [P, P])
        dmask = sb("d_mask", [P, S1])
        spread = sb("spread", [P, S1, P], F32R)
        gather = sb("gather", [P, S1, P])
        v_hi, v_lo = sb("v_hi", [P, NC, B, R1 + 1], F32R), sb("v_lo", [P, NC, B, R1 + 1], F32R)
        ruk = sb("ruk", [P, NC, TOK])
        kv = sb("kv", [P, 2, NC, B, S])
        state = sb("state", [P, 2, NC, B, S])
        z = sb("z", [P, 2, NC, TOK])
        att = sb("att", [P, NC, TOK])
        sq = sb("sq", [P, NC, TOK])
        epsc = sb("eps", [P, 1])
        (mats, dmask_ok, spread_ok, gather_ok, vcut, ruk_ok, v_full, kv_ok, s0_ok, st_ok, z_ok, g_full, ru_full, att_ok,
         mean_full, cent_ok, sq_ok, var_full, std_ok, rstd_ok, n_ok, gn_ok, gated, o_full) = (
            sem(n) for n in ("mats", "dmask_ok", "spread_ok", "gather_ok", "v_cut", "ruk_ok", "v_full", "kv_ok", "s0_ok",
                             "states_ok", "z_ok", "gathered", "ru_full", "att_ok", "mean_full", "centred", "squared", "var_full",
                             "std_ok", "rstd_ok", "normed", "affine", "gated", "out_full"))
        half = lambda n: slice((n % 2) * HALF, (n % 2 + 1) * HALF)
        bh = lambda n: slice(2 * (n % 2), 2 * (n % 2) + 2)
        batches = lambda ap: ap.rearrange("p (b s) -> p b s", s=S)
        flatb = lambda ap: ap.rearrange("p b s -> p (b s)")

        with nc.Block() as block:
            @block.gpsimd
            def _(pool):
                pool.memset(epsc[:, :], EPS0)
                pool.memset(gather[:, :, :], 0.0)
                pool.memset(same[:, :], 1.0).then_inc(mats, 1)
                v = same[:, :].rearrange("p (h e) -> p h e", e=S1)
                pool.wait_ge(mats, 1)
                pool.affine_select(out=v, in_=v, compare_op=ALU.is_ge, fill=0.0, base=0, pattern=[[-S1, HP], [0, S1]], channel_multiplier=1).then_inc(mats, 1)
                pool.wait_ge(mats, 2)
                pool.affine_select(out=v, in_=v, compare_op=ALU.is_ge, fill=0.0, base=S1 - 1, pattern=[[S1, HP], [0, S1]], channel_multiplier=-1).then_inc(mats, 1)
                for e in range(S1):
                    pool.wait_ge(st_ok, (e + 1) * NC)
                    if e >= 2:
                        pool.wait_ge(g_full, e - 1)
                    for c in range(NC):
                        pool.tensor_tensor(z[:, e % 2, c, :], rT[:, c, :], flatb(state[:, e % 2, c, :, :]), ALU.mult).then_inc(z_ok, 1)

            @block.vector
            def _(dve):
                dve.tensor_reduce(dmask[:, :], chip.ident[:, :].rearrange("p (h e) -> p e h", e=S1), AX.X, ALU.add).then_inc(dmask_ok, 1)
                dve.tensor_copy(v_hi[:, :, :, 0:R1], vT[:, :, :, :]).then_inc(vcut, 1)
                dve.wait_ge(vcut, 1)
                dve.tensor_tensor(v_lo[:, :, :, 0:R1], vT[:, :, :, :], v_hi[:, :, :, 0:R1].bitcast(F32), ALU.subtract).then_inc(vcut, 1)
                dve.wait_ge(mats, 3)
                dve.wait_ge(dmask_ok, 1)
                for e in range(S1):
                    dve.tensor_scalar(spread[:, e, :], same[:, :], dmask[:, e:e + 1], None, ALU.mult).then_inc(spread_ok, 1)
                for e in range(S1):
                    dve.tensor_copy(gather[:, e, e:P:S1], same[:, e:P:S1]).then_inc(gather_ok, 1)
                for e in range(S1):
                    for n in range(4):
                        c = n // 2
                        u = e * 4 + n
                        dve.wait_ge(v_full, u + 1)
                        if e >= 2:
                            dve.wait_ge(st_ok, (e - 2) * NC + c + 1)
                        dve.tensor_tensor(kv[:, e % 2, c, bh(n), :], kT[:, c, bh(n), 0:S], batches(ps[:, u % 4, :]), ALU.mult).then_inc(kv_ok, 1)
                    dve.wait_ge(kv_ok, 4 * e + 4)
                    dve.tensor_copy(kv[:, e % 2, :, :, 0:1], m['s0'][:, :, :, e:e + 1]).then_inc(s0_ok, 1)
                    dve.wait_ge(s0_ok, e + 1)
                    for c in range(NC):
                        if e >= 2:
                            dve.wait_ge(z_ok, (e - 2) * NC + c + 1)
                        dve.tensor_tensor_scan(flatb(state[:, e % 2, c, :, :]), flatb(wT[:, c, :, :]), flatb(kv[:, e % 2, c, :, :]), 0.0, ALU.mult, ALU.add).then_inc(st_ok, 1)
                    if e == 0:
                        for c in range(NC):
                            dve.scalar_tensor_tensor(batches(ruk[:, c, :]), batches(rT[:, c, :]), chip.vec('L1_xattn_faaaa', c), kT[:, c, :, 1:R1], ALU.mult, ALU.mult).then_inc(ruk_ok, 1)
                for n in range(4):
                    c = n // 2
                    dve.wait_ge(ru_full, n + 1)
                    dve.tensor_tensor(batches(att[:, c, half(n)]), batches(ps[:, n, :]), vT[:, c, bh(n), 1:R1], ALU.mult).then_inc(att_ok, 1)
                for n in range(4):
                    dve.wait_ge(att_ok, n + 1)
                    dve.wait_ge(g_full, S1)
                    dve.tensor_tensor(att[:, n // 2, half(n)], att[:, n // 2, half(n)], ps[:, 4 + n, :], ALU.add).then_inc(att_ok, 1)
                for n in range(4):
                    dve.wait_ge(mean_full, n + 1)
                    dve.scalar_tensor_tensor(att[:, n // 2, half(n)], ps[:, n, :], -1.0 / S1, att[:, n // 2, half(n)], ALU.mult, ALU.add).then_inc(cent_ok, 1)
                for n in range(4):
                    c = n // 2
                    dve.wait_ge(std_ok, n + 1)
                    dve.reciprocal(sq[:, c, half(n)], sq[:, c, half(n)]).then_inc(rstd_ok, 1)
                    dve.wait_ge(rstd_ok, n + 1)
                    dve.tensor_tensor(att[:, c, half(n)], att[:, c, half(n)], sq[:, c, half(n)], ALU.mult).then_inc(n_ok, 1)
                    dve.wait_ge(n_ok, n + 1)
                    dve.tensor_scalar(att[:, c, half(n)], att[:, c, half(n)], chip.vec('L1_xattn_gn_w', c), chip.vec('L1_xattn_gn_b', c), ALU.mult, ALU.add).then_inc(gn_ok, 1)
                    dve.wait_ge(gn_ok, n + 1)
                    dve.scalar_tensor_tensor(z[:, 0, c, half(n)], att[:, c, half(n)], 0.5, gT[:, c, half(n)], ALU.mult, ALU.mult).then_inc(gated, 1)
                for q in range(4):
                    dve.wait_ge(o_full, q + 1)
                    dve.tensor_tensor(chip.x[:, 2 * q:2 * q + 2, :], chip.x[:, 2 * q:2 * q + 2, :], ps[:, 4 + q, :].rearrange("p (j n) -> p j n", j=2), ALU.add)

            @block.scalar
            def _(act):
                for n in range(4):
                    act.wait_ge(cent_ok, n + 1)
                    act.activation(sq[:, n // 2, half(n)], att[:, n // 2, half(n)], ACT.Square).then_inc(sq_ok, 1)
                for n in range(4):
                    act.wait_ge(var_full, n + 1)
                    act.activation(sq[:, n // 2, half(n)], ps[:, 4 + n, :], ACT.Sqrt, scale=1.0 / S1, bias=epsc[:, :]).then_inc(std_ok, 1)

            @block.tensor
            def _(pe):
                pe.wait_ge(vcut, 2)
                for e in range(S1 + 1):
                    if e < S1:
                        pe.wait_ge(spread_ok, e + 1)
                        for n in range(4):
                            u = e * 4 + n
                            if u >= 4:
                                pe.wait_ge(kv_ok, u - 3)
                            c = n // 2
                            out = batches(ps[:, u % 4, :])
                            pe.matmul(out, spread[:, e, :], v_hi[:, c, bh(n), 0:S], start=True, stop=False)
                            pe.matmul(out, spread[:, e, :], v_lo[:, c, bh(n), 0:S], start=False, stop=True).then_inc(v_full, 1)
                    if e >= 1:
                        g = e - 1
                        if g == 0:
                            pe.wait_ge(gather_ok, S1)
                        pe.wait_ge(z_ok, NC * g + NC)
                        for n in range(4):
                            mm = pe.matmul(ps[:, 4 + n, :], gather[:, g, :], z[:, g % 2, n // 2, half(n)], start=g == 0, stop=g == S1 - 1)
                        mm.then_inc(g_full, 1)
                pe.wait_ge(ruk_ok, NC)
                for n in range(4):
                    pe.wait_ge(kv_ok, 4 * S1)
                    pe.matmul(ps[:, n, :], same[:, :], ruk[:, n // 2, half(n)], start=True, stop=True).then_inc(ru_full, 1)
                for n in range(4):
                    pe.wait_ge(att_ok, 4 + n + 1)
                    pe.matmul(ps[:, n, :], same[:, :], att[:, n // 2, half(n)], start=True, stop=True).then_inc(mean_full, 1)
                for n in range(4):
                    pe.wait_ge(sq_ok, n + 1)
                    pe.matmul(ps[:, 4 + n, :], same[:, :], sq[:, n // 2, half(n)], start=True, stop=True).then_inc(var_full, 1)
                for t in range(NT):
                    if t % 4 == 0:
                        pe.wait_ge(gated, 3 + t // 4)
                    for c in range(NC):
                        mm = pe.matmul(ps[:, 4 + t // 2, (t % 2) * D:(t % 2 + 1) * D], z[:, 0, c, t * P:(t + 1) * P], m['w']['Wo'][:, c, :], start=c == 0, stop=c == NC - 1)
                    if t % 2:
                        mm.then_inc(o_full, 1)


def stage_channel_mix(chip, m, xe):
    nc, ps = chip.nc, chip.psum
    w = m['w']
    with ExitStack() as st:
        sb = lambda n, s, t=F32: st.enter_context(nc.sbuf_tensor(f"cm_{n}", s, t))
        sem = lambda n: chip.semaphore(f"cm_{n}")
        sx, xk, xr = sb("shift", [P, NC, B, S]), sb("xk", [P, NC, B, S]), sb("xr", [P, NC, B, S])
        relu, kk = sb("relu", [P, NC, TOK]), sb("kk", [P, NC, TOK])
        gate = sb("gate", [P, NT, D])
        t1 = sb("t1", [P, NT, D])
        shifted, mixed, k_full, r_ok, kk_ok, r_full, th_ok, g_ok, v_full, t_ok = (
            sem(n) for n in ("shifted", "mixed", "k_full", "relu_ok", "kk_ok", "r_full", "tanh_ok", "gate_ok", "v_full", "t_ok"))
        half = lambda n: slice((n % 2) * HALF, (n % 2 + 1) * HALF)
        bh = lambda n: slice(2 * (n % 2), 2 * (n % 2) + 2)
        cur = lambda c: xe[:, c, :, 1:R1]
        with nc.Block() as block:
            @block.vector
            def _(dve):
                dve.tensor_copy(xe[:, :, :, 0:1], chip.vecs[:, :, PREV:PREV + B].unsqueeze(3)).then_inc(shifted, 1)
                dve.wait_ge(shifted, 1)
                for c in range(NC):
                    dve.tensor_tensor(sx[:, c, :, :], xe[:, c, :, 0:S], cur(c), ALU.subtract).then_inc(shifted, 1)
                for dst, v in ((xk, 'L1_xattn_ffn_maa_k'), (xr, 'L1_xattn_ffn_maa_r')):
                    for c in range(NC):
                        dve.wait_ge(shifted, c + 2)
                        dve.scalar_tensor_tensor(dst[:, c, :, :], sx[:, c, :, :], chip.vec(v, c), cur(c), ALU.mult, ALU.add).then_inc(mixed, 1)
                for n in range(4):
                    dve.wait_ge(r_ok, n + 1)
                    dve.scalar_tensor_tensor(kk[:, n // 2, half(n)], ps[:, n, :], 0.0, relu[:, n // 2, half(n)], ALU.max, ALU.mult).then_inc(kk_ok, 1)
                for q in range(4):
                    dve.wait_ge(th_ok, q + 1)
                    dve.tensor_scalar(gate[:, 2 * q:2 * q + 2, :], gate[:, 2 * q:2 * q + 2, :], 0.5, 0.5, ALU.mult, ALU.add).then_inc(g_ok, 1)
                for q in range(4):
                    dve.wait_ge(v_full, q + 1)
                    dve.wait_ge(g_ok, q + 1)
                    dve.tensor_tensor(t1[:, 2 * q:2 * q + 2, :], gate[:, 2 * q:2 * q + 2, :], ps[:, q, :].rearrange("p (j n) -> p j n", j=2), ALU.mult).then_inc(t_ok, 1)
                    dve.wait_ge(t_ok, q + 1)
                    dve.tensor_tensor(chip.x[:, 2 * q:2 * q + 2, :], chip.x[:, 2 * q:2 * q + 2, :], t1[:, 2 * q:2 * q + 2, :], ALU.add)

            @block.scalar
            def _(act):
                for n in range(4):
                    act.wait_ge(k_full, n + 1)
                    act.activation(relu[:, n // 2, half(n)], ps[:, n, :], ACT.Relu).then_inc(r_ok, 1)
                for q in range(4):
                    act.wait_ge(r_full, q + 1)
                    act.activation(gate[:, 2 * q:2 * q + 2, :], ps[:, 4 + q, :].rearrange("p (j n) -> p j n", j=2), ACT.Tanh, scale=0.5).then_inc(th_ok, 1)

            @block.tensor
            def _(pe):
                for n in range(4):
                    pe.wait_ge(mixed, 2)
                    for c in range(NC):
                        mm = pe.matmul(ps[:, n, :], w['ffn_Wk'][:, c, (n // 2) * P:(n // 2 + 1) * P], xk[:, c, bh(n), :].rearrange("p b s -> p (b s)"), start=c == 0, stop=c == NC - 1)
                    mm.then_inc(k_full, 1)
                pe.wait_ge(mixed, 4)
                for t in range(NT):
                    for c in range(NC):
                        mm = pe.matmul(ps[:, 4 + t // 2, (t % 2) * D:(t % 2 + 1) * D], xr[:, c, t // 2, (t % 2) * P:(t % 2 + 1) * P], w['ffn_Wr'][:, c, :], start=c == 0, stop=c == NC - 1)
                    if t % 2:
                        mm.then_inc(r_full, 1)
                pe.wait_ge(kk_ok, 4)
                for t in range(NT):
                    for c in range(NC):
                        mm = pe.matmul(ps[:, t // 2, (t % 2) * D:(t % 2 + 1) * D], kk[:, c, t * P:(t + 1) * P], w['ffn_Wv'][:, c, :], start=c == 0, stop=c == NC - 1)
                    if t % 2:
                        mm.then_inc(v_full, 1)


class Small:

    def __init__(self, tag, heads, kv_heads, width, scale, passes):
        self.tag, self.H, self.KV, self.W, self.scale, self.passes = tag, heads, kv_heads, width, scale, passes
        self.R = 32 // width
        self.G = heads // 4
        self.kv_cols = kv_heads * width
        self.per_chunk = P // (4 * width)


L2 = Small("l2", 16, 16, 16, 16 ** -0.5, 2)
L3 = Small("l3", 32, 8, 8, 1.0 / float(np.sqrt(np.float32(8.0))), 1)
BIG = 3e38


def stage_turn(chip, tag, rows, out, out2=None, rows2=None):
    nc, ps = chip.nc, chip.psum
    jobs = [(rows, out, n) for n in range(4)] + ([(rows2, out2, n) for n in range(4)] if rows2 is not None else [])
    turned = chip.semaphore(f"{tag}_turned")
    with nc.Block() as block:
        @block.tensor
        def _(pe):
            for k, (src, _dst, n) in enumerate(jobs):
                for t in range(4):
                    mm = pe.transpose(ps[:, k, t * P:(t + 1) * P], src[:, (n % 2) * 4 + t, (n // 2) * P:(n // 2 + 1) * P], chip.ident[:, :])
                mm.then_inc(turned, 1)

        def evacuate(eng, mine, copy):
            for k, (_src, dst, n) in enumerate(jobs):
                if k % 2 == mine:
                    eng.wait_ge(turned, k + 1)
                    copy(dst[:, n // 2, (n % 2) * HALF:(n % 2 + 1) * HALF], ps[:, k, :])

        @block.scalar
        def _(act):
            evacuate(act, 0, lambda o, i: act.activation(o, i, ACT.Copy))

        @block.vector
        def _(dve):
            evacuate(dve, 1, dve.tensor_copy)


def stage_small_project(chip, sh, wq, wk, wv, q_src, k_src, q_bias, k_bias, v_bias, mem):
    nc, ps = chip.nc, chip.psum
    tag, KC = sh.tag, max(1, sh.kv_cols // P)
    KR = min(P, sh.kv_cols)
    q_hi, q_lo, k_hi, k_lo, v1 = mem
    with ExitStack() as st:
        sb = lambda n, s, t=F32: st.enter_context(nc.sbuf_tensor(f"{tag}_{n}", s, t))
        sem = lambda n: chip.semaphore(f"{tag}_{n}")
        full = sb("qk_full", [P, 8, BANK])
        nq = sb("neg_bq", [P, NC])
        pe_full, whole, hi_ok, lo_ok, v_full, nq_ok = (sem(n) for n in ("p_full", "p_whole", "p_hi", "p_lo", "p_v", "p_bias"))
        pieces = [('q', c, h) for c in range(NC) for h in range(2)] + [('k', c, h) for c in range(KC) for h in range(2)]
        dst = lambda p, hi: ((q_hi if hi else q_lo) if p[0] == 'q' else (k_hi if hi else k_lo))[0:P if p[0] == 'q' else KR, p[1], p[2] * HALF:(p[2] + 1) * HALF]
        np_ = len(pieces)
        with nc.Block() as block:
            @block.tensor
            def _(pe):
                for i, (w, c, h) in enumerate(pieces):
                    cols = slice(h * HALF, (h + 1) * HALF)
                    rows = P if w == 'q' else KR
                    for k in range(NC):
                        mm = pe.matmul(ps[0:rows, i, :], (wq if w == 'q' else wk)[:, k, c * P:c * P + rows],
                                       (q_src if w == 'q' else k_src)[:, k, cols], start=k == 0, stop=k == NC - 1)
                    mm.then_inc(pe_full, 1)
                for t in range(NT):
                    if t % 2 == 0 and t // 2 < np_:
                        pe.wait_ge(whole, t // 2 + 1)
                    for k in range(NC):
                        mm = pe.matmul(ps[:, t // 2, (t % 2) * D:(t % 2) * D + sh.kv_cols], k_src[:, k, t * P:(t + 1) * P], wv[:, k, :],
                                       start=k == 0, stop=k == NC - 1)
                    if t % 2:
                        mm.then_inc(v_full, 1)

            @block.scalar
            def _(act):
                if q_bias:
                    act.wait_ge(nq_ok, NC)
                for i, (w, c, h) in enumerate(pieces):
                    rows = P if w == 'q' else KR
                    act.wait_ge(pe_full, i + 1)
                    bias = 0.0
                    if q_bias:
                        bias = nq[:, c:c + 1] if w == 'q' else k_bias[0:rows, :]
                    act.activation(full[0:rows, i, :], ps[0:rows, i, :], ACT.Identity, scale=-sh.scale if w == 'q' else 1.0, bias=bias).then_inc(whole, 1)

            @block.vector
            def _(dve):
                if q_bias:
                    for c in range(NC):
                        dve.tensor_scalar(nq[:, c:c + 1], q_bias(c), -sh.scale, None, ALU.mult).then_inc(nq_ok, 1)
                dve.memset(v1[:, :, :, sh.W:sh.W + 1], 1.0)
                if KR < P:
                    for half_k in (k_hi, k_lo):
                        dve.memset(half_k[KR:P, 0, :].bitcast(F32), 0.0)
                for i, p in enumerate(pieces):
                    rows = P if p[0] == 'q' else KR
                    dve.wait_ge(whole, i + 1)
                    dve.tensor_copy(dst(p, True), full[0:rows, i, :]).then_inc(hi_ok, 1)
                for t in range(NT):
                    dve.wait_ge(v_full, t // 2 + 1)
                    src = ps[:, t // 2, (t % 2) * D:(t % 2) * D + sh.kv_cols].rearrange("p (h e) -> p h e", e=sh.W)
                    if v_bias is None:
                        dve.tensor_copy(v1[:, t, :, 0:sh.W], src)
                    else:
                        dve.tensor_tensor(v1[:, t, :, 0:sh.W], src, v_bias.rearrange("p (h e) -> p h e", e=sh.W), ALU.add)

            @block.gpsimd
            def _(pool):
                for i, p in enumerate(pieces):
                    rows = P if p[0] == 'q' else KR
                    pool.wait_ge(hi_ok, i + 1)
                    pool.tensor_tensor(dst(p, False), full[0:rows, i, :], dst(p, True).bitcast(F32), ALU.subtract)


def stage_small_attention(chip, sh, mem, wo, mask_of, finish):
    nc, ps = chip.nc, chip.psum
    tag, H, W, G, R = sh.tag, sh.H, sh.W, sh.G, sh.R
    q_hi, q_lo, k_hi, k_lo, v1 = mem
    with ExitStack() as st:
        sb = lambda n, s, t=F32: st.enter_context(nc.sbuf_tensor(f"{tag}_{n}", s, t))
        sem = lambda n: chip.semaphore(f"{tag}_{n}")
        NK = sh.passes
        selq = sb("place_q", [P, 2, sh.per_chunk, 4, R, W], F32R)
        nselk = 1 if NK == 2 else 2
        selk = sb("place_k", [P, nselk, sh.per_chunk if NK == 2 else G, 4, R, W], F32R)
        qs, ks = sb("q_stack", [P, G, S], F32R), sb("k_stack", [P, NK * G, S], F32R)
        mask = sb("mask_neg", [P, 2 if sh is L3 else 1, S])
        sc = sb("scores", [P, 4, 2, S])
        m = sb("neg_max", [P, 4, 2])
        pr = sb("prob", [P, 4, 2, S])
        pT = sb("prob_T", [P, 4, BANK])
        rec = sb("inv_total", [P, 2, H])
        att = sb("att", [P, 2, H, W])
        attT = sb("att_T", [P, BANK])
        (zeroed, placed, sel_full, act_read, dve_read, s_full, s_read, p_ok, turned, act_ev, dve_ev, a_done, a_full, a_read,
         rec_ok, att_ok, mask_ok, s_begun) = (
            sem(n) for n in ("zeroed", "placed", "stack_full", "act_read", "dve_read", "scores_full", "scores_read", "exp_ok",
                             "turned", "turned_act", "turned_dve", "sum_done", "sums_full", "sums_read", "inv_ok", "att_ok", "mask_ok", "mask_begun"))
        pieces = [('q', g) for g in range(0, G, 2)] + [('k', g) for g in range(0, NK * G, 2)]
        NS = len(pieces)
        PER = NS // 2 + 1
        assert NS % 2 == 0 and H % 2 == 0

        with nc.Block() as block:
            @block.gpsimd
            def _(pool):
                pool.memset(selq[:].rearrange("p a g j r w -> p (a g j r w)").bitcast(F32), 0.0).then_inc(zeroed, 1)
                pool.memset(selk[:].rearrange("p a g j r w -> p (a g j r w)").bitcast(F32), 0.0).then_inc(zeroed, 1)

            @block.tensor
            def _(pe):
                pe.sem_inc(turned, 4)
                pe.sem_inc(a_done, 4)
                pe.wait_ge(placed, 1)

                with pe.Fori(0, B) as b:
                    base = b * PER
                    cols = bass.ds(b * S, S)
                    for s, (w, g0) in enumerate(pieces):
                        pe.wait_ge(act_read if s % 2 == 0 else dve_read, base + s // 2 + 1)
                        for j in range(2):
                            g = g0 + j
                            out = ps[:, 6 + s % 2, j * S:(j + 1) * S]
                            if w == 'q':
                                for part, src in enumerate((q_hi, q_lo)):
                                    mm = pe.matmul(out, selq[:, part, g % sh.per_chunk].rearrange("p j r w -> p (j r w)"),
                                                   src[:, g // sh.per_chunk, cols], start=part == 0, stop=part == 1)
                            elif NK == 2:
                                src = k_hi if g < G else k_lo
                                mm = pe.matmul(out, selk[:, 0, g % sh.per_chunk].rearrange("p j r w -> p (j r w)"),
                                               src[:, (g % G) // sh.per_chunk, cols], start=True, stop=True)
                            else:
                                for part, src in enumerate((k_hi, k_lo)):
                                    mm = pe.matmul(out, selk[:, part, g].rearrange("p j r w -> p (j r w)"), src[:, 0, cols],
                                                   start=part == 0, stop=part == 1)
                        mm.then_inc(sel_full, 1)

                    def scores(u):
                        g, j = u // 4, u % 4
                        rows = slice(32 * j, 32 * j + 32)
                        if u == 0:
                            pe.wait_ge(act_read, base + PER)
                            pe.wait_ge(dve_read, base + PER)
                        pe.wait_ge(s_read, b * H + u + 1)
                        for q in range(2):
                            for k in range(NK):
                                mm = pe.matmul(ps[:, u % 2, q * S:(q + 1) * S], qs[rows, g, q * P:(q + 1) * P], ks[rows, k * G + g, :],
                                               start=k == 0, stop=k == NK - 1, tile_position=(32 * j, 0))
                        mm.then_inc(s_full, 1)

                    def turn(u):
                        pe.wait_ge(p_ok, b * H + u + 5)
                        pe.wait_ge(act_ev if u % 2 == 0 else dve_ev, b * (H // 2) + u // 2 + 1)
                        for t in range(2):
                            for q in range(2):
                                mm = pe.transpose(ps[:, 2 + u % 2, t * S + q * P:t * S + (q + 1) * P], pr[:, u % 4, q, t * P:(t + 1) * P], chip.ident[:, :])
                        mm.then_inc(turned, 1)

                    def sums(u):
                        if u == 0:
                            pe.wait_ge(a_read, b + 1)
                        pe.wait_ge(act_ev if u % 2 == 0 else dve_ev, b * (H // 2) + u // 2 + 2)
                        for q in range(2):
                            for t in range(2):
                                mm = pe.matmul(ps[:, 4 + q, u * (W + 1):(u + 1) * (W + 1)], pT[:, u % 4, t * S + q * P:t * S + (q + 1) * P],
                                               v1[:, b * 2 + t, u * sh.KV // H, :], start=t == 0, stop=t == 1)
                        mm.then_inc(a_done, 1)

                    scores(0)
                    scores(1)
                    for u in range(H):
                        turn(u)
                        if u + 2 < H:
                            scores(u + 2)
                        if u:
                            sums(u - 1)
                    sums(H - 1)
                    pe.wait_ge(att_ok, b * 2 + 2)
                    pe.wait_ge(act_read, base + PER)
                    for q in range(2):
                        for c in range(NC):
                            mm = pe.transpose(ps[:, 6, (q * 2 + c) * P:(q * 2 + c + 1) * P], att[:, q].rearrange("p h w -> p (h w)")[:, c * P:(c + 1) * P], chip.ident[:, :])
                    mm.then_inc(sel_full, 1)
                    pe.wait_ge(act_read, base + PER + 1)
                    pe.wait_ge(dve_read, base + PER)
                    for q in range(2):
                        for c in range(NC):
                            mm = pe.matmul(ps[:, 7, q * D:(q + 1) * D], attT[:, (q * 2 + c) * P:(q * 2 + c + 1) * P], wo[:, c, :], start=c == 0, stop=c == NC - 1)
                    mm.then_inc(sel_full, 1)

            def stack_out(s):
                w, g0 = pieces[s]
                return (qs if w == 'q' else ks)[:, g0:g0 + 2, :], ps[:, 6 + s % 2, :].rearrange("p (g s) -> p g s", g=2)

            @block.scalar
            def _(act):
                act.sem_inc(act_read, 1)
                act.sem_inc(act_ev, 1)
                act.sem_inc(p_ok, 4)
                with act.Fori(0, B) as b:
                    for s in range(0, NS, 2):
                        act.wait_ge(sel_full, b * (NS + 2) + s + 1)
                        act.activation(*stack_out(s), ACT.Copy).then_inc(act_read, 1)
                    for u in range(H + 1):
                        if u < H:
                            act.wait_ge(s_read, b * H + u + 3)
                            act.wait_ge(turned, b * H + u + 1)
                            for q in range(2):
                                e = act.activation(pr[:, u % 4, q, :], sc[:, u % 4, q, :], ACT.Exp, scale=-1.0, bias=m[:, u % 4, q:q + 1])
                            e.then_inc(p_ok, 1)
                        t = u - 1
                        if t >= 0 and t % 2 == 0:
                            act.wait_ge(turned, b * H + t + 5)
                            act.wait_ge(a_done, b * H + t + 1)
                            act.activation(pT[:, t % 4, :], ps[:, 2, :], ACT.Copy).then_inc(act_ev, 1)
                    act.wait_ge(sel_full, b * (NS + 2) + NS + 1)
                    act.activation(attT[:, :], ps[:, 6, :], ACT.Copy).then_inc(act_read, 1)

            @block.vector
            def _(dve):
                dve.sem_inc(dve_read, 1)
                dve.sem_inc(dve_ev, 1)
                dve.sem_inc(s_read, 2)
                dve.sem_inc(a_read, 1)
                dve.wait_ge(zeroed, 2)
                ident = lambda n, cols: chip.ident[:, 0:n * cols].rearrange("p (g j w) -> p g j w", g=n, w=W)
                last = None
                for part in range(2):
                    for r in range(R):
                        if r % 2 == part:
                            for g in range(sh.per_chunk):
                                last = dve.tensor_copy(selq[:, part, g, :, r, :], chip.ident[:, g * 4 * W:(g + 1) * 4 * W].rearrange("p (j w) -> p j w", w=W))
                if NK == 2:
                    for r in range(R):
                        for g in range(sh.per_chunk):
                            last = dve.tensor_copy(selk[:, 0, g, :, r, :], chip.ident[:, g * 4 * W:(g + 1) * 4 * W].rearrange("p (j w) -> p j w", w=W))
                else:
                    for part in range(2):
                        for r in range(2 * part, 2 * part + 2):
                            for j in range(4):
                                last = dve.tensor_copy(selk[:, part, :, j, r, :], chip.ident[:, 0:G * W].rearrange("p (g w) -> p g w", w=W))
                last.then_inc(placed, 1)
                with dve.Fori(0, B) as b:
                    mask_of(dve, b, mask, mask_ok)
                    for s in range(1, NS, 2):
                        dve.wait_ge(sel_full, b * (NS + 2) + s + 1)
                        dve.tensor_copy(*stack_out(s)).then_inc(dve_read, 1)
                    for u in range(H + 2):
                        if u < H:
                            dve.wait_ge(s_full, b * H + u + 1)
                            dve.wait_ge(p_ok, b * H + u + 1)
                            dve.sem_inc(s_begun, 1)
                            for q in range(2):
                                e = dve.tensor_tensor_reduce(sc[:, u % 4, q, :], ps[:, u % 2, q * S:(q + 1) * S], mask[:, q if sh is L3 else 0, :],
                                                             1.0, BIG, ALU.add, ALU.min, m[:, u % 4, q:q + 1])
                            e.then_inc(s_read, 1)
                        t = u - 2
                        if t >= 0 and t % 2 == 1:
                            dve.wait_ge(turned, b * H + t + 5)
                            dve.wait_ge(a_done, b * H + t + 1)
                            dve.tensor_copy(pT[:, t % 4, :], ps[:, 3, :]).then_inc(dve_ev, 1)
                    dve.wait_ge(a_done, b * H + H + 4)
                    for q in range(2):
                        a = ps[:, 4 + q, 0:H * (W + 1)].rearrange("p (h w) -> p h w", w=W + 1)
                        dve.reciprocal(rec[:, q, :].unsqueeze(2), a[:, :, W:W + 1]).then_inc(rec_ok, 1)
                    for q in range(2):
                        a = ps[:, 4 + q, 0:H * (W + 1)].rearrange("p (h w) -> p h w", w=W + 1)
                        dve.wait_ge(rec_ok, b * 2 + q + 1)
                        e = dve.tensor_tensor(att[:, q], a[:, :, 0:W], rec[:, q, :].unsqueeze(2).to_broadcast([P, H, W]), ALU.mult)
                        e.then_inc(att_ok, 1)
                    dve.wait_ge(att_ok, b * 2 + 2)
                    dve.sem_inc(a_read, 1)
                    dve.wait_ge(sel_full, b * (NS + 2) + NS + 2)
                    finish(dve, b, ps[:, 7, :].rearrange("p (q n) -> p q n", q=2)).then_inc(dve_read, 1)

            if sh is L3:
                block.sync(mask_of.load)


def stage_final_norm(chip, out):
    nc = chip.nc
    with ExitStack() as st:
        sb = lambda n, s: st.enter_context(nc.sbuf_tensor(f"fin_{n}", s, F32))
        sem = lambda n: chip.semaphore(f"fin_{n}")
        bn, mv, ve, rstd = sb("bn", [P, NT, 6]), sb("mean_var", [P, NT, 2]), sb("var_eps", [P, NT]), sb("rstd", [P, NT])
        y, z = sb("y", [P, NT, D]), sb("z", [P, NT, D])
        stats, aggr, var_ok, rstd_ok, y_ok, z_ok, o_ok, stored = (sem(n) for n in ("stats", "aggr", "var_ok", "rstd_ok", "y_ok", "z_ok", "o_ok", "stored"))
        R = ROWS.index('L3_xattn_gamma')
        with nc.Block() as block:
            @block.gpsimd
            def _(pool):
                pool.wait_ge(var_ok, 1)
                pool.tensor_tensor(rstd[:, :], ve[:, :], chip.expo[:, :], ALU.pow).then_inc(rstd_ok, 1)

            @block.vector
            def _(dve):
                for j in range(NT):
                    dve.bn_stats(bn[:, j, :], chip.x[:, j, :]).then_inc(stats, 1)
                for j in range(NT):
                    dve.wait_ge(stats, j + 1)
                    dve.bn_aggr(mv[:, j, :], bn[:, j, :]).then_inc(aggr, 1)
                dve.wait_ge(aggr, NT)
                dve.tensor_scalar(ve[:, :], mv[:, :, 1], 1e-6, None, ALU.add).then_inc(var_ok, 1)
                dve.wait_ge(rstd_ok, 1)
                for j in range(NT):
                    dve.tensor_scalar(y[:, j, :], chip.x[:, j, :], mv[:, j, 0:1], rstd[:, j:j + 1], ALU.subtract, ALU.mult).then_inc(y_ok, 1)
                    if j % 2:
                        q = j // 2
                        two = slice(2 * q, 2 * q + 2)
                        dve.wait_ge(y_ok, j + 1)
                        dve.tensor_tensor(z[:, two, :], y[:, two, :], chip.rows[:, R:R + 1, :].to_broadcast([P, 2, D]), ALU.mult).then_inc(z_ok, 1)
                        dve.wait_ge(z_ok, q + 1)
                        dve.tensor_tensor(y[:, two, :], z[:, two, :], chip.rows[:, R + 1:R + 2, :].to_broadcast([P, 2, D]), ALU.add).then_inc(o_ok, 1)

            @block.sync
            def _(sp):
                for q in range(4):
                    sp.wait_ge(o_ok, q + 1)
                    sp.dma_start(tiles_of(out)[:, 2 * q:2 * q + 2, :], y[:, 2 * q:2 * q + 2, :]).then_inc(stored, 16)
                sp.wait_ge(stored, 64)


def layers_2_and_3(chip, d, out):
    nc = chip.nc
    with ExitStack() as both:
        sb = lambda n, s, t=F32: both.enter_context(nc.sbuf_tensor(n, s, t))
        ld = chip.semaphore("ld_layers23")
        w2 = {n: sb(f"l2_w{n}", [P, NC, D]) for n in 'qkvo'}
        w3 = {n: sb(f"l3_w{n}", [P, NC, L3.kv_cols if n in 'kv' else D]) for n in 'qkvo'}
        mask8 = sb("mask_bytes", [P, B * S], U8)
        gate = sb("gate", [P, 1])
        bk3, bv3 = sb("l3_bk", [L3.kv_cols, 1]), sb("l3_bv", [P, L3.kv_cols])
        aT, cT, xT = sb("ctx_normed_T", [P, NC, TOK]), sb("ctx_T", [P, NC, TOK]), sb("x_T", [P, NC, TOK])
        mask3 = sb("mask3", [P, 2, S])
        maskf, masks2 = sb("mask_f", [P, B, S]), sb("mask2", [P, B, S])
        dv_ok, ld3, neg_ok = (chip.semaphore(n) for n in ("mask2_ok", "ld_mask3", "mask3_taken"))

        def load(sp):
            total = 0
            for n in 'qkvo':
                sp.dma_start(w2[n][:, :, :], d[f'L2_xattn_W{n}_T'].rearrange("(c p) n -> p c n", p=P)).then_inc(ld, 16)
                sp.dma_start(w3[n][:, :, :], d[f'L3_xattn_W{n}'].rearrange("(c p) n -> p c n", p=P)).then_inc(ld, 16)
            sp.dma_start(mask8[:, :], d['mask_BxS2_bf1'].rearrange("(a b) s -> a (b s)", a=1).to_broadcast([P, B * S])).then_inc(ld, 16)
            sp.dma_start(gate[:, :], d['L2_xattn_gate'].rearrange("(a n) -> a n", a=1).to_broadcast([P, 1])).then_inc(ld, 16)
            sp.dma_start(bk3[:, :], d['L3_xattn_bk'].rearrange("(n a) -> n a", a=1)).then_inc(ld, 16)
            sp.dma_start(bv3[:, :], d['L3_xattn_bv'].rearrange("(a n) -> a n", a=1).to_broadcast([P, L3.kv_cols])).then_inc(ld, 16)
            sp.wait_ge(ld, 16 * 12)

        flat = lambda c, half: aT[:, c, half * HALF:(half + 1) * HALF].rearrange("p (b s) -> p b s", b=2)
        stage_layernorm(chip, "ln_ctx", chip.ctx, lambda c: chip.vec('L2_xattn_ln_gamma', c), lambda c: chip.vec('L2_xattn_ln_beta', c),
                        EPS0, plain=flat, prefetch=load)
        stage_turn(chip, "t2", chip.x, xT, cT, chip.ctx)

        steps = chip.semaphore("mask_steps")
        with nc.Block() as block:
            @block.vector
            def _(dve):
                mf = maskf[:, :, :].rearrange("p b s -> p (b s)")
                dve.tensor_copy(mf, mask8[:, :]).then_inc(steps, 1)
                dve.wait_ge(steps, 1)
                dve.tensor_scalar(mf, mf, 1.0, -BIG, ALU.subtract, ALU.mult).then_inc(steps, 1)
                dve.wait_ge(steps, 2)
                dve.tensor_scalar(masks2[:, :, :].rearrange("p b s -> p (b s)"), mf, BIG, None, ALU.mult)

            @block.scalar
            def _(act):
                act.activation(gate[:, :], gate[:, :], ACT.Tanh)

        def halves(stack, sh):
            t = lambda n, s, dt: stack.enter_context(nc.sbuf_tensor(f"{sh.tag}_{n}", s, dt))
            KC = max(1, sh.kv_cols // P)
            return (t("q_hi", [P, NC, TOK], F32R), t("q_lo", [P, NC, TOK], F32R), t("k_hi", [P, KC, TOK], F32R), t("k_lo", [P, KC, TOK], F32R),
                    t("v_ones", [P, NT, sh.KV, sh.W + 1], F32))

        with ExitStack() as l2:
            mem = halves(l2, L2)
            stage_small_project(chip, L2, w2['q'], w2['k'], w2['v'], xT, aT, None, None, None, mem)

            def mask_of(dve, b, tile, ok):
                dve.tensor_copy(tile[:, 0, :], masks2[:, b, :]).then_inc(ok, 1)
                dve.wait_ge(ok, b + 1)

            def finish(dve, b, o):
                rows = chip.x[:, bass.ds(b * 2, 2), :]
                return dve.scalar_tensor_tensor(rows, o, gate[:, :], rows, ALU.mult, ALU.add)

            stage_small_attention(chip, L2, mem, w2['o'], mask_of, finish)

        stage_turn(chip, "t3", chip.x, xT)
        with ExitStack() as l3:
            mem = halves(l3, L3)
            stage_small_project(chip, L3, w3['q'], w3['k'], w3['v'], xT, cT, lambda c: chip.vec('L3_xattn_bq', c), bk3, bv3[:, :], mem)

            def mask_of(dve, b, tile, ok):
                dve.wait_ge(ld3, b * 16 + 16)
                dve.tensor_scalar(tile[:, :, :], mask3[:, :, :], -1.0, None, ALU.mult).then_inc(ok, 1)
                dve.wait_ge(ok, b + 1)
                dve.sem_inc(neg_ok, 1)

            def load_masks(sp):
                src = d['mask_Bx1xSxS2_ff0'].rearrange("b a (u p) t -> p (b a u) t", p=P)
                sp.dma_start(mask3[:, :, :], src[:, 0:2, :]).then_inc(ld3, 16)
                with sp.Fori(1, B) as b:
                    sp.wait_ge(neg_ok, b)
                    sp.dma_start(mask3[:, :, :], src[:, bass.ds(b * 2, 2), :]).then_inc(ld3, 16)

            mask_of.load = load_masks

            def finish(dve, b, o):
                rows = chip.x[:, bass.ds(b * 2, 2), :]
                return dve.tensor_tensor(rows, o, rows, ALU.add)

            with nc.Block() as block:
                @block.vector
                def _(dve):
                    r = ROWS.index('L3_xattn_bo')
                    dve.tensor_tensor(chip.x[:, :, :], chip.x[:, :, :], chip.rows[:, r:r + 1, :].to_broadcast([P, NT, D]), ALU.add)
            stage_small_attention(chip, L3, mem, w3['o'], mask_of, finish)
        stage_final_norm(chip, out)


def build(nc, d, out):
    with ExitStack() as stack:
        chip = Chip(nc, stack)
        with ExitStack() as l0:
            sb = lambda n, s, t=F32R: l0.enter_context(nc.sbuf_tensor(n, s, t))
            ctx_hi, ctx_lo = sb("ctxT_hi", [P, NC, TOK]), sb("ctxT_lo", [P, NC, TOK])
            h_hi, h_lo = sb("hT_hi", [P, NC, TOK]), sb("hT_lo", [P, NC, TOK])
            stage_setup(chip, d, ctx_hi, ctx_lo)
            for a in (1, 2):
                L = f"L0_xattn_ln{a}_"
                stage_layernorm(chip, f"ln{a}", chip.x, lambda c: chip.vec(L + "scale", c), lambda c: chip.vec(L + "offset", c),
                                EPS0, hi=h_hi, lo=h_lo, add=ROWS.index(f"L0_xattn_bo{a}"))
                stage_cross_attention(chip, d, a, h_hi, h_lo, ctx_hi, ctx_lo)
            w1_raw, w2_raw = sb("w_fc1_raw", [P, NC, FF], F32), sb("w_fc2_raw", [P, NF, D], F32)
            ld_w = chip.semaphore("ld_mlp")

            def load_mlp(sp):
                sp.dma_start(w1_raw[:, :, :], d['L0_xattn_w_fc1'].rearrange("(c p) n -> p c n", p=P)).then_inc(ld_w, 16)
                sp.dma_start(w2_raw[:, :, :], d['L0_xattn_w_fc2'].rearrange("(f p) n -> p f n", p=P)).then_inc(ld_w, 16)

            L = "L0_xattn_ln_mlp_"
            stage_layernorm(chip, "ln_mlp", chip.x, lambda c: chip.vec(L + "scale", c), lambda c: chip.vec(L + "offset", c),
                            EPS0, hi=h_hi, lo=h_lo, add=ROWS.index("L0_xattn_b_fc2"), prefetch=load_mlp)
            stage_mlp(chip, w1_raw, w2_raw, ld_w, h_hi, h_lo)
        chip.renew_semaphores()
        with ExitStack() as l1:
            sb = lambda n, s: l1.enter_context(nc.sbuf_tensor(n, s, F32))
            m, load = layer1_memory(chip, l1, d)
            xe = sb("xn_T", [P, NC, B, R1])
            after = lambda c, half: xe[:, c, 2 * half:2 * half + 2, 1:R1]
            stage_layernorm(chip, "ln_r1", chip.x, lambda c: chip.vec('L1_xattn_ln1_w', c), lambda c: chip.vec('L1_xattn_ln1_b', c),
                            EPS0, plain=after, prefetch=load)
            with ExitStack() as seq:
                sq = lambda n, s: seq.enter_context(nc.sbuf_tensor(n, s, F32))
                kT, vT = sq("k_T", [P, NC, B, R1]), sq("v_T", [P, NC, B, R1])
                wT = sq("w_T", [P, NC, B, S])
                rT, gT = sq("r_T", [P, NC, TOK]), sq("g_T", [P, NC, TOK])
                stage_rwkv_mix(chip, m, xe, kT, vT, rT, wT, gT)
                stage_rwkv_scan(chip, m, kT, vT, rT, wT, gT)
            stage_layernorm(chip, "ln_r2", chip.x, lambda c: chip.vec('L1_xattn_ln2_w', c), lambda c: chip.vec('L1_xattn_ln2_b', c),
                            EPS0, plain=after)
            stage_channel_mix(chip, m, xe)
        layers_2_and_3(chip, d, out)


_DIRECT = ['x', 'ctx_2048'] + [f'L0_xattn_w{n}{a}' for a in (1, 2) for n in 'qkvo'] + ['L0_xattn_w_fc1', 'L0_xattn_w_fc2']
_DIRECT += [f'L1_xattn_{n}' for n in ('maa_w1', 'maa_w2', 'decay_w1', 'decay_w2')]
_DIRECT += ['mask_BxS2_bf1', 'mask_Bx1xSxS2_ff0', 'L2_xattn_gate', 'L3_xattn_bk', 'L3_xattn_bv'] + [f'L3_xattn_W{n}' for n in 'qkvo']
_TURNED = [f'L1_xattn_{n}' for n in L1_WEIGHTS] + [f'L2_xattn_W{n}' for n in 'qkvo']


def kernel(**inputs):
    import numpy as _np
    import concourse.bacc as _bacc
    from concourse import mybir as _mybir
    from concourse.bass_utils import run_bass_kernel_spmd as _run

    laid = {n: _np.ascontiguousarray(inputs[n]) for n in _DIRECT}
    laid.update({n + '_T': _np.ascontiguousarray(_np.transpose(inputs[n])) for n in _TURNED})
    laid['vecs'] = _np.concatenate([_np.reshape(inputs[n], (-1, D)) for n in VECS]
                                   + [_np.reshape(inputs['ctx_2048'][:, i], (-1, D)) for i in range(2)], 0)
    laid['hvecs'] = _np.concatenate([_np.reshape(inputs[n], (-1, K0)) for n in HVECS + ['L0_xattn_b_fc1']], 0)
    laid['rows'] = _np.concatenate([_np.reshape(inputs[n], (-1,)) for n in ROWS], 0)
    nc = _bacc.Bacc("TRN2", target_bir_lowering=False, num_devices=1)
    arrays, d = {}, {}
    for name, a in laid.items():
        arrays[f"in_{name}"] = a
        d[name] = nc.dram_tensor(f"in_{name}", a.shape, _mybir.dt.from_np(a.dtype), kind="ExternalInput").ap()
    out = nc.dram_tensor("out_0_dram", (B, S, D), F32, kind="ExternalOutput").ap()
    build(nc, d, out)
    r = _run(nc, [arrays], core_ids=[0])
    return r.results[0]["out_0_dram"]
```

```python
from contextlib import ExitStack

import numpy as np

import concourse.bass as bass
from concourse import mybir

F32 = mybir.dt.float32
F32R = mybir.dt.float32r
U8 = mybir.dt.uint8
ALU = mybir.AluOpType
ACT = mybir.ActivationFunctionType
AX = mybir.AxisListType

P = 128
B, S, D = 4, 256, 256
TOK = B * S
NT = TOK // P
NC = D // P
H0, K0 = 16, 128
PAIR = 2
NPAIR = H0 // PAIR
HW = PAIR * K0
FF = 1024
NF = FF // P
EPS0 = 1e-5
HALF = TOK // 2
BANK = 512

VECS = ['L0_xattn_ln1_scale', 'L0_xattn_ln1_offset', 'L0_xattn_ln2_scale', 'L0_xattn_ln2_offset',
        'L0_xattn_ln_mlp_scale', 'L0_xattn_ln_mlp_offset', 'L1_xattn_ln1_w', 'L1_xattn_ln1_b',
        'L1_xattn_ln2_w', 'L1_xattn_ln2_b', 'L1_xattn_maa_x', 'L1_xattn_maa_stack', 'L1_xattn_time_decay',
        'L1_xattn_faaaa', 'L1_xattn_gn_w', 'L1_xattn_gn_b', 'L1_xattn_ffn_maa_k', 'L1_xattn_ffn_maa_r',
        'L2_xattn_ln_gamma', 'L2_xattn_ln_beta', 'L3_xattn_bq']
VROWS = {}
for _n in VECS:
    VROWS[_n] = sum(5 if m == 'L1_xattn_maa_stack' else 1 for m in VECS[:VECS.index(_n)])
PREV = len(VECS) + 4
NV = PREV + 2 * B
HVECS = [f'L0_xattn_{n}{a}' for a in (1, 2) for n in ('bq', 'bk', 'bias_k', 'bias_v', 'bv')]
NHV = len(HVECS) * H0 + NF
ROWS = ['L0_xattn_bo1', 'L0_xattn_bo2', 'L0_xattn_b_fc2', 'L3_xattn_bo', 'L3_xattn_gamma', 'L3_xattn_beta']


class Chip:

    def __init__(self, nc, stack):
        self.nc = nc

        def sb(name, shape, dt=F32):
            return stack.enter_context(nc.sbuf_tensor(name, shape, dt))

        self.x = sb("x_rows", [P, NT, D])
        self.ctx = sb("ctx_rows", [P, NT, D])
        self.ident = sb("ident", [P, P])
        self.vecs = sb("vecs_T", [P, NC, NV])
        self.hvecs = sb("hvecs_T", [P, NHV])
        self.rows = sb("rows_bc", [P, len(ROWS), D])
        self.expo = sb("minus_half", [P, NT])
        self.psum = stack.enter_context(nc.psum_tensor("psum", [P, 8, BANK], F32))

        self.semaphores = []

    def semaphore(self, name):
        self.semaphores.append(self.nc.alloc_semaphore(name))
        return self.semaphores[-1]

    def renew_semaphores(self):
        self.nc.all_engine_barrier()
        self.nc.clear_and_free_semaphores(self.semaphores)
        self.nc.all_engine_barrier()
        self.semaphores = []

    def vec(self, name, c, i=0):
        r = VROWS[name] + i
        return self.vecs[:, c, r:r + 1]


def tiles_of(dram):
    return dram.rearrange("b (u p) d -> p (b u) d", p=P)


def stage_setup(chip, d, ctx_hi, ctx_lo):
    nc, ps = chip.nc, chip.psum
    with ExitStack() as st:
        sb = lambda n, s, t=F32: st.enter_context(nc.sbuf_tensor(n, s, t))
        sem = lambda n: chip.semaphore(n)
        vraw = sb("vecs_raw", [NV, D])
        hraw = sb("hvecs_raw", [NHV // 2, 2, K0])
        ld_ctx, ld_vec, ld_x, ld_rows = sem("ld_ctx"), sem("ld_vec"), sem("ld_x"), sem("ld_rows")
        ident_zero, ident_ok, turned, hi_done, lo_done, vec_done = (
            sem("ident_zero"), sem("ident_ok"), sem("turned"), sem("ctx_hi_done"), sem("ctx_lo_done"), sem("vec_done"))
        with nc.Block() as block:
            @block.sync
            def _(sp):
                for j in range(2):
                    sp.dma_start(chip.ctx[:, j * 4:j * 4 + 4, :], tiles_of(d['ctx_2048'])[:, j * 4:j * 4 + 4, :]).then_inc(ld_ctx, 16)
                sp.dma_start(chip.x[:, :, :], tiles_of(d['x'])).then_inc(ld_x, 16)
                sp.wait_ge(ld_x, 16)

            @block.scalar
            def _(act):
                act.dma_start(vraw[:, :], d['vecs']).then_inc(ld_vec, 16)
                act.dma_start(hraw[:, :, :], d['hvecs'].rearrange("(t r) k -> r t k", t=2)).then_inc(ld_vec, 16)
                act.dma_start(chip.rows[:, :, :].rearrange("p r d -> p (r d)"),
                              d['rows'].rearrange("(a n) -> a n", a=1).to_broadcast([P, len(ROWS) * D])).then_inc(ld_rows, 16)
                for n in range(4):
                    act.wait_ge(turned, n + 1)
                    act.activation(ctx_hi[:, n // 2, (n % 2) * HALF:(n % 2 + 1) * HALF], ps[:, n, :], ACT.Copy).then_inc(hi_done, 1)
                act.wait_ge(ld_rows, 16)

            @block.gpsimd
            def _(pool):
                pool.memset(chip.expo[:, :], -0.5)
                pool.memset(chip.ident[:, :], 0.0).then_inc(ident_zero, 1)
                pool.wait_ge(ident_zero, 1)
                pool.affine_select(out=chip.ident[:, :], in_=chip.ident[:, :], compare_op=ALU.not_equal, fill=1.0,
                                   base=0, pattern=[[-1, P]], channel_multiplier=1).then_inc(ident_ok, 1)

            @block.tensor
            def _(pe):
                pe.wait_ge(ident_ok, 1)
                for n in range(4):
                    pe.wait_ge(ld_ctx, 32)
                    c, half = n // 2, n % 2
                    for t in range(4):
                        mm = pe.transpose(ps[:, n, t * P:(t + 1) * P], chip.ctx[:, half * 4 + t, c * P:(c + 1) * P], chip.ident[:, :])
                    mm.then_inc(turned, 1)
                pe.wait_ge(ld_vec, 32)
                for c in range(NC):
                    pe.transpose(ps[:, 4, c * NV:(c + 1) * NV], vraw[:, c * P:(c + 1) * P], chip.ident[0:NV, 0:NV])
                R = NHV // 2
                for t in range(2):
                    mm = pe.transpose(ps[:, 5, t * R:(t + 1) * R], hraw[:, t, :], chip.ident[0:R, 0:R])
                mm.then_inc(turned, 1)

            @block.vector
            def _(dve):
                for n in range(4):
                    dve.wait_ge(hi_done, n + 1)
                    sl = slice((n % 2) * HALF, (n % 2 + 1) * HALF)
                    dve.tensor_tensor(ctx_lo[:, n // 2, sl], ps[:, n, :], ctx_hi[:, n // 2, sl].bitcast(F32), ALU.subtract).then_inc(lo_done, 1)
                dve.wait_ge(turned, 5)
                dve.tensor_copy(chip.vecs[:, :, :], ps[:, 4, 0:NC * NV].rearrange("p (c v) -> p c v", c=NC))
                dve.tensor_copy(chip.hvecs[:, :], ps[:, 5, 0:NHV])


def stage_layernorm(chip, tag, rows, scale_of, offset_of, eps, hi=None, lo=None, plain=None, add=None, prefetch=None):
    nc, ps = chip.nc, chip.psum
    with ExitStack() as st:
        sb = lambda n, s, t=F32: st.enter_context(nc.sbuf_tensor(f"{tag}_{n}", s, t))
        sem = lambda n: chip.semaphore(f"{tag}_{n}")
        xn = sb("normed", [P, NT, D])
        bn = sb("bn", [P, NT, 6])
        mv = sb("mean_var", [P, NT, 2])
        ve = sb("var_eps", [P, NT])
        rstd = sb("rstd", [P, NT])
        full = sb("full", [P, 4, BANK]) if hi is not None else None
        piece = lambda t, n: t[:, n % 2, (n // 2) * HALF:(n // 2 + 1) * HALF]
        stats, aggr, var_ok, rstd_ok, normed, turned, full_ok, hi_ok = (
            sem(n) for n in ("stats", "aggr", "var_ok", "rstd_ok", "normed", "turned", "full_ok", "hi_ok"))
        with nc.Block() as block:
            if prefetch:
                block.sync(prefetch)

            @block.gpsimd
            def _(pool):
                for h in range(2):
                    pool.wait_ge(var_ok, h + 1)
                    pool.tensor_tensor(rstd[:, 4 * h:4 * h + 4], ve[:, 4 * h:4 * h + 4], chip.expo[:, 4 * h:4 * h + 4], ALU.pow).then_inc(rstd_ok, 1)
                if add is not None:
                    pool.wait_ge(normed, NT)
                    pool.tensor_tensor(rows[:, 4:8, :], rows[:, 4:8, :], chip.rows[:, add:add + 1, :].to_broadcast([P, 4, D]), ALU.add)
                if hi is not None:
                    for n in (0, 2):
                        pool.wait_ge(hi_ok, n + 1)
                        pool.tensor_tensor(piece(lo, n), full[:, n, :], piece(hi, n).bitcast(F32), ALU.subtract)

            @block.vector
            def _(dve):
                def statistics(h):
                    for j in range(4 * h, 4 * h + 4):
                        dve.bn_stats(bn[:, j, :], rows[:, j, :]).then_inc(stats, 1)
                    for j in range(4 * h, 4 * h + 4):
                        dve.wait_ge(stats, j + 1)
                        dve.bn_aggr(mv[:, j, :], bn[:, j, :]).then_inc(aggr, 1)
                    dve.wait_ge(aggr, 4 * h + 4)
                    dve.tensor_scalar(ve[:, 4 * h:4 * h + 4], mv[:, 4 * h:4 * h + 4, 1], float(eps), None, ALU.add).then_inc(var_ok, 1)

                def normalise(h):
                    dve.wait_ge(rstd_ok, h + 1)
                    for j in range(4 * h, 4 * h + 4):
                        dve.tensor_scalar(xn[:, j, :], rows[:, j, :], mv[:, j, 0:1], rstd[:, j:j + 1], ALU.subtract, ALU.mult).then_inc(normed, 1)

                statistics(0)
                statistics(1)
                normalise(0)
                normalise(1)
                if add is not None:
                    dve.wait_ge(normed, 4)
                    dve.tensor_tensor(rows[:, 0:4, :], rows[:, 0:4, :], chip.rows[:, add:add + 1, :].to_broadcast([P, 4, D]), ALU.add)
                if hi is not None:
                    for n in range(4):
                        dve.wait_ge(full_ok, n + 1)
                        dve.tensor_copy(piece(hi, n), full[:, n, :]).then_inc(hi_ok, 1)
                        if n % 2 == 0:
                            continue
                        dve.wait_ge(hi_ok, n + 1)
                        dve.tensor_tensor(piece(lo, n), full[:, n, :], piece(hi, n).bitcast(F32), ALU.subtract)

            @block.tensor
            def _(pe):
                for n in range(4):
                    half, c = n // 2, n % 2
                    pe.wait_ge(normed, half * 4 + 4)
                    for t in range(4):
                        mm = pe.transpose(ps[:, n, t * P:(t + 1) * P], xn[:, half * 4 + t, c * P:(c + 1) * P], chip.ident[:, :])
                    mm.then_inc(turned, 1)

            @block.scalar
            def _(act):
                for n in range(4):
                    half, c = n // 2, n % 2
                    act.wait_ge(turned, n + 1)
                    if hi is not None:
                        act.activation(full[:, n, :], ps[:, n, :], ACT.Identity, scale=scale_of(c), bias=offset_of(c)).then_inc(full_ok, 1)
                    else:
                        act.activation(plain(c, half), ps[:, n, :].rearrange("p (b s) -> p b s", b=2), ACT.Identity,
                                       scale=scale_of(c), bias=offset_of(c))


def attention_weights(chip, stack, d, a):
    L = f"L0_xattn_"
    sb = lambda n, s: stack.enter_context(chip.nc.sbuf_tensor(f"a{a}_{n}", s, F32))
    w = {n: d[f"{L}w{n}{a}"].rearrange("(c p) n -> p c n", p=P) for n in 'qkv'}
    raw = {n: sb(f"w{n}_raw", [P, NC, HW]) for n in 'qkv'}
    raw['o'] = sb("wo_raw", [P, H0, D])
    ld = {n: chip.semaphore(f"a{a}_ld_w{n}") for n in 'qkvo'}

    def load(sp):
        for n in 'qkv':
            sp.dma_start(raw[n][:, :, :], w[n][:, :, 0:HW]).then_inc(ld[n], 16)
        sp.dma_start(raw['o'][:, :, :], d[f"{L}wo{a}"].rearrange("(h k) n -> k h n", k=K0)).then_inc(ld['o'], 16)

    return w, raw, ld, load


def stage_cross_attention(chip, a, weights, h_hi, h_lo, ctx_hi, ctx_lo):
    nc, ps = chip.nc, chip.psum
    C = float(K0) ** -0.5
    at = (a - 1) * 5 * H0
    W3, raw, ld, _load = weights
    wo_raw, ld_q, ld_k, ld_v, ld_o = raw['o'], ld['q'], ld['k'], ld['v'], ld['o']
    with ExitStack() as st:
        sb = lambda n, s, t=F32: st.enter_context(nc.sbuf_tensor(f"a{a}_{n}", s, t))
        sem = lambda n: chip.semaphore(f"a{a}_{n}")
        whi = {n: sb(f"w{n}_hi", [P, NC, HW], F32R) for n in 'qkvo'}
        wlo = {n: sb(f"w{n}_lo", [P, NC, HW], F32R) for n in 'qkvo'}
        qk_hi = {n: sb(f"{n}_hi", [P, PAIR, TOK], F32R) for n in 'qc'}
        qk_lo = {n: sb(f"{n}_lo", [P, PAIR, TOK], F32R) for n in 'qc'}
        E_LATE, M_LATE, I_LATE = 2, 1, 3
        KW = S + 2
        k_hi = sb("k_hi", [P, PAIR, B, KW], F32R)
        k_lo = sb("k_lo", [P, PAIR, B, KW], F32R)
        v_hi = sb("v_hi", [P, NT, HW], F32R)
        v_lo = sb("v_lo", [P, NT, HW], F32R)
        prob = sb("prob", [P, 4, 2, KW])
        negm = sb("neg_max", [P, 4, 2])
        tot = sb("total", [P, 4, 2])
        rtot = sb("inv_total", [P, 4, 2])
        pt_hi = sb("probT_hi", [P, 4, BANK], F32R)
        pt_lo = sb("probT_lo", [P, 4, BANK], F32R)
        one = sb("ones", [P, 2])
        pb = sb("prob_bias", [P, NT, NPAIR, PAIR])
        bcol = sb("bias_cols", [P, 3, NPAIR, PAIR])
        qk_cols = sb("qk_cols", [P, 2, PAIR])
        v_cols = sb("v_cols", [P, PAIR])
        wo_pair = sb("wo_pair", [P, PAIR, D])
        kb_hi = sb("bias_k_hi", [P, NPAIR, PAIR], F32R)
        kb_lo = sb("bias_k_lo", [P, NPAIR, PAIR], F32R)
        dvm = sb("bias_v_diag", [P, H0, H0])
        bvo = sb("bias_out", [H0, D])
        pb_T = sb("prob_bias_T", [H0, TOK])

        (q_split, k_split, v_split, o_split, rounded, q_rounded, cols_ok, cols_cur, ld_op, kcols,
         acc_full, acc_hi, acc_free, s_done, s_max, s_exp, s_sum, s_norm, t_done, t_hi, t_free, bias_full, bias_read, dv_ok) = (
            sem(n) for n in ("wq_split", "wk_split", "wv_split", "wo_split",
                             "w_rounded", "wq_rounded", "cols_ok", "cols_cur", "ld_wo_pair", "bias_k_cols",
                             "acc_full", "acc_hi", "acc_free", "scores_done", "max_done", "exp_done", "inv_done",
                             "norm_done", "turned", "turned_hi", "turned_free", "bias_full", "bias_read", "bias_v_ok"))
        split = {'q': q_split, 'k': k_split, 'v': v_split}
        hv = lambda k: chip.hvecs[:, at + k * H0:at + (k + 1) * H0]

        PRE = ['Q0', 'Q1', 'K0', 'K1', 'Q2', 'Q3', 'K2', 'K3']
        STEP = ("S0 O0 O1 S1 O2 O3 V0 S2 T0 V1 S3 V2 T1 S4 V3 Q0 T2 S5 Q1 K0 T3 S6 K1 A0 Q2 T4 "
                "A1 S7 T5 Q3 T6 A2 K2 T7 K3 A3").split()
        FIRST = [s for s in STEP if s[0] != 'O']
        LAST = [s for s in STEP if s[0] not in 'QK']
        TAIL = ['O0', 'O1', 'O2', 'O3']
        HIS = 16
        USES = HIS + 4
        base_of = lambda i: len(PRE) if isinstance(i, int) and i == 0 else i * USES + len(PRE) - 4
        END = base_of(NPAIR - 1) + 12 + 4
        use_of = lambda order, s: [x for x in order if x[0] in 'VAQKO'].index(s)
        acc = lambda n: ps[:, n % 2, :]
        s_bank = lambda u: ps[:, 2 + 2 * (u % 2):4 + 2 * (u % 2), 0:KW]
        t_bank = lambda u: ps[:, 6 + u % 2, :]
        U = 2 * B

        def three(pe, out, l_hi, l_lo, r_hi, r_lo, first, last):
            pe.matmul(out, l_hi, r_hi, start=first, stop=False)
            pe.matmul(out, l_hi, r_lo, start=False, stop=False)
            return pe.matmul(out, l_lo, r_hi, start=False, stop=last)

        def steps(eng, body):
            body(0, FIRST)
            with eng.Fori(1, NPAIR - 1) as i:
                body(i, STEP)
            body(NPAIR - 1, LAST)
            body(NPAIR, TAIL)

        def project_out(s, h_dst, half):
            if s[0] == 'Q':
                cols = slice(half * HALF, (half + 1) * HALF)
                return qk_hi['q'][:, h_dst, cols], qk_lo['q'][:, h_dst, cols]
            return k_hi[:, h_dst, 2 * half:2 * half + 2, 0:S], k_lo[:, h_dst, 2 * half:2 * half + 2, 0:S]

        def like(s, view):
            return view.rearrange("p (b s) -> p b s", b=2) if s[0] == 'K' else view

        def later(order, what, steps):
            out, held = [], []
            for s in order:
                out.append(s)
                held = [(t, n - 1) for t, n in held]
                out += [t for t, n in held if n == 0]
                held = [(t, n) for t, n in held if n > 0]
                if s[0] == 'S':
                    held.append((what + s[1], steps))
            return out + [t for t, n in held]

        def act_order(order):
            out = [s for s in later(order, 'E', E_LATE) if s[0] in 'EVATQK' or s == 'S2']
            return [('R0' if s == 'S2' else s) for s in out]

        def dve_order(order):
            out = []
            for s in later(later(order, 'M', M_LATE), 'I', I_LATE):
                if s == 'S2':
                    out.append('R0')
                elif s[0] != 'S':
                    out.append(s)
            return out

        with nc.Block() as block:
            @block.sync
            def _(sp):
                sp.wait_ge(ld_o, 16)
                sp.dma_start(wo_pair[:, :, :], wo_raw[:, 0:PAIR, :]).then_inc(ld_op, 16)
                with sp.Fori(1, NPAIR) as i:
                    for n in 'qkv':
                        sp.wait_ge(split[n], i)
                        sp.dma_start(raw[n][:, :, :], W3[n][:, :, bass.ds(i * HW, HW)]).then_inc(ld[n], 16)
                    sp.wait_ge(o_split, i)
                    sp.dma_start(wo_pair[:, :, :], wo_raw[:, bass.ds(i * PAIR, PAIR), :]).then_inc(ld_op, 16)

            @block.gpsimd
            def _(pool):
                rounds = [0]
                ones = one[:, 0:1].to_broadcast([P, NC, HW])

                def cut(src, n, count, done):
                    pool.tensor_tensor(whi[n][:, :, :], src, ones, ALU.mult).then_inc(rounded, 1)
                    pool.wait_ge(rounded, count + 1)
                    pool.tensor_tensor(wlo[n][:, :, :], src, whi[n][:, :, :].bitcast(F32), ALU.subtract).then_inc(done, 1)

                pool.memset(one[:, :], 1.0).then_inc(rounded, 1)
                pool.wait_ge(rounded, 1)
                pool.wait_ge(ld_k, 16)
                cut(raw['k'][:, :, :], 'k', 1, k_split)
                pool.wait_ge(ld_v, 16)
                cut(raw['v'][:, :, :], 'v', 2, v_split)

                def body(i, order):
                    last = order is LAST

                    def norm(u):
                        h, b = u // B, u % B
                        pool.wait_ge(s_sum, i * U + u + 1)
                        pool.tensor_tensor(prob[:, u % 4, :, 0:S], prob[:, u % 4, :, 0:S],
                                           rtot[:, u % 4, :].unsqueeze(2).to_broadcast([P, 2, S]), ALU.mult)
                        pool.tensor_tensor(pb[:, 2 * b:2 * b + 2, i, h:h + 1], prob[:, u % 4, :, S:S + 1], rtot[:, u % 4, :].unsqueeze(2), ALU.mult).then_inc(s_norm, 1)

                    if order is TAIL:
                        return
                    norm(0)
                    norm(1)
                    if order is not FIRST:
                        pool.wait_ge(acc_full, base_of(i) + 4)
                    pool.wait_ge(ld_op, i * 16 + 16)
                    cut(wo_pair[:, :, :], 'o', i * 3 + 3, o_split)
                    norm(2)
                    if not last:
                        pool.wait_ge(ld_k, i * 16 + 32)
                        cut(raw['k'][:, :, :], 'k', i * 3 + 4, k_split)
                    for u in range(3, U):
                        norm(u)
                        if u == U - 2 and not last:
                            pool.wait_ge(ld_v, i * 16 + 32)
                            cut(raw['v'][:, :, :], 'v', i * 3 + 5, v_split)

                steps(pool, body)

            @block.tensor
            def _(pe):
                pe.sem_inc(t_done, 4)

                def project(s, i, n, total):
                    w, h, half = s[0].lower(), int(s[1]) // 2, int(s[1]) % 2
                    for c in range(NC):
                        cols = slice(half * HALF, (half + 1) * HALF)
                        rh, rl = (h_hi, h_lo) if w == 'q' else (ctx_hi, ctx_lo)
                        mm = three(pe, acc(n), whi[w][:, c, h * K0:(h + 1) * K0], wlo[w][:, c, h * K0:(h + 1) * K0],
                                   rh[:, c, cols], rl[:, c, cols], c == 0, c == NC - 1)
                    mm.then_inc(acc_full, 1)

                pe.wait_ge(q_split, 1)
                for n, s in enumerate(PRE):
                    if s == 'K0':
                        pe.wait_ge(k_split, 1)
                    if n >= 2:
                        pe.wait_ge(acc_free, n - 1)
                    project(s, 0, n, n)
                    if n == 1:
                        pe.wait_ge(ld_o, 16)
                        pe.wait_ge(dv_ok, 2)
                    if n:
                        for h in range(3 * (n - 1), min(3 * n, H0)):
                            mm = pe.matmul(ps[0:H0, 7, 0:D], dvm[:, h, :], wo_raw[:, h, :], start=h == 0, stop=h == H0 - 1)
                            if h == H0 - 1:
                                mm.then_inc(bias_full, 1)

                def bias_token():
                    pe.wait_ge(s_exp, 2 * U * NPAIR + 4)
                    pe.wait_ge(s_norm, U * NPAIR)
                    for j in range(NT):
                        mm = pe.transpose(ps[0:H0, 4 + j // 4, (j % 4) * P:(j % 4 + 1) * P], pb[:, j, :, :].rearrange("p i h -> p (i h)"), chip.ident[:, :])
                    mm.then_inc(bias_full, 1)

                def body(i, order):
                    base = base_of(i) if order is not TAIL else END - 4
                    if order is TAIL:
                        bias_token()
                    for s in order:
                        k, m = s[0], int(s[1])
                        if k in 'VAQKO':
                            n = use_of(order, s)
                            pe.wait_ge(acc_free, base + n - 1)
                        if k in 'QK':
                            if s in ('Q0', 'K0'):
                                pe.wait_ge(split[k.lower()], i + 2)
                            project(s, i, n, base + n)
                        if k == 'V':
                            if m == 0:
                                pe.wait_ge(v_split, i + 1)
                            for j in range(2):
                                t = 2 * m + j
                                for c in range(NC):
                                    mm = three(pe, acc(n)[:, j * HW:(j + 1) * HW], ctx_hi[:, c, t * P:(t + 1) * P], ctx_lo[:, c, t * P:(t + 1) * P],
                                               whi['v'][:, c, :], wlo['v'][:, c, :], c == 0, c == NC - 1)
                            mm.then_inc(acc_full, 1)
                        if k == 'S':
                            h, b = m // B, m % B
                            if m == 0:
                                if order is FIRST:
                                    pe.wait_ge(acc_free, PRE.index('K1') + 1)
                                else:
                                    pe.wait_ge(acc_free, base - USES + use_of(STEP, 'K1') + 1)
                                pe.wait_ge(kcols, i + 1)
                            pe.wait_ge(s_exp, 2 * (i * U + m) + 2)
                            for q in range(2):
                                cols = slice(b * S + q * P, b * S + (q + 1) * P)
                                mm = three(pe, s_bank(m)[:, q, :], qk_hi['q'][:, h, cols], qk_lo['q'][:, h, cols],
                                           k_hi[:, h, b, :], k_lo[:, h, b, :], True, True)
                            mm.then_inc(s_done, 1)
                        if k == 'T':
                            pe.wait_ge(s_norm, i * U + m + 1)
                            pe.wait_ge(t_free, i * U + m + 1)
                            for t in range(2):
                                for q in range(2):
                                    mm = pe.transpose(t_bank(m)[:, t * S + q * P:t * S + (q + 1) * P], prob[:, m % 4, q, t * P:(t + 1) * P], chip.ident[:, :])
                            mm.then_inc(t_done, 1)
                        if k == 'A':
                            pe.wait_ge(t_free, i * U + 2 * m + 4)
                            if m == 0:
                                pe.wait_ge(acc_free, base + use_of(order, 'V3') + 1)
                            for u in (2 * m, 2 * m + 1):
                                h, b = u // B, u % B
                                for t in range(2):
                                    mm = three(pe, acc(n)[:, (u % 2) * S:(u % 2 + 1) * S], v_hi[:, 2 * b + t, h * K0:(h + 1) * K0], v_lo[:, 2 * b + t, h * K0:(h + 1) * K0],
                                               pt_hi[:, u % 4, t * S:(t + 1) * S], pt_lo[:, u % 4, t * S:(t + 1) * S], t == 0, t == 1)
                            mm.then_inc(acc_full, 1)
                        if k == 'O':
                            if m == 0:
                                pe.wait_ge(o_split, i)
                                pe.wait_ge(acc_free, base)
                            for j in range(2):
                                t = 2 * m + j
                                for h in range(PAIR):
                                    mm = three(pe, acc(n)[:, j * D:(j + 1) * D], qk_hi['c'][:, h, t * P:(t + 1) * P], qk_lo['c'][:, h, t * P:(t + 1) * P],
                                               whi['o'][:, h, :], wlo['o'][:, h, :], h == 0, h == PAIR - 1 and order is not TAIL)
                                if order is TAIL:
                                    pe.wait_ge(bias_read, 1)
                                    mm = pe.matmul(acc(n)[:, j * D:(j + 1) * D], pb_T[:, t * P:(t + 1) * P], bvo[:, :], start=False, stop=True)
                            mm.then_inc(acc_full, 1)

                steps(pe, body)

            @block.scalar
            def _(act):
                act.sem_inc(s_exp, 4)
                act.wait_ge(ld_q, 16)
                act.activation(whi['q'][:, :, :], raw['q'][:, :, :], ACT.Copy, scale=C).then_inc(q_rounded, 1)
                act.wait_ge(cols_cur, 1)

                def qk(s, n, i, count):
                    h, half = int(s[1]) // 2, int(s[1]) % 2
                    act.wait_ge(acc_full, count + 1)
                    act.activation(project_out(s, h, half)[0], like(s, acc(n)), ACT.Identity,
                                   bias=qk_cols[:, 0 if s[0] == 'Q' else 1, h:h + 1]).then_inc(acc_hi, 1)

                for n, s in enumerate(PRE):
                    qk(s, n, 0, n)

                def body(i, order):
                    last = order is LAST
                    base = base_of(i) if order is not TAIL else END - 4
                    for s in act_order(order):
                        k, m = s[0], int(s[1])
                        if k == 'E':
                            act.wait_ge(s_max, i * U + m + 1)
                            act.wait_ge(t_done, i * U + m + 1)
                            for q in range(2):
                                act.activation(prob[:, m % 4, q, 0:S + 1], s_bank(m)[:, q, 0:S + 1], ACT.Exp,
                                               bias=negm[:, m % 4, q:q + 1], accum_out=tot[:, m % 4, q:q + 1]).then_inc(s_exp, 1)
                        elif k == 'T':
                            act.wait_ge(t_done, i * U + m + 5)
                            act.activation(pt_hi[:, m % 4, :], t_bank(m), ACT.Copy).then_inc(t_hi, 1)
                        elif k == 'R':
                            if not last:
                                act.wait_ge(ld_q, i * 16 + 32)
                                act.activation(whi['q'][:, :, :], raw['q'][:, :, :], ACT.Copy, scale=C).then_inc(q_rounded, 1)
                        elif k in 'QK':
                            if s == 'Q0':
                                act.wait_ge(cols_cur, 2 * i + 3)
                            qk(s, use_of(order, s), i + 1, base + use_of(order, s))
                        elif k in 'VA':
                            n = use_of(order, s)
                            act.wait_ge(acc_full, base + n + 1)
                            if s == 'A0':
                                act.wait_ge(cols_cur, 2 * i + 2)
                            if k == 'V':
                                act.activation(v_hi[:, 2 * m:2 * m + 2, :], acc(n).rearrange("p (j n) -> p j n", j=2), ACT.Copy).then_inc(acc_hi, 1)
                            else:
                                act.activation(qk_hi['c'][:, m // 2, (m % 2) * HALF:(m % 2 + 1) * HALF], acc(n), ACT.Identity,
                                               bias=v_cols[:, m // 2:m // 2 + 1]).then_inc(acc_hi, 1)

                steps(act, body)

            @block.vector
            def _(dve):
                dve.sem_inc(t_free, 1)
                dve.wait_ge(q_rounded, 1)
                dve.scalar_tensor_tensor(wlo['q'][:, :, :], raw['q'][:, :, :], C, whi['q'][:, :, :].bitcast(F32), ALU.mult, ALU.subtract).then_inc(q_split, 1)
                dve.tensor_scalar(bcol[:, 0, :, :], hv(0).rearrange("p (i h) -> p i h", h=PAIR), C, None, ALU.mult)
                dve.tensor_copy(bcol[:, 1, :, :], hv(1).rearrange("p (i h) -> p i h", h=PAIR))
                dve.tensor_copy(bcol[:, 2, :, :], hv(4).rearrange("p (i h) -> p i h", h=PAIR))
                dve.memset(k_hi[:, :, :, S:KW].bitcast(F32), 0.0)
                dve.memset(k_lo[:, :, :, S:KW].bitcast(F32), 0.0)
                dve.memset(dvm[:, :, :], 0.0).then_inc(dv_ok, 1)
                dve.wait_ge(dv_ok, 1)
                dve.tensor_tensor(dvm[:, :, :].rearrange("p a b -> p (a b)")[:, 0:H0 * H0:H0 + 1], hv(3), hv(4), ALU.subtract).then_inc(dv_ok, 1)
                dve.tensor_copy(kb_hi[:, :, :], hv(2).rearrange("p (i h) -> p i h", h=PAIR)).then_inc(cols_ok, 1)
                dve.wait_ge(cols_ok, 1)
                dve.tensor_tensor(kb_lo[:, :, :], hv(2).rearrange("p (i h) -> p i h", h=PAIR), kb_hi[:, :, :].bitcast(F32), ALU.subtract).then_inc(cols_ok, 1)
                dve.wait_ge(cols_ok, 2)
                dve.tensor_copy(qk_cols[:, :, :], bcol[:, 0:2, 0, :]).then_inc(cols_cur, 1)
                dve.wait_ge(cols_cur, 1)

                def qk(s, n, i, count):
                    h, half = int(s[1]) // 2, int(s[1]) % 2
                    hi, lo = project_out(s, h, half)
                    dve.wait_ge(acc_hi, count + 1)
                    dve.scalar_tensor_tensor(lo, like(s, acc(n)), qk_cols[:, 0 if s[0] == 'Q' else 1, h:h + 1],
                                             hi.bitcast(F32), ALU.add, ALU.subtract).then_inc(acc_free, 1)

                def key_cols(i):
                    for dst, src in ((k_hi, kb_hi), (k_lo, kb_lo)):
                        ins = dve.tensor_copy(dst[:, :, :, S:S + 1], src[:, i, :].bitcast(F32).unsqueeze(2).unsqueeze(3).to_broadcast([P, PAIR, B, 1]))
                    ins.then_inc(kcols, 1)

                for n, s in enumerate(PRE):
                    qk(s, n, 0, n)
                key_cols(0)
                dve.wait_ge(bias_full, 1)
                dve.tensor_copy(bvo[:, :], ps[0:H0, 7, 0:D]).then_inc(t_free, 1)

                def body(i, order):
                    last = order is LAST
                    base = base_of(i) if order is not TAIL else END - 4
                    hi_base = i * HIS + len(PRE)
                    if order is TAIL:
                        dve.wait_ge(bias_full, 2)
                        dve.tensor_copy(pb_T[:, :], ps[0:H0, 4:6, :].rearrange("p b n -> p (b n)")).then_inc(bias_read, 1)
                    his = [s for s in order if s[0] in 'VAQK']
                    for s in dve_order(order):
                        k, m = s[0], int(s[1])
                        if k == 'M':
                            dve.wait_ge(s_done, i * U + m + 1)
                            dve.tensor_reduce(negm[:, m % 4, :], s_bank(m)[:, :, 0:S + 1], AX.X, ALU.max, negate=True).then_inc(s_max, 1)
                        elif k == 'I':
                            dve.wait_ge(s_exp, 2 * (i * U + m) + 6)
                            dve.reciprocal(rtot[:, m % 4, :], tot[:, m % 4, :]).then_inc(s_sum, 1)
                        elif k == 'T':
                            dve.wait_ge(t_hi, i * U + m + 1)
                            dve.tensor_tensor(pt_lo[:, m % 4, :], t_bank(m), pt_hi[:, m % 4, :].bitcast(F32), ALU.subtract).then_inc(t_free, 1)
                        elif k == 'R':
                            dve.wait_ge(acc_free, base)
                            dve.tensor_copy(v_cols[:, :], bcol[:, 2, i, :]).then_inc(cols_cur, 1)
                            if not last:
                                dve.tensor_copy(qk_cols[:, :, :], bcol[:, 0:2, i + 1, :]).then_inc(cols_cur, 1)
                                dve.wait_ge(q_rounded, i + 2)
                                dve.scalar_tensor_tensor(wlo['q'][:, :, :], raw['q'][:, :, :], C, whi['q'][:, :, :].bitcast(F32),
                                                         ALU.mult, ALU.subtract).then_inc(q_split, 1)
                        elif k in 'QK':
                            if s == 'Q0':
                                dve.wait_ge(cols_cur, 2 * i + 3)
                            qk(s, use_of(order, s), i + 1, hi_base + his.index(s))
                            if s == 'K3':
                                key_cols(i + 1)
                        elif k == 'V':
                            dve.wait_ge(acc_hi, hi_base + his.index(s) + 1)
                            dve.tensor_tensor(v_lo[:, 2 * m:2 * m + 2, :], acc(use_of(order, s)).rearrange("p (j n) -> p j n", j=2),
                                              v_hi[:, 2 * m:2 * m + 2, :].bitcast(F32), ALU.subtract).then_inc(acc_free, 1)
                        elif k == 'A':
                            dve.wait_ge(acc_hi, hi_base + his.index(s) + 1)
                            cols = slice((m % 2) * HALF, (m % 2 + 1) * HALF)
                            dve.scalar_tensor_tensor(qk_lo['c'][:, m // 2, cols], acc(use_of(order, s)), v_cols[:, m // 2:m // 2 + 1],
                                                     qk_hi['c'][:, m // 2, cols].bitcast(F32), ALU.add, ALU.subtract).then_inc(acc_free, 1)
                        elif k == 'O':
                            n = use_of(order, s)
                            dve.wait_ge(acc_full, base + n + 1)
                            dve.tensor_tensor(chip.x[:, 2 * m:2 * m + 2, :], chip.x[:, 2 * m:2 * m + 2, :],
                                              acc(n).rearrange("p (j n) -> p j n", j=2), ALU.add).then_inc(acc_free, 1)

                steps(dve, body)


def stage_mlp(chip, w1_raw, w2_raw, ld_w, h_hi, h_lo):
    nc, ps = chip.nc, chip.psum
    bias1 = lambda f: chip.hvecs[:, len(HVECS) * H0 + f:len(HVECS) * H0 + f + 1]
    with ExitStack() as st:
        sb = lambda n, s, t=F32R: st.enter_context(nc.sbuf_tensor(f"mlp_{n}", s, t))
        sem = lambda n: chip.semaphore(f"mlp_{n}")
        w1_hi, w1_lo = sb("w1_hi", [P, NC, FF]), sb("w1_lo", [P, NC, FF])
        w2_hi, w2_lo = sb("w2_hi", [P, NF, D]), sb("w2_lo", [P, NF, D])
        u = sb("u", [P, 4, BANK], F32)
        u_hi, u_lo = sb("u_hi", [P, NF, TOK]), sb("u_lo", [P, NF, TOK])
        w_hi_ok, w1_ok, w2_hi_ok, w2_ok, full, gelu, u_hi_ok, u_ok, out_full, out_free = (
            sem(n) for n in ("w1_hi_ok", "w1_ok", "w2_hi_ok", "w2_ok", "full", "gelu", "u_hi_ok", "u_ok", "out_full", "out_free"))
        part = lambda f: slice(f * P, (f + 1) * P)
        half = lambda n: slice((n % 2) * HALF, (n % 2 + 1) * HALF)
        NU = 2 * NF
        with nc.Block() as block:
            @block.scalar
            def _(act):
                act.wait_ge(ld_w, 32)
                for q in range(4):
                    act.activation(w1_hi[:, :, q * 256:(q + 1) * 256], w1_raw[:, :, q * 256:(q + 1) * 256], ACT.Copy).then_inc(w_hi_ok, 1)
                for n in range(NU):
                    act.wait_ge(full, n + 1)
                    if n >= 4:
                        act.wait_ge(u_ok, n - 3)
                    act.activation(u[:, n % 4, :], ps[:, n % 4, :], ACT.Gelu, bias=bias1(n // 2)).then_inc(gelu, 1)

            @block.gpsimd
            def _(pool):
                pool.wait_ge(ld_w, 32)
                for q in range(4):
                    pool.wait_ge(w2_hi_ok, q + 1)
                    pool.tensor_tensor(w2_lo[:, 2 * q:2 * q + 2, :], w2_raw[:, 2 * q:2 * q + 2, :],
                                       w2_hi[:, 2 * q:2 * q + 2, :].bitcast(F32), ALU.subtract).then_inc(w2_ok, 1)

            @block.vector
            def _(dve):
                dve.wait_ge(ld_w, 32)
                for q in range(4):
                    dve.wait_ge(w_hi_ok, q + 1)
                    cols = slice(q * 256, (q + 1) * 256)
                    dve.tensor_tensor(w1_lo[:, :, cols], w1_raw[:, :, cols], w1_hi[:, :, cols].bitcast(F32), ALU.subtract).then_inc(w1_ok, 1)
                for q in range(4):
                    dve.tensor_copy(w2_hi[:, 2 * q:2 * q + 2, :], w2_raw[:, 2 * q:2 * q + 2, :]).then_inc(w2_hi_ok, 1)
                for n in range(NU):
                    dve.wait_ge(gelu, n + 1)
                    dve.tensor_copy(u_hi[:, n // 2, half(n)], u[:, n % 4, :]).then_inc(u_hi_ok, 1)
                    dve.wait_ge(u_hi_ok, n + 1)
                    dve.tensor_tensor(u_lo[:, n // 2, half(n)], u[:, n % 4, :], u_hi[:, n // 2, half(n)].bitcast(F32), ALU.subtract).then_inc(u_ok, 1)
                for m in range(4):
                    dve.wait_ge(out_full, m + 1)
                    dve.tensor_tensor(chip.x[:, 2 * m:2 * m + 2, :], chip.x[:, 2 * m:2 * m + 2, :],
                                      ps[:, 4 + m, :].rearrange("p (j n) -> p j n", j=2), ALU.add).then_inc(out_free, 1)

            @block.tensor
            def _(pe):
                def three(out, l_hi, l_lo, r_hi, r_lo, first, last):
                    pe.matmul(out, l_hi, r_hi, start=first, stop=False)
                    pe.matmul(out, l_hi, r_lo, start=False, stop=False)
                    return pe.matmul(out, l_lo, r_hi, start=False, stop=last)

                for n in range(NU):
                    f = n // 2
                    pe.wait_ge(w1_ok, f // 2 + 1)
                    if n >= 4:
                        pe.wait_ge(gelu, n - 3)
                    for c in range(NC):
                        mm = three(ps[:, n % 4, :], w1_hi[:, c, part(f)], w1_lo[:, c, part(f)], h_hi[:, c, half(n)], h_lo[:, c, half(n)], c == 0, c == NC - 1)
                    mm.then_inc(full, 1)
                pe.wait_ge(u_ok, NU)
                pe.wait_ge(w2_ok, 4)
                for t in range(NT):
                    for f in range(NF):
                        mm = three(ps[:, 4 + t // 2, (t % 2) * D:(t % 2 + 1) * D], u_hi[:, f, part(t)], u_lo[:, f, part(t)], w2_hi[:, f, :], w2_lo[:, f, :], f == 0, f == NF - 1)
                    if t % 2:
                        mm.then_inc(out_full, 1)


E1 = 256
H1, S1 = 32, 8
KM = 32
NMIX = 5
KD = 64
L1_WEIGHTS = ['Wr', 'Wk', 'Wv', 'Wg', 'Wo', 'ffn_Wk', 'ffn_Wr', 'ffn_Wv']
R1 = S + 1


def layer1_memory(chip, st, d):
    nc = chip.nc
    """Weights and start values of layer 1, and the function that loads them."""
    sb = lambda n, s: st.enter_context(nc.sbuf_tensor(f"r_{n}", s, F32))
    w = {n: sb(n, [P, NC, E1]) for n in L1_WEIGHTS}
    m = {'w': w, 'maa_w1': sb("maa_w1", [P, NC, NMIX * KM]), 'maa_w2': sb("maa_w2", [P, E1]), 'maa_w2e': sb("maa_w2e", [KM, E1]),
         'decay_w1': sb("decay_w1", [P, NC, KD]), 'decay_w2': sb("decay_w2", [KD, E1]),
         's0': sb("s0", [P, NC, B, S1]), 'ld': chip.semaphore("ld_layer1")}
    ld = m['ld']
    count = [0]

    def load(sp):
        def go(dst, src):
            sp.dma_start(dst, src).then_inc(ld, 16)
            count[0] += 16

        for b in range(B):
            go(m['s0'][:, :, b, :], d['ctx_2048'][b, 2:2 + S1, :].rearrange("r (q e) -> (r q) e", e=S1).rearrange("(c p) e -> p c e", p=P))
        go(m['maa_w1'][:, :, :], d['L1_xattn_maa_w1'].rearrange("(c p) n -> p c n", p=P))
        go(m['maa_w2'][:, :], d['L1_xattn_maa_w2'][0:4].rearrange("i k n -> (i k) n"))
        go(m['maa_w2e'][:, :], d['L1_xattn_maa_w2'][4])
        go(m['decay_w1'][:, :, :], d['L1_xattn_decay_w1'].rearrange("(c p) n -> p c n", p=P))
        go(m['decay_w2'][:, :], d['L1_xattn_decay_w2'])
        for n in L1_WEIGHTS:
            go(w[n][:, :, :], d[f'L1_xattn_{n}_T'].rearrange("(c p) n -> p c n", p=P))
        sp.wait_ge(ld, count[0])

    return m, load


def stage_rwkv_mix(chip, m, xe, kT, vT, rT, wT, gT):
    nc, ps = chip.nc, chip.psum
    w = m['w']
    with ExitStack() as st:
        sb = lambda n, s, t=F32: st.enter_context(nc.sbuf_tensor(f"mix_{n}", s, t))
        sem = lambda n: chip.semaphore(f"mix_{n}")
        sx = sb("shift", [P, NC, B, S])
        first = sb("first", [P, NC, B, S])
        lowA, lowB = sb("lowA", [P, TOK]), sb("lowB", [KM, TOK])
        scaled = sb("scaled", [P, 2, NC, TOK])
        mixed = sb("mixed", [P, 2, NC, TOK])
        dec = sb("dec", [KD, TOK])
        e1 = sb("e1", [P, 2, BANK])
        th = sb("th", [P, 2, BANK])
        cur = lambda c: xe[:, c, :, 1:R1]
        flat = lambda ap: ap.rearrange("p b s -> p (b s)")
        batches = lambda ap: ap.rearrange("p (b s) -> p b s", s=S)
        MIX = {'w': 1, 'k': 0, 'v': 2, 'r': 3, 'g': 4}
        ORDER = 'wkvrg'
        uses = [('low', n, 'act') for n in range(4)]
        uses += [('mw', n, 'dve') for n in range(4)] + [('mk', n, 'dve') for n in range(4)] + [('d1', n, 'act') for n in range(2)]
        uses += [('mv', n, 'dve') for n in range(4)] + [('pk', n, 'act') for n in range(4)] + [('d2', n, 'act') for n in range(4)]
        uses += [('mr', n, 'dve') for n in range(4)] + [('pv', n, 'act') for n in range(4)] + [('mg', n, 'dve') for n in range(4)]
        uses += [('pr', n, 'act') for n in range(4)] + [('pg', n, 'dve') for n in range(4)]
        num = {u[:2]: i for i, u in enumerate(uses)}
        nth = lambda i: sum(u[2] == uses[i][2] for u in uses[:i + 1])
        full, act_free, dve_free, shifted, first_ok, low_ok, scaled_ok, mix_dve, mix_pool, dec_ok, e_ok, th_ok = (
            sem(n) for n in ("full", "act_read", "dve_read", "shifted", "first_ok", "low_ok", "scaled_ok", "mixed_dve",
                             "mixed_pool", "dec_ok", "e_ok", "th_ok"))
        ch = lambda n: (n // 2, n % 2)
        half = lambda n: slice((n % 2) * HALF, (n % 2 + 1) * HALF)
        bh = lambda n: slice(2 * (n % 2), 2 * (n % 2) + 2)

        with nc.Block() as block:
            @block.tensor
            def _(pe):
                def begin(key):
                    n = num[key]
                    if n >= 8:
                        pe.wait_ge(act_free if uses[n - 8][2] == 'act' else dve_free, nth(n - 8))
                    return ps[:, n % 8, :]

                def product(key, weight, cols, src, rows=P):
                    out = begin(key)[0:rows, :]
                    for c in range(NC):
                        mm = pe.matmul(out, weight[:, c, cols], src(c), start=c == 0, stop=c == NC - 1)
                    mm.then_inc(full, 1)

                for key in [u[:2] for u in uses]:
                    what, n = key
                    if what == 'low':
                        pe.wait_ge(first_ok, 2)
                        src = lambda c: flat(first[:, c, bh(n), :])
                        product(key, m['maa_w1'], slice(0, P) if n < 2 else slice(P, NMIX * KM), src, P if n < 2 else KM)
                    elif what[0] == 'm':
                        i, (c, _h) = MIX[what[1]], ch(n)
                        pe.wait_ge(low_ok, 4)
                        out = begin(key)
                        if i < 4:
                            lhs, rhs = m['maa_w2'][KM * i:KM * i + KM, c * P:(c + 1) * P], lowA[KM * i:KM * i + KM, half(n)]
                        else:
                            lhs, rhs = m['maa_w2e'][:, c * P:(c + 1) * P], lowB[:, half(n)]
                        tile = (KM * i, 0) if i < 4 else (0, 0)
                        pe.matmul(out, lhs, rhs, start=True, stop=True, tile_position=tile).then_inc(full, 1)
                    elif what == 'd1':
                        if n == 0:
                            pe.wait_ge(mix_dve, 1)
                            pe.wait_ge(mix_pool, 1)
                        product(key, m['decay_w1'], slice(0, KD), lambda c: mixed[:, 0, c, half(n)], KD)
                    elif what == 'd2':
                        pe.wait_ge(dec_ok, 2)
                        out = begin(key)
                        pe.matmul(out, m['decay_w2'][:, (n // 2) * P:(n // 2 + 1) * P], dec[:, half(n)], start=True, stop=True).then_inc(full, 1)
                    else:
                        i = ORDER.index(what[1])
                        if n == 0:
                            pe.wait_ge(mix_dve, i + 1)
                            pe.wait_ge(mix_pool, i + 1)
                        product(key, w['W' + what[1]], slice((n // 2) * P, (n // 2 + 1) * P), lambda c: mixed[:, i % 2, c, half(n)])

            @block.vector
            def _(dve):
                dve.tensor_copy(xe[:, :, :, 0:1], chip.vecs[:, :, PREV + B:PREV + 2 * B].unsqueeze(3)).then_inc(shifted, 1)
                dve.wait_ge(shifted, 1)
                for c in range(NC):
                    dve.tensor_tensor(sx[:, c, :, :], xe[:, c, :, 0:S], cur(c), ALU.subtract).then_inc(shifted, 1)
                for c in range(NC):
                    dve.wait_ge(shifted, c + 2)
                    dve.scalar_tensor_tensor(first[:, c, :, :], sx[:, c, :, :], chip.vec('L1_xattn_maa_x', c), cur(c), ALU.mult, ALU.add).then_inc(first_ok, 1)
                for i, x in enumerate(ORDER):
                    if i >= 2:
                        prior = ORDER[i - 2]
                        dve.wait_ge(full, num[('d1', 1) if prior == 'w' else ('p' + prior, 3)] + 1)
                        dve.wait_ge(mix_pool, i - 1)
                    for n in range(4):
                        c, h = ch(n)
                        dve.wait_ge(full, num[('m' + x, n)] + 1)
                        dve.scalar_tensor_tensor(batches(scaled[:, i % 2, c, half(n)]), batches(ps[:, num[('m' + x, n)] % 8, :]),
                                                 chip.vec('L1_xattn_maa_stack', c, MIX[x]), sx[:, c, bh(n), :], ALU.add, ALU.mult).then_inc(dve_free, 1)
                    dve.wait_ge(dve_free, nth(num[('m' + x, 3)]))
                    dve.tensor_tensor(batches(mixed[:, i % 2, 0, :]), batches(scaled[:, i % 2, 0, :]), cur(0), ALU.add).then_inc(mix_dve, 1)
                for n in range(4):
                    c, h = ch(n)
                    dve.wait_ge(th_ok, n + 1)
                    dve.scalar_tensor_tensor(gT[:, c, half(n)], th[:, n % 2, :], 1.0, ps[:, num[('pg', n)] % 8, :], ALU.add, ALU.mult).then_inc(dve_free, 1)

            @block.gpsimd
            def _(pool):
                for t in (kT, vT, wT):
                    pool.memset(t[:, :, :, 0:1], 0.0)
                for i, x in enumerate(ORDER):
                    pool.wait_ge(dve_free, nth(num[('m' + x, 3)]))
                    pool.tensor_tensor(batches(mixed[:, i % 2, 1, :]), batches(scaled[:, i % 2, 1, :]), cur(1), ALU.add).then_inc(mix_pool, 1)

            @block.scalar
            def _(act):
                for i, (what, n, reader) in enumerate(uses):
                    c, h = ch(n)
                    src = ps[:, i % 8, :]
                    if what == 'pg':
                        act.wait_ge(full, i + 1)
                        if n >= 2:
                            act.wait_ge(dve_free, nth(num[('pg', n - 2)]))
                        act.activation(th[:, n % 2, :], src, ACT.Tanh, scale=0.5).then_inc(th_ok, 1)
                        continue
                    if reader != 'act':
                        continue
                    act.wait_ge(full, i + 1)
                    if what == 'low':
                        dst, src = (lowA[:, half(n)], src) if n < 2 else (lowB[:, half(n)], src[0:KM, :])
                        act.activation(dst, src, ACT.Tanh).then_inc(act_free, 1)
                        if n == 3:
                            act.wait_ge(act_free, nth(i))
                            act.sem_inc(low_ok, 4)
                    elif what == 'd1':
                        act.activation(dec[:, half(n)], src[0:KD, :], ACT.Tanh).then_inc(act_free, 1)
                        if n == 1:
                            act.wait_ge(act_free, nth(i))
                            act.sem_inc(dec_ok, 2)
                    elif what == 'd2':
                        act.activation(e1[:, n % 2, :], src, ACT.Exp, bias=chip.vec('L1_xattn_time_decay', c)).then_inc(act_free, 1)
                        act.wait_ge(act_free, nth(i))
                        act.activation(wT[:, c, bh(n), 1:S], batches(e1[:, n % 2, :])[:, :, 0:S - 1], ACT.Exp, scale=-1.0).then_inc(e_ok, 1)
                        act.wait_ge(e_ok, n + 1)
                    elif what in ('pk', 'pv'):
                        act.activation((kT if what == 'pk' else vT)[:, c, bh(n), 1:R1], batches(src), ACT.Copy).then_inc(act_free, 1)
                    elif what == 'pr':
                        act.activation(rT[:, c, half(n)], src, ACT.Copy).then_inc(act_free, 1)


def stage_rwkv_scan(chip, m, kT, vT, rT, wT, gT):
    nc, ps = chip.nc, chip.psum
    HP = P // S1
    with ExitStack() as st:
        sb = lambda n, s, t=F32: st.enter_context(nc.sbuf_tensor(f"scan_{n}", s, t))
        sem = lambda n: chip.semaphore(f"scan_{n}")
        same = sb("same_head", [P, P])
        dmask = sb("d_mask", [P, S1])
        spread = sb("spread", [P, S1, P], F32R)
        gather = sb("gather", [P, S1, P])
        v_hi, v_lo = sb("v_hi", [P, NC, B, R1 + 1], F32R), sb("v_lo", [P, NC, B, R1 + 1], F32R)
        ruk = sb("ruk", [P, NC, TOK])
        kv = sb("kv", [P, 2, NC, B, S])
        state = sb("state", [P, 2, NC, B, S])
        z = sb("z", [P, 2, NC, TOK])
        att = sb("att", [P, NC, TOK])
        sq = sb("sq", [P, NC, TOK])
        ru = sb("ru", [P, NC, TOK])
        LATE = 2
        SEQ = (0, 2, 1, 3)
        epsc = sb("eps", [P, 1])
        (mats, dmask_ok, spread_ok, gather_ok, vcut, ruk_ok, v_full, kv_ok, s0_ok, st_ok, z_ok, g_full, ru_full, att_ok,
         mean_full, cent_ok, sq_ok, var_full, log_ok, rstd_ok, gn_ok, gated, o_full, ru_read) = (
            sem(n) for n in ("mats", "dmask_ok", "spread_ok", "gather_ok", "v_cut", "ruk_ok", "v_full", "kv_ok", "s0_ok",
                             "states_ok", "z_ok", "gathered", "ru_full", "att_ok", "mean_full", "centred", "squared", "var_full",
                             "log_ok", "rstd_ok", "normed", "gated", "out_full", "ru_read"))
        half = lambda n: slice((n % 2) * HALF, (n % 2 + 1) * HALF)
        bh = lambda n: slice(2 * (n % 2), 2 * (n % 2) + 2)
        batches = lambda ap: ap.rearrange("p (b s) -> p b s", s=S)
        flatb = lambda ap: ap.rearrange("p b s -> p (b s)")

        with nc.Block() as block:
            @block.gpsimd
            def _(pool):
                pool.memset(epsc[:, :], EPS0)
                pool.memset(gather[:, :, :], 0.0)
                pool.memset(same[:, :], 1.0).then_inc(mats, 1)
                v = same[:, :].rearrange("p (h e) -> p h e", e=S1)
                pool.wait_ge(mats, 1)
                pool.affine_select(out=v, in_=v, compare_op=ALU.is_ge, fill=0.0, base=0, pattern=[[-S1, HP], [0, S1]], channel_multiplier=1).then_inc(mats, 1)
                pool.wait_ge(mats, 2)
                pool.affine_select(out=v, in_=v, compare_op=ALU.is_ge, fill=0.0, base=S1 - 1, pattern=[[S1, HP], [0, S1]], channel_multiplier=-1).then_inc(mats, 1)
                for e in range(S1):
                    pool.wait_ge(st_ok, (e + 1) * NC)
                    if e >= 2:
                        pool.wait_ge(g_full, e - 1)
                    for c in range(NC):
                        pool.tensor_tensor(z[:, e % 2, c, :], rT[:, c, :], flatb(state[:, e % 2, c, :, :]), ALU.mult).then_inc(z_ok, 1)

            @block.vector
            def _(dve):
                dve.tensor_reduce(dmask[:, :], chip.ident[:, :].rearrange("p (h e) -> p e h", e=S1), AX.X, ALU.add).then_inc(dmask_ok, 1)
                dve.wait_ge(vcut, 1)
                dve.tensor_tensor(v_lo[:, :, :, 0:R1], vT[:, :, :, :], v_hi[:, :, :, 0:R1].bitcast(F32), ALU.subtract).then_inc(vcut, 1)
                dve.wait_ge(mats, 3)
                dve.wait_ge(dmask_ok, 1)
                for e in range(S1):
                    dve.tensor_scalar(spread[:, e, :], same[:, :], dmask[:, e:e + 1], None, ALU.mult).then_inc(spread_ok, 1)
                for e in range(S1):
                    dve.tensor_copy(gather[:, e, e:P:S1], same[:, e:P:S1]).then_inc(gather_ok, 1)
                for e in range(S1):
                    for n in range(4):
                        c = n // 2
                        u = e * 4 + n
                        dve.wait_ge(v_full, u + 1)
                        if e >= 2:
                            dve.wait_ge(st_ok, (e - 2) * NC + c + 1)
                        dve.tensor_tensor(kv[:, e % 2, c, bh(n), :], kT[:, c, bh(n), 0:S], batches(ps[:, u % 4, :]), ALU.mult).then_inc(kv_ok, 1)
                    dve.wait_ge(kv_ok, 4 * e + 4)
                    dve.tensor_copy(kv[:, e % 2, :, :, 0:1], m['s0'][:, :, :, e:e + 1]).then_inc(s0_ok, 1)
                    dve.wait_ge(s0_ok, e + 1)
                    for c in range(NC):
                        if e >= 2:
                            dve.wait_ge(z_ok, (e - 2) * NC + c + 1)
                        dve.tensor_tensor_scan(flatb(state[:, e % 2, c, :, :]), flatb(wT[:, c, :, :]), flatb(kv[:, e % 2, c, :, :]), 0.0, ALU.mult, ALU.add).then_inc(st_ok, 1)
                    if e == 0:
                        for c in range(NC):
                            dve.scalar_tensor_tensor(batches(ruk[:, c, :]), batches(rT[:, c, :]), chip.vec('L1_xattn_faaaa', c), kT[:, c, :, 1:R1], ALU.mult, ALU.mult).then_inc(ruk_ok, 1)
                for n in SEQ:
                    dve.wait_ge(ru_read, 4)
                    dve.tensor_tensor(batches(att[:, n // 2, half(n)]), batches(ru[:, n // 2, half(n)]), vT[:, n // 2, bh(n), 1:R1], ALU.mult).then_inc(att_ok, 1)

                def centre(i):
                    n = SEQ[i]
                    dve.wait_ge(mean_full, i + 1)
                    dve.scalar_tensor_tensor(att[:, n // 2, half(n)], ps[:, n, :], -1.0 / S1, att[:, n // 2, half(n)], ALU.mult, ALU.add).then_inc(cent_ok, 1)

                for i, n in enumerate(SEQ):
                    dve.wait_ge(att_ok, i + 1)
                    dve.wait_ge(g_full, S1 + i)
                    dve.tensor_tensor(att[:, n // 2, half(n)], att[:, n // 2, half(n)], ps[:, 4 + n, :], ALU.add).then_inc(att_ok, 1)
                    if i >= 2:
                        centre(i - 2)
                centre(2)
                centre(3)

                def gate(i):
                    n = SEQ[i]
                    dve.wait_ge(gn_ok, i + 1)
                    dve.scalar_tensor_tensor(z[:, 0, n // 2, half(n)], att[:, n // 2, half(n)], chip.vec('L1_xattn_gn_b', n // 2), gT[:, n // 2, half(n)],
                                             ALU.add, ALU.mult).then_inc(gated, 1)

                for i, n in enumerate(SEQ):
                    c = n // 2
                    dve.wait_ge(rstd_ok, i + 1)
                    dve.scalar_tensor_tensor(att[:, c, half(n)], att[:, c, half(n)], chip.vec('L1_xattn_gn_w', c), sq[:, c, half(n)], ALU.mult, ALU.mult).then_inc(gn_ok, 1)
                    if i:
                        gate(i - 1)
                gate(3)
                for q in range(4):
                    dve.wait_ge(o_full, q + 1)
                    dve.scalar_tensor_tensor(chip.x[:, 2 * q:2 * q + 2, :], ps[:, 4 + q, :].rearrange("p (j n) -> p j n", j=2), 0.5,
                                             chip.x[:, 2 * q:2 * q + 2, :], ALU.mult, ALU.add)

            @block.scalar
            def _(act):
                act.activation(v_hi[:, :, :, 0:R1], vT[:, :, :, :], ACT.Copy).then_inc(vcut, 1)
                for n in range(4):
                    act.wait_ge(ru_full, n + 1)
                    act.activation(ru[:, n // 2, half(n)], ps[:, 4 + n, :], ACT.Copy).then_inc(ru_read, 1)
                for i, n in enumerate(SEQ):
                    act.wait_ge(cent_ok, i + 1)
                    act.activation(sq[:, n // 2, half(n)], att[:, n // 2, half(n)], ACT.Square).then_inc(sq_ok, 1)
                for i, n in enumerate(SEQ):
                    act.wait_ge(var_full, i + 1)
                    act.activation(sq[:, n // 2, half(n)], ps[:, 4 + n, :], ACT.Ln, scale=1.0 / S1, bias=epsc[:, :]).then_inc(log_ok, 1)
                for i, n in enumerate(SEQ):
                    act.wait_ge(log_ok, i + 1)
                    act.activation(sq[:, n // 2, half(n)], sq[:, n // 2, half(n)], ACT.Exp, scale=-0.5).then_inc(rstd_ok, 1)

            @block.tensor
            def _(pe):
                pe.wait_ge(vcut, 2)
                for e in range(S1 + LATE):
                    if e < S1:
                        pe.wait_ge(spread_ok, e + 1)
                        for n in range(4):
                            u = e * 4 + n
                            if u >= 4:
                                pe.wait_ge(kv_ok, u - 3)
                            c = n // 2
                            out = batches(ps[:, u % 4, :])
                            pe.matmul(out, spread[:, e, :], v_hi[:, c, bh(n), 0:S], start=True, stop=False)
                            pe.matmul(out, spread[:, e, :], v_lo[:, c, bh(n), 0:S], start=False, stop=True).then_inc(v_full, 1)
                    if e == LATE - 1:
                        pe.wait_ge(ruk_ok, NC)
                        for n in range(4):
                            pe.matmul(ps[:, 4 + n, :], same[:, :], ruk[:, n // 2, half(n)], start=True, stop=True).then_inc(ru_full, 1)
                    if e >= LATE:
                        g = e - LATE
                        if g == 0:
                            pe.wait_ge(gather_ok, S1)
                            pe.wait_ge(ru_read, 4)
                        pe.wait_ge(z_ok, NC * g + NC)
                        for n in SEQ:
                            mm = pe.matmul(ps[:, 4 + n, :], gather[:, g, :], z[:, g % 2, n // 2, half(n)], start=g == 0, stop=g == S1 - 1)
                            if g == S1 - 1:
                                mm.then_inc(g_full, 1)
                        if g < S1 - 1:
                            mm.then_inc(g_full, 1)
                for i, n in enumerate(SEQ):
                    pe.wait_ge(att_ok, 4 + i + 1)
                    pe.matmul(ps[:, n, :], same[:, :], att[:, n // 2, half(n)], start=True, stop=True).then_inc(mean_full, 1)
                for i, n in enumerate(SEQ):
                    pe.wait_ge(sq_ok, i + 1)
                    pe.matmul(ps[:, 4 + n, :], same[:, :], sq[:, n // 2, half(n)], start=True, stop=True).then_inc(var_full, 1)
                for t in range(NT):
                    if t % 4 == 0:
                        pe.wait_ge(gated, 2 + 2 * (t // 4))
                        pe.wait_ge(log_ok, 4)
                    for c in range(NC):
                        mm = pe.matmul(ps[:, 4 + t // 2, (t % 2) * D:(t % 2 + 1) * D], z[:, 0, c, t * P:(t + 1) * P], m['w']['Wo'][:, c, :], start=c == 0, stop=c == NC - 1)
                    if t % 2:
                        mm.then_inc(o_full, 1)


def stage_channel_mix(chip, m, xe):
    nc, ps = chip.nc, chip.psum
    w = m['w']
    with ExitStack() as st:
        sb = lambda n, s, t=F32: st.enter_context(nc.sbuf_tensor(f"cm_{n}", s, t))
        sem = lambda n: chip.semaphore(f"cm_{n}")
        sx, xk, xr = sb("shift", [P, NC, B, S]), sb("xk", [P, NC, B, S]), sb("xr", [P, NC, B, S])
        relu, kk = sb("relu", [P, NC, TOK]), sb("kk", [P, NC, TOK])
        gate = sb("gate", [P, NT, D])
        t1 = sb("t1", [P, NT, D])
        shifted, mixed, k_full, r_ok, kk_ok, r_full, th_ok, g_ok, v_full, t_ok = (
            sem(n) for n in ("shifted", "mixed", "k_full", "relu_ok", "kk_ok", "r_full", "tanh_ok", "gate_ok", "v_full", "t_ok"))
        half = lambda n: slice((n % 2) * HALF, (n % 2 + 1) * HALF)
        bh = lambda n: slice(2 * (n % 2), 2 * (n % 2) + 2)
        cur = lambda c: xe[:, c, :, 1:R1]
        with nc.Block() as block:
            @block.vector
            def _(dve):
                dve.tensor_copy(xe[:, :, :, 0:1], chip.vecs[:, :, PREV:PREV + B].unsqueeze(3)).then_inc(shifted, 1)
                dve.wait_ge(shifted, 1)
                for c in range(NC):
                    dve.tensor_tensor(sx[:, c, :, :], xe[:, c, :, 0:S], cur(c), ALU.subtract).then_inc(shifted, 1)
                for dst, v in ((xk, 'L1_xattn_ffn_maa_k'), (xr, 'L1_xattn_ffn_maa_r')):
                    for c in range(NC):
                        dve.wait_ge(shifted, c + 2)
                        dve.scalar_tensor_tensor(dst[:, c, :, :], sx[:, c, :, :], chip.vec(v, c), cur(c), ALU.mult, ALU.add).then_inc(mixed, 1)
                for n in range(4):
                    dve.wait_ge(r_ok, n + 1)
                    dve.scalar_tensor_tensor(kk[:, n // 2, half(n)], ps[:, n, :], 0.0, relu[:, n // 2, half(n)], ALU.max, ALU.mult).then_inc(kk_ok, 1)
                for q in range(4):
                    dve.wait_ge(th_ok, q + 1)
                    dve.tensor_scalar(gate[:, 2 * q:2 * q + 2, :], gate[:, 2 * q:2 * q + 2, :], 0.5, 0.5, ALU.mult, ALU.add).then_inc(g_ok, 1)
                for q in range(4):
                    dve.wait_ge(v_full, q + 1)
                    dve.wait_ge(g_ok, q + 1)
                    dve.tensor_tensor(t1[:, 2 * q:2 * q + 2, :], gate[:, 2 * q:2 * q + 2, :], ps[:, q, :].rearrange("p (j n) -> p j n", j=2), ALU.mult).then_inc(t_ok, 1)
                    dve.wait_ge(t_ok, q + 1)
                    dve.tensor_tensor(chip.x[:, 2 * q:2 * q + 2, :], chip.x[:, 2 * q:2 * q + 2, :], t1[:, 2 * q:2 * q + 2, :], ALU.add)

            @block.scalar
            def _(act):
                for n in range(4):
                    act.wait_ge(k_full, n + 1)
                    act.activation(relu[:, n // 2, half(n)], ps[:, n, :], ACT.Relu).then_inc(r_ok, 1)
                for q in range(4):
                    act.wait_ge(r_full, q + 1)
                    act.activation(gate[:, 2 * q:2 * q + 2, :], ps[:, 4 + q, :].rearrange("p (j n) -> p j n", j=2), ACT.Tanh, scale=0.5).then_inc(th_ok, 1)

            @block.tensor
            def _(pe):
                for n in range(4):
                    pe.wait_ge(mixed, 2)
                    for c in range(NC):
                        mm = pe.matmul(ps[:, n, :], w['ffn_Wk'][:, c, (n // 2) * P:(n // 2 + 1) * P], xk[:, c, bh(n), :].rearrange("p b s -> p (b s)"), start=c == 0, stop=c == NC - 1)
                    mm.then_inc(k_full, 1)
                pe.wait_ge(mixed, 4)
                for t in range(NT):
                    for c in range(NC):
                        mm = pe.matmul(ps[:, 4 + t // 2, (t % 2) * D:(t % 2 + 1) * D], xr[:, c, t // 2, (t % 2) * P:(t % 2 + 1) * P], w['ffn_Wr'][:, c, :], start=c == 0, stop=c == NC - 1)
                    if t % 2:
                        mm.then_inc(r_full, 1)
                pe.wait_ge(kk_ok, 4)
                for t in range(NT):
                    for c in range(NC):
                        mm = pe.matmul(ps[:, t // 2, (t % 2) * D:(t % 2 + 1) * D], kk[:, c, t * P:(t + 1) * P], w['ffn_Wv'][:, c, :], start=c == 0, stop=c == NC - 1)
                    if t % 2:
                        mm.then_inc(v_full, 1)


class Small:

    def __init__(self, tag, heads, kv_heads, width, scale, passes):
        self.tag, self.H, self.KV, self.W, self.scale, self.passes = tag, heads, kv_heads, width, scale, passes
        self.R = 32 // width
        self.G = heads // 4
        self.kv_cols = kv_heads * width
        self.per_chunk = P // (4 * width)


L2 = Small("l2", 16, 16, 16, 16 ** -0.5, 2)
L3 = Small("l3", 32, 8, 8, 1.0 / float(np.sqrt(np.float32(8.0))), 1)
BIG = 3e38


def stage_turn(chip, tag, rows, out, out2=None, rows2=None):
    nc, ps = chip.nc, chip.psum
    jobs = [(rows, out, n) for n in range(4)] + ([(rows2, out2, n) for n in range(4)] if rows2 is not None else [])
    turned = chip.semaphore(f"{tag}_turned")
    with nc.Block() as block:
        @block.tensor
        def _(pe):
            for k, (src, _dst, n) in enumerate(jobs):
                for t in range(4):
                    mm = pe.transpose(ps[:, k, t * P:(t + 1) * P], src[:, (n % 2) * 4 + t, (n // 2) * P:(n // 2 + 1) * P], chip.ident[:, :])
                mm.then_inc(turned, 1)

        def evacuate(eng, mine, copy):
            for k, (_src, dst, n) in enumerate(jobs):
                if k % 2 == mine:
                    eng.wait_ge(turned, k + 1)
                    copy(dst[:, n // 2, (n % 2) * HALF:(n % 2 + 1) * HALF], ps[:, k, :])

        @block.scalar
        def _(act):
            evacuate(act, 0, lambda o, i: act.activation(o, i, ACT.Copy))

        @block.vector
        def _(dve):
            evacuate(dve, 1, dve.tensor_copy)


def stage_small_project(chip, sh, wq, wk, wv, q_src, k_src, q_bias, k_bias, v_bias, mem):
    nc, ps = chip.nc, chip.psum
    tag, KC = sh.tag, max(1, sh.kv_cols // P)
    KR = min(P, sh.kv_cols)
    q_hi, q_lo, k_hi, k_lo, v1 = mem
    with ExitStack() as st:
        sb = lambda n, s, t=F32: st.enter_context(nc.sbuf_tensor(f"{tag}_{n}", s, t))
        sem = lambda n: chip.semaphore(f"{tag}_{n}")
        full = sb("qk_full", [P, 8, BANK])
        nq = sb("neg_bq", [P, NC])
        pe_full, whole, hi_ok, lo_ok, v_full, nq_ok = (sem(n) for n in ("p_full", "p_whole", "p_hi", "p_lo", "p_v", "p_bias"))
        pieces = [('q', c, h) for c in range(NC) for h in range(2)] + [('k', c, h) for c in range(KC) for h in range(2)]
        dst = lambda p, hi: ((q_hi if hi else q_lo) if p[0] == 'q' else (k_hi if hi else k_lo))[0:P if p[0] == 'q' else KR, p[1], p[2] * HALF:(p[2] + 1) * HALF]
        np_ = len(pieces)
        with nc.Block() as block:
            @block.tensor
            def _(pe):
                for i, (w, c, h) in enumerate(pieces):
                    cols = slice(h * HALF, (h + 1) * HALF)
                    rows = P if w == 'q' else KR
                    for k in range(NC):
                        mm = pe.matmul(ps[0:rows, i, :], (wq if w == 'q' else wk)[:, k, c * P:c * P + rows],
                                       (q_src if w == 'q' else k_src)[:, k, cols], start=k == 0, stop=k == NC - 1)
                    mm.then_inc(pe_full, 1)
                for t in range(NT):
                    if t % 2 == 0 and t // 2 < np_:
                        pe.wait_ge(whole, t // 2 + 1)
                    for k in range(NC):
                        mm = pe.matmul(ps[:, t // 2, (t % 2) * D:(t % 2) * D + sh.kv_cols], k_src[:, k, t * P:(t + 1) * P], wv[:, k, :],
                                       start=k == 0, stop=k == NC - 1)
                    if t % 2:
                        mm.then_inc(v_full, 1)

            @block.scalar
            def _(act):
                if q_bias:
                    act.wait_ge(nq_ok, NC)
                for i, (w, c, h) in enumerate(pieces):
                    rows = P if w == 'q' else KR
                    act.wait_ge(pe_full, i + 1)
                    bias = 0.0
                    if q_bias:
                        bias = nq[:, c:c + 1] if w == 'q' else k_bias[0:rows, :]
                    act.activation(full[0:rows, i, :], ps[0:rows, i, :], ACT.Identity, scale=-sh.scale if w == 'q' else 1.0, bias=bias).then_inc(whole, 1)

            @block.vector
            def _(dve):
                if q_bias:
                    for c in range(NC):
                        dve.tensor_scalar(nq[:, c:c + 1], q_bias(c), -sh.scale, None, ALU.mult).then_inc(nq_ok, 1)
                dve.memset(v1[:, :, :, sh.W:sh.W + 1], 1.0)
                dve.memset(v1[:, :, :, sh.W + 1:32], 0.0)
                if KR < P:
                    for half_k in (k_hi, k_lo):
                        dve.memset(half_k[KR:P, 0, :].bitcast(F32), 0.0)
                for i, p in enumerate(pieces):
                    rows = P if p[0] == 'q' else KR
                    dve.wait_ge(whole, i + 1)
                    dve.tensor_copy(dst(p, True), full[0:rows, i, :]).then_inc(hi_ok, 1)
                for t in range(NT):
                    dve.wait_ge(v_full, t // 2 + 1)
                    src = ps[:, t // 2, (t % 2) * D:(t % 2) * D + sh.kv_cols].rearrange("p (h e) -> p h e", e=sh.W)
                    if v_bias is None:
                        dve.tensor_copy(v1[:, t, :, 0:sh.W], src)
                    else:
                        dve.tensor_tensor(v1[:, t, :, 0:sh.W], src, v_bias.rearrange("p (h e) -> p h e", e=sh.W), ALU.add)

            @block.gpsimd
            def _(pool):
                for i, p in enumerate(pieces):
                    rows = P if p[0] == 'q' else KR
                    pool.wait_ge(hi_ok, i + 1)
                    pool.tensor_tensor(dst(p, False), full[0:rows, i, :], dst(p, True).bitcast(F32), ALU.subtract)


def stage_small_stack(chip, sh, mem, qs, ks):
    nc, ps = chip.nc, chip.psum
    W, G, R, NK = sh.W, sh.G, sh.R, sh.passes
    q_hi, q_lo, k_hi, k_lo, _v1 = mem
    with ExitStack() as st:
        sb = lambda n, s, t=F32: st.enter_context(nc.sbuf_tensor(f"{sh.tag}_{n}", s, t))
        sem = lambda n: chip.semaphore(f"{sh.tag}_{n}")
        selq = sb("place_q", [P, 2, sh.per_chunk, 4, R, W], F32R)
        selk = sb("place_k", [P, 1 if NK == 2 else 2, sh.per_chunk if NK == 2 else G, 4, R, W], F32R)
        zeroed, placed, full, act_read, dve_read = (sem(n) for n in ("zeroed", "placed", "stack_full", "stack_act", "stack_dve"))
        pieces = [(w, g, h) for h in range(2) for w, n in (('q', G), ('k', NK * G)) for g in range(n)]
        cols = lambda h: slice(h * HALF, (h + 1) * HALF)

        with nc.Block() as block:
            @block.gpsimd
            def _(pool):
                pool.memset(selq[:].rearrange("p a g j r w -> p (a g j r w)").bitcast(F32), 0.0).then_inc(zeroed, 1)
                pool.memset(selk[:].rearrange("p a g j r w -> p (a g j r w)").bitcast(F32), 0.0).then_inc(zeroed, 1)

            @block.tensor
            def _(pe):
                pe.wait_ge(placed, 1)
                for s, (w, g, h) in enumerate(pieces):
                    if s >= 8:
                        pe.wait_ge(act_read if s % 2 == 0 else dve_read, (s - 8) // 2 + 1)
                    out = ps[:, s % 8, :]
                    if w == 'q':
                        for part, src in enumerate((q_hi, q_lo)):
                            mm = pe.matmul(out, selq[:, part, g % sh.per_chunk].rearrange("p j r w -> p (j r w)"),
                                           src[:, g // sh.per_chunk, cols(h)], start=part == 0, stop=part == 1)
                    elif NK == 2:
                        mm = pe.matmul(out, selk[:, 0, g % sh.per_chunk].rearrange("p j r w -> p (j r w)"),
                                       (k_hi if g < G else k_lo)[:, (g % G) // sh.per_chunk, cols(h)], start=True, stop=True)
                    else:
                        for part, src in enumerate((k_hi, k_lo)):
                            mm = pe.matmul(out, selk[:, part, g].rearrange("p j r w -> p (j r w)"), src[:, 0, cols(h)],
                                           start=part == 0, stop=part == 1)
                    mm.then_inc(full, 1)

            def evacuate(eng, mine, done, copy):
                for s, (w, g, h) in enumerate(pieces):
                    if s % 2 == mine:
                        eng.wait_ge(full, s + 1)
                        copy((qs if w == 'q' else ks)[:, g, cols(h)], ps[:, s % 8, :]).then_inc(done, 1)

            @block.scalar
            def _(act):
                evacuate(act, 0, act_read, lambda o, i: act.activation(o, i, ACT.Copy))

            @block.vector
            def _(dve):
                dve.wait_ge(zeroed, 2)
                ident = lambda n, k: chip.ident[:, 0:n * k * W].rearrange("p (g j w) -> p g j w", g=n, w=W)
                for r in range(R):
                    for g in range(sh.per_chunk):
                        last = dve.tensor_copy(selq[:, r % 2, g, :, r, :], ident(sh.per_chunk, 4)[:, g])
                if NK == 2:
                    for r in range(R):
                        for g in range(sh.per_chunk):
                            last = dve.tensor_copy(selk[:, 0, g, :, r, :], ident(sh.per_chunk, 4)[:, g])
                else:
                    for r in range(R):
                        for j in range(4):
                            last = dve.tensor_copy(selk[:, r // 2, :, j, r, :], ident(G, 1)[:, :, 0])
                last.then_inc(placed, 1)
                evacuate(dve, 1, dve_read, dve.tensor_copy)


def stage_small_attention(chip, sh, qs, ks, v1, masks):
    nc, ps = chip.nc, chip.psum
    tag, H, W, G, NK = sh.tag, sh.H, sh.W, sh.G, sh.passes
    LEAD = 3
    NM = masks.shape[1] // B
    with ExitStack() as st:
        sb = lambda n, s, t=F32: st.enter_context(nc.sbuf_tensor(f"{tag}_{n}", s, t))
        sem = lambda n: chip.semaphore(f"{tag}_{n}")
        mask = sb("mask_neg", [P, NM, S])
        sc = sb("scores", [P, 4, 2, S])
        m = sb("neg_max", [P, 4, 2])
        pr = sb("prob", [P, 4, 2, S])
        pT = sb("prob_T", [P, 4, BANK])
        vb = sb("v_batch", [P, 2, sh.KV, 32])
        qb, kb = sb("q_batch", [P, G, S], F32R), sb("k_batch", [P, NK * G, S], F32R)
        stack_in = [sem(f"stack_in{g}") for g in range(G)]
        s_full, s_begun, s_read, p_ok, turned, act_ev, dve_ev, a_done, a_read, mask_ok = (
            sem(n) for n in ("scores_full", "scores_begun", "scores_read", "exp_ok", "turned", "turned_act", "turned_dve",
                             "sum_done", "sums_read", "mask_ok"))
        v_in = [sem(f"v_in{g}") for g in range(G)]
        assert H % 4 == 0

        def batches(eng, step):
            with eng.Fori(0, B - 1) as b:
                step(b, False)
            step(B - 1, True)

        def ahead(u, lead, last):
            n, v = (u + lead) // H, (u + lead) % H
            return None if n and last else (n, v)

        with nc.Block() as block:
            @block.tensor
            def _(pe):
                pe.sem_inc(turned, 4)
                pe.sem_inc(a_done, 4)

                def scores(b, u):
                    g, j = u // 4, u % 4
                    rows = slice(32 * j, 32 * j + 32)
                    if j == 0:
                        pe.wait_ge(stack_in[g], b * 16 * (1 + NK) + 16 * (1 + NK))
                    pe.wait_ge(s_read, b * H + u + 1)
                    for q in range(2):
                        for k in range(NK):
                            mm = pe.matmul(ps[:, u % 4, q * S:(q + 1) * S], qb[rows, g, q * P:(q + 1) * P], kb[rows, k * G + g, :],
                                           start=k == 0, stop=k == NK - 1, tile_position=(32 * j, 0))
                    mm.then_inc(s_full, 1)

                def turn(b, u):
                    pe.wait_ge(p_ok, b * H + u + 5)
                    pe.wait_ge(act_ev if u % 2 == 0 else dve_ev, b * (H // 2) + u // 2 + 1)
                    for t in range(2):
                        for q in range(2):
                            mm = pe.transpose(ps[:, 4 + u % 2, t * S + q * P:t * S + (q + 1) * P], pr[:, u % 4, q, t * P:(t + 1) * P], chip.ident[:, :])
                    mm.then_inc(turned, 1)

                def sums(b, u):
                    if u % 4 == 0:
                        pe.wait_ge(v_in[u // 4], b * 16 + 16)
                        pe.wait_ge(a_read, b * G + u // 4 + 1)
                    pe.wait_ge(act_ev if u % 2 == 0 else dve_ev, b * (H // 2) + u // 2 + 2)
                    for t in range(2):
                        mm = pe.matmul(ps[32 * (u % 4):32 * (u % 4) + 32, 6 + u // 4 % 2, 0:S], vb[:, t, u * sh.KV // H, :],
                                       pT[:, u % 4, t * S:(t + 1) * S], start=t == 0, stop=t == 1, tile_position=(0, 32 * (u % 4)))
                    mm.then_inc(a_done, 1)

                for u in range(LEAD):
                    scores(0, u)

                def step(b, last):
                    for u in range(H):
                        turn(b, u)
                        nxt = ahead(u, LEAD, last)
                        if nxt:
                            scores(b + nxt[0], nxt[1])
                        if u:
                            sums(b, u - 1)
                    sums(b, H - 1)

                batches(pe, step)

            @block.scalar
            def _(act):
                act.sem_inc(act_ev, 1)
                act.sem_inc(p_ok, 4)

                def exp(b, u):
                    act.wait_ge(s_read, b * H + u + 5)
                    act.wait_ge(turned, b * H + u + 1)
                    for q in range(2):
                        e = act.activation(pr[:, u % 4, q, :], sc[:, u % 4, q, :], ACT.Exp, scale=-1.0, bias=m[:, u % 4, q:q + 1])
                    e.then_inc(p_ok, 1)

                for u in range(LEAD - 1):
                    exp(0, u)

                def step(b, last):
                    for u in range(H):
                        if u % 2 == 0:
                            act.wait_ge(turned, b * H + u + 5)
                            act.wait_ge(a_done, b * H + u + 1)
                            act.activation(pT[:, u % 4, :], ps[:, 4, :], ACT.Copy).then_inc(act_ev, 1)
                        nxt = ahead(u, LEAD - 1, last)
                        if nxt:
                            exp(b + nxt[0], nxt[1])

                batches(act, step)

            @block.vector
            def _(dve):
                dve.sem_inc(dve_ev, 1)
                dve.sem_inc(s_read, 4)
                dve.sem_inc(a_read, 2)

                def least(b, u):
                    if u == 0:
                        dve.wait_ge(s_read, b * H + 4)
                        dve.tensor_copy(mask[:, :, :], masks[:, bass.ds(b * NM, NM), :]).then_inc(mask_ok, 1)
                        dve.wait_ge(mask_ok, b + 1)
                    dve.wait_ge(s_full, b * H + u + 1)
                    dve.wait_ge(p_ok, b * H + u + 1)
                    dve.sem_inc(s_begun, 1)
                    for q in range(2):
                        e = dve.tensor_tensor_reduce(sc[:, u % 4, q, :], ps[:, u % 4, q * S:(q + 1) * S], mask[:, q % NM, :],
                                                     1.0, BIG, ALU.add, ALU.min, m[:, u % 4, q:q + 1])
                    e.then_inc(s_read, 1)

                def keep(b, g):
                    dve.wait_ge(a_done, b * H + 4 * g + 8)
                    dve.tensor_copy(qs[:, g, bass.ds(b * S, S)].bitcast(F32), ps[:, 6 + g % 2, 0:S]).then_inc(a_read, 1)

                for u in range(LEAD):
                    least(0, u)

                def step(b, last):
                    for u in range(H):
                        if u % 2:
                            dve.wait_ge(turned, b * H + u + 5)
                            dve.wait_ge(a_done, b * H + u + 1)
                            dve.tensor_copy(pT[:, u % 4, :], ps[:, 5, :]).then_inc(dve_ev, 1)
                        nxt = ahead(u, LEAD, last)
                        if nxt:
                            least(b + nxt[0], nxt[1])
                        if u % 4 == 0 and u:
                            keep(b, u // 4 - 1)
                    keep(b, G - 1)

                batches(dve, step)

            @block.sync
            def _(sp):
                def load(b, g):
                    sp.dma_start(qb[:, g, :].bitcast(F32), qs[:, g, bass.ds(b * S, S)].bitcast(F32)).then_inc(stack_in[g], 16)
                    for k in range(NK):
                        sp.dma_start(kb[:, k * G + g, :].bitcast(F32), ks[:, k * G + g, bass.ds(b * S, S)].bitcast(F32)).then_inc(stack_in[g], 16)

                def load_v(b, g):
                    n = sh.KV // G * 32
                    sp.dma_start(vb[:].rearrange("p t h w -> p t (h w)")[:, :, g * n:(g + 1) * n],
                                 v1[:].rearrange("p t h w -> p t (h w)")[:, bass.ds(2 * b, 2), g * n:(g + 1) * n]).then_inc(v_in[g], 16)

                for g in range(G):
                    load(0, g)
                    load_v(0, g)
                with sp.Fori(0, B - 1) as b:
                    for g in range(G):
                        sp.wait_ge(s_full, b * H + 4 * g + 4)
                        load(b + 1, g)
                        if g:
                            sp.wait_ge(a_done, b * H + 4 * g + 4)
                            load_v(b + 1, g - 1)
                    sp.wait_ge(a_done, b * H + H + 4)
                    load_v(b + 1, G - 1)


def stage_small_divide(chip, sh, qs, att):
    nc, ps = chip.nc, chip.psum
    W, G = sh.W, sh.G
    with ExitStack() as st:
        sem = lambda n: chip.semaphore(f"{sh.tag}_{n}")
        turned, read, inv_ok = sem("sums_turned"), sem("turned_read"), sem("inv_ok")
        jobs = [(t, g) for t in range(NT) for g in range(0, G, 4)]
        rec = st.enter_context(nc.sbuf_tensor(f"{sh.tag}_inv_total", [P, 8, BANK // 32], F32))
        with nc.Block() as block:
            @block.tensor
            def _(pe):
                for k, (t, g) in enumerate(jobs):
                    if k >= 8:
                        pe.wait_ge(read, k - 7)
                    for i in range(4):
                        mm = pe.transpose(ps[:, k % 8, i * P:(i + 1) * P], qs[:, g + i, t * P:(t + 1) * P].bitcast(F32), chip.ident[:, :])
                    mm.then_inc(turned, 1)

            @block.vector
            def _(dve):
                heads = lambda k: ps[:, k % 8, :].rearrange("p (h w) -> p h w", w=32)

                def divide(k):
                    t, g = jobs[k]
                    dve.wait_ge(inv_ok, k + 1)
                    dve.tensor_tensor(att[:, t, g * 4 * W:(g + 4) * 4 * W].rearrange("p (h w) -> p h w", w=W), heads(k)[:, :, 0:W],
                                      rec[:, k % 8, :].unsqueeze(2).to_broadcast([P, 16, W]), ALU.mult).then_inc(read, 1)

                for k in range(len(jobs)):
                    dve.wait_ge(turned, k + 1)
                    dve.reciprocal(rec[:, k % 8, :].unsqueeze(2), heads(k)[:, :, W:W + 1]).then_inc(inv_ok, 1)
                    if k:
                        divide(k - 1)
                divide(len(jobs) - 1)


def stage_small_output(chip, sh, attT, wo, finish):
    nc, ps = chip.nc, chip.psum
    full = chip.semaphore(f"{sh.tag}_out_full")
    with nc.Block() as block:
        @block.tensor
        def _(pe):
            for t in range(NT):
                for c in range(NC):
                    mm = pe.matmul(ps[:, 4 + t // 2, (t % 2) * D:(t % 2 + 1) * D], attT[:, c, t * P:(t + 1) * P], wo[:, c, :], start=c == 0, stop=c == NC - 1)
                if t % 2:
                    mm.then_inc(full, 1)

        @block.vector
        def _(dve):
            for n in range(NT // 2):
                dve.wait_ge(full, n + 1)
                finish(dve, slice(2 * n, 2 * n + 2), ps[:, 4 + n, :].rearrange("p (t n) -> p t n", t=2))


def stage_final_norm(chip, out):
    nc = chip.nc
    with ExitStack() as st:
        sb = lambda n, s: st.enter_context(nc.sbuf_tensor(f"fin_{n}", s, F32))
        sem = lambda n: chip.semaphore(f"fin_{n}")
        bn, mv, ve, rstd = sb("bn", [P, NT, 6]), sb("mean_var", [P, NT, 2]), sb("var_eps", [P, NT]), sb("rstd", [P, NT])
        y, z = sb("y", [P, NT, D]), sb("z", [P, NT, D])
        stats, aggr, var_ok, rstd_ok, y_ok, z_ok, o_ok, stored = (sem(n) for n in ("stats", "aggr", "var_ok", "rstd_ok", "y_ok", "z_ok", "o_ok", "stored"))
        R = ROWS.index('L3_xattn_gamma')
        with nc.Block() as block:
            @block.gpsimd
            def _(pool):
                pool.wait_ge(var_ok, 1)
                pool.tensor_tensor(rstd[:, :], ve[:, :], chip.expo[:, :], ALU.pow).then_inc(rstd_ok, 1)

            @block.vector
            def _(dve):
                for j in range(NT):
                    dve.bn_stats(bn[:, j, :], chip.x[:, j, :]).then_inc(stats, 1)
                for j in range(NT):
                    dve.wait_ge(stats, j + 1)
                    dve.bn_aggr(mv[:, j, :], bn[:, j, :]).then_inc(aggr, 1)
                dve.wait_ge(aggr, NT)
                dve.tensor_scalar(ve[:, :], mv[:, :, 1], 1e-6, None, ALU.add).then_inc(var_ok, 1)
                dve.wait_ge(rstd_ok, 1)
                for j in range(NT):
                    dve.tensor_scalar(y[:, j, :], chip.x[:, j, :], mv[:, j, 0:1], rstd[:, j:j + 1], ALU.subtract, ALU.mult).then_inc(y_ok, 1)
                    if j % 2:
                        q = j // 2
                        two = slice(2 * q, 2 * q + 2)
                        dve.wait_ge(y_ok, j + 1)
                        dve.tensor_tensor(z[:, two, :], y[:, two, :], chip.rows[:, R:R + 1, :].to_broadcast([P, 2, D]), ALU.mult).then_inc(z_ok, 1)
                        dve.wait_ge(z_ok, q + 1)
                        dve.tensor_tensor(y[:, two, :], z[:, two, :], chip.rows[:, R + 1:R + 2, :].to_broadcast([P, 2, D]), ALU.add).then_inc(o_ok, 1)

            @block.sync
            def _(sp):
                for q in range(4):
                    sp.wait_ge(o_ok, q + 1)
                    sp.dma_start(tiles_of(out)[:, 2 * q:2 * q + 2, :], y[:, 2 * q:2 * q + 2, :]).then_inc(stored, 16)
                sp.wait_ge(stored, 64)


def layers_2_and_3(chip, d, out):
    nc = chip.nc
    with ExitStack() as both:
        sb = lambda n, s, t=F32: both.enter_context(nc.sbuf_tensor(n, s, t))
        ld = chip.semaphore("ld_layers23")
        w2 = {n: sb(f"l2_w{n}", [P, NC, D]) for n in 'qkvo'}
        w3 = {n: sb(f"l3_w{n}", [P, NC, L3.kv_cols if n in 'kv' else D]) for n in 'qkvo'}
        mask8 = sb("mask_bytes", [P, B * S], U8)
        gate = sb("gate", [P, 1])
        bk3, bv3 = sb("l3_bk", [L3.kv_cols, 1]), sb("l3_bv", [P, L3.kv_cols])
        aT, cT, xT = sb("ctx_normed_T", [P, NC, TOK]), sb("ctx_T", [P, NC, TOK]), sb("x_T", [P, NC, TOK])
        mask3 = sb("mask3", [P, NT, S])
        maskf, masks2 = sb("mask_f", [P, B, S]), sb("mask2", [P, B, S])

        def load(sp):
            total = 0
            for n in 'qkvo':
                sp.dma_start(w2[n][:, :, :], d[f'L2_xattn_W{n}_T'].rearrange("(c p) n -> p c n", p=P)).then_inc(ld, 16)
                sp.dma_start(w3[n][:, :, :], d[f'L3_xattn_W{n}'].rearrange("(c p) n -> p c n", p=P)).then_inc(ld, 16)
            sp.dma_start(mask8[:, :], d['mask_BxS2_bf1'].rearrange("(a b) s -> a (b s)", a=1).to_broadcast([P, B * S])).then_inc(ld, 16)
            sp.dma_start(gate[:, :], d['L2_xattn_gate'].rearrange("(a n) -> a n", a=1).to_broadcast([P, 1])).then_inc(ld, 16)
            sp.dma_start(bk3[:, :], d['L3_xattn_bk'].rearrange("(n a) -> n a", a=1)).then_inc(ld, 16)
            sp.dma_start(bv3[:, :], d['L3_xattn_bv'].rearrange("(a n) -> a n", a=1).to_broadcast([P, L3.kv_cols])).then_inc(ld, 16)
            sp.dma_start(mask3[:, :, :], d['mask_Bx1xSxS2_ff0'].rearrange("b a (u p) t -> p (b a u) t", p=P)).then_inc(ld, 16)
            sp.wait_ge(ld, 16 * 13)

        flat = lambda c, half: aT[:, c, half * HALF:(half + 1) * HALF].rearrange("p (b s) -> p b s", b=2)
        stage_layernorm(chip, "ln_ctx", chip.ctx, lambda c: chip.vec('L2_xattn_ln_gamma', c), lambda c: chip.vec('L2_xattn_ln_beta', c),
                        EPS0, plain=flat, prefetch=load)
        stage_turn(chip, "t2", chip.x, xT, cT, chip.ctx)

        steps = chip.semaphore("mask_steps")
        with nc.Block() as block:
            @block.vector
            def _(dve):
                mf = maskf[:, :, :].rearrange("p b s -> p (b s)")
                dve.tensor_copy(mf, mask8[:, :]).then_inc(steps, 1)
                dve.wait_ge(steps, 1)
                dve.tensor_scalar(mf, mf, 1.0, -BIG, ALU.subtract, ALU.mult).then_inc(steps, 1)
                dve.wait_ge(steps, 2)
                dve.tensor_scalar(masks2[:, :, :].rearrange("p b s -> p (b s)"), mf, BIG, None, ALU.mult)

            @block.scalar
            def _(act):
                act.activation(gate[:, :], gate[:, :], ACT.Tanh)

        def attend(sh, w, q_src, k_src, biases, masks, att, finish):
            with ExitStack() as layer:
                t = lambda n, s, dt=F32R: layer.enter_context(nc.sbuf_tensor(f"{sh.tag}_{n}", s, dt))
                qs, ks = t("q_stack", [P, sh.G, TOK]), t("k_stack", [P, sh.passes * sh.G, TOK])
                v1 = t("v_ones", [P, NT, sh.KV, 32], F32)
                with ExitStack() as compact:
                    t = lambda n, s: compact.enter_context(nc.sbuf_tensor(f"{sh.tag}_{n}", s, F32R))
                    KC = max(1, sh.kv_cols // P)
                    mem = (t("q_hi", [P, NC, TOK]), t("q_lo", [P, NC, TOK]), t("k_hi", [P, KC, TOK]), t("k_lo", [P, KC, TOK]), v1)
                    stage_small_project(chip, sh, w['q'], w['k'], w['v'], q_src, k_src, *biases, mem)
                    stage_small_stack(chip, sh, mem, qs, ks)
                stage_small_attention(chip, sh, qs, ks, v1, masks)
                stage_small_divide(chip, sh, qs, att)
            stage_turn(chip, f"{sh.tag}_att", att, xT)
            stage_small_output(chip, sh, xT, w['o'], finish)

        att = sb("att_rows", [P, NT, D])

        def gated(dve, two, o):
            dve.scalar_tensor_tensor(chip.x[:, two, :], o, gate[:, :], chip.x[:, two, :], ALU.mult, ALU.add)

        attend(L2, w2, xT, aT, (None, None, None), masks2, att, gated)

        stage_turn(chip, "t3", chip.x, xT)
        with nc.Block() as block:
            @block.vector
            def _(dve):
                r = ROWS.index('L3_xattn_bo')
                dve.tensor_tensor(chip.x[:, :, :], chip.x[:, :, :], chip.rows[:, r:r + 1, :].to_broadcast([P, NT, D]), ALU.add)

            @block.gpsimd
            def _(pool):
                pool.tensor_scalar(mask3[:, :, :], mask3[:, :, :], -1.0, None, ALU.mult)

        attend(L3, w3, xT, cT, (lambda c: chip.vec('L3_xattn_bq', c), bk3, bv3[:, :]), mask3, att,
               lambda dve, two, o: dve.tensor_tensor(chip.x[:, two, :], o, chip.x[:, two, :], ALU.add))
        stage_final_norm(chip, out)


def build(nc, d, out):
    with ExitStack() as stack:
        chip = Chip(nc, stack)
        with ExitStack() as l0:
            sb = lambda n, s, t=F32R: l0.enter_context(nc.sbuf_tensor(n, s, t))
            ctx_hi, ctx_lo = sb("ctxT_hi", [P, NC, TOK]), sb("ctxT_lo", [P, NC, TOK])
            h_hi, h_lo = sb("hT_hi", [P, NC, TOK]), sb("hT_lo", [P, NC, TOK])
            stage_setup(chip, d, ctx_hi, ctx_lo)
            for a in (1, 2):
                L = f"L0_xattn_ln{a}_"
                with ExitStack() as attention:
                    weights = attention_weights(chip, attention, d, a)
                    stage_layernorm(chip, f"ln{a}", chip.x, lambda c: chip.vec(L + "scale", c), lambda c: chip.vec(L + "offset", c),
                                    EPS0, hi=h_hi, lo=h_lo, add=ROWS.index(f"L0_xattn_bo{a}"), prefetch=weights[3])
                    stage_cross_attention(chip, a, weights, h_hi, h_lo, ctx_hi, ctx_lo)
            w1_raw, w2_raw = sb("w_fc1_raw", [P, NC, FF], F32), sb("w_fc2_raw", [P, NF, D], F32)
            ld_w = chip.semaphore("ld_mlp")

            def load_mlp(sp):
                sp.dma_start(w1_raw[:, :, :], d['L0_xattn_w_fc1'].rearrange("(c p) n -> p c n", p=P)).then_inc(ld_w, 16)
                sp.dma_start(w2_raw[:, :, :], d['L0_xattn_w_fc2'].rearrange("(f p) n -> p f n", p=P)).then_inc(ld_w, 16)

            L = "L0_xattn_ln_mlp_"
            stage_layernorm(chip, "ln_mlp", chip.x, lambda c: chip.vec(L + "scale", c), lambda c: chip.vec(L + "offset", c),
                            EPS0, hi=h_hi, lo=h_lo, add=ROWS.index("L0_xattn_b_fc2"), prefetch=load_mlp)
            stage_mlp(chip, w1_raw, w2_raw, ld_w, h_hi, h_lo)
        chip.renew_semaphores()
        with ExitStack() as l1:
            sb = lambda n, s: l1.enter_context(nc.sbuf_tensor(n, s, F32))
            m, load = layer1_memory(chip, l1, d)
            xe = sb("xn_T", [P, NC, B, R1])
            after = lambda c, half: xe[:, c, 2 * half:2 * half + 2, 1:R1]
            stage_layernorm(chip, "ln_r1", chip.x, lambda c: chip.vec('L1_xattn_ln1_w', c), lambda c: chip.vec('L1_xattn_ln1_b', c),
                            EPS0, plain=after, prefetch=load)
            with ExitStack() as seq:
                sq = lambda n, s: seq.enter_context(nc.sbuf_tensor(n, s, F32))
                kT, vT = sq("k_T", [P, NC, B, R1]), sq("v_T", [P, NC, B, R1])
                wT = sq("w_T", [P, NC, B, S])
                rT, gT = sq("r_T", [P, NC, TOK]), sq("g_T", [P, NC, TOK])
                stage_rwkv_mix(chip, m, xe, kT, vT, rT, wT, gT)
                stage_rwkv_scan(chip, m, kT, vT, rT, wT, gT)
            stage_layernorm(chip, "ln_r2", chip.x, lambda c: chip.vec('L1_xattn_ln2_w', c), lambda c: chip.vec('L1_xattn_ln2_b', c),
                            EPS0, plain=after)
            stage_channel_mix(chip, m, xe)
        chip.renew_semaphores()
        layers_2_and_3(chip, d, out)


_DIRECT = ['x', 'ctx_2048'] + [f'L0_xattn_w{n}{a}' for a in (1, 2) for n in 'qkvo'] + ['L0_xattn_w_fc1', 'L0_xattn_w_fc2']
_DIRECT += [f'L1_xattn_{n}' for n in ('maa_w1', 'maa_w2', 'decay_w1', 'decay_w2')]
_DIRECT += ['mask_BxS2_bf1', 'mask_Bx1xSxS2_ff0', 'L2_xattn_gate', 'L3_xattn_bk', 'L3_xattn_bv'] + [f'L3_xattn_W{n}' for n in 'qkvo']
_TURNED = [f'L1_xattn_{n}' for n in L1_WEIGHTS] + [f'L2_xattn_W{n}' for n in 'qkvo']


def kernel(**inputs):
    import numpy as _np
    import concourse.bacc as _bacc
    from concourse import mybir as _mybir
    from concourse.bass_utils import run_bass_kernel_spmd as _run

    laid = {n: _np.ascontiguousarray(inputs[n]) for n in _DIRECT}
    laid.update({n + '_T': _np.ascontiguousarray(_np.transpose(inputs[n])) for n in _TURNED})
    laid['vecs'] = _np.concatenate([_np.reshape(inputs[n], (-1, D)) for n in VECS]
                                   + [_np.reshape(inputs['ctx_2048'][:, i], (-1, D)) for i in range(2)], 0)
    laid['hvecs'] = _np.concatenate([_np.reshape(inputs[n], (-1, K0)) for n in HVECS + ['L0_xattn_b_fc1']], 0)
    laid['rows'] = _np.concatenate([_np.reshape(inputs[n], (-1,)) for n in ROWS], 0)
    nc = _bacc.Bacc("TRN2", target_bir_lowering=False, num_devices=1)
    arrays, d = {}, {}
    for name, a in laid.items():
        arrays[f"in_{name}"] = a
        d[name] = nc.dram_tensor(f"in_{name}", a.shape, _mybir.dt.from_np(a.dtype), kind="ExternalInput").ap()
    out = nc.dram_tensor("out_0_dram", (B, S, D), F32, kind="ExternalOutput").ap()
    build(nc, d, out)
    r = _run(nc, [arrays], core_ids=[0])
    return r.results[0]["out_0_dram"]
```

```python
from contextlib import ExitStack

import numpy as np

import concourse.bass as bass
from concourse import mybir

F32 = mybir.dt.float32
F32R = mybir.dt.float32r
U8 = mybir.dt.uint8
ALU = mybir.AluOpType
ACT = mybir.ActivationFunctionType
AX = mybir.AxisListType

P = 128
B, S, D = 4, 256, 256
TOK = B * S
NT = TOK // P
NC = D // P
H0, K0 = 16, 128
PAIR = 2
NPAIR = H0 // PAIR
HW = PAIR * K0
FF = 1024
NF = FF // P
EPS0 = 1e-5
HALF = TOK // 2
BANK = 512

VECS = ['L0_xattn_ln1_scale', 'L0_xattn_ln1_offset', 'L0_xattn_ln2_scale', 'L0_xattn_ln2_offset',
        'L0_xattn_ln_mlp_scale', 'L0_xattn_ln_mlp_offset', 'L1_xattn_ln1_w', 'L1_xattn_ln1_b',
        'L1_xattn_ln2_w', 'L1_xattn_ln2_b', 'L1_xattn_maa_x', 'L1_xattn_maa_stack', 'L1_xattn_time_decay',
        'L1_xattn_faaaa', 'L1_xattn_gn_w', 'L1_xattn_gn_b', 'L1_xattn_ffn_maa_k', 'L1_xattn_ffn_maa_r',
        'L2_xattn_ln_gamma', 'L2_xattn_ln_beta', 'L3_xattn_bq']
VROWS = {}
for _n in VECS:
    VROWS[_n] = sum(5 if m == 'L1_xattn_maa_stack' else 1 for m in VECS[:VECS.index(_n)])
PREV = len(VECS) + 4
NV = PREV + 2 * B
HVECS = [f'L0_xattn_{n}{a}' for a in (1, 2) for n in ('bq', 'bk', 'bias_k', 'bias_v', 'bv')]
NHV = len(HVECS) * H0 + NF
ROWS = ['L0_xattn_bo1', 'L0_xattn_bo2', 'L0_xattn_b_fc2', 'L3_xattn_bo', 'L3_xattn_gamma', 'L3_xattn_beta']


class Chip:

    def __init__(self, nc, stack):
        self.nc = nc

        def sb(name, shape, dt=F32):
            return stack.enter_context(nc.sbuf_tensor(name, shape, dt))

        self.x = sb("x_rows", [P, NT, D])
        self.ctx = sb("ctx_rows", [P, NT, D])
        self.ident = sb("ident", [P, P])
        self.vecs = sb("vecs_T", [P, NC, NV])
        self.hvecs = sb("hvecs_T", [P, NHV])
        self.rows = sb("rows_bc", [P, len(ROWS), D])
        self.expo = sb("minus_half", [P, NT])
        self.psum = stack.enter_context(nc.psum_tensor("psum", [P, 8, BANK], F32))

        self.semaphores = []

    def semaphore(self, name):
        self.semaphores.append(self.nc.alloc_semaphore(name))
        return self.semaphores[-1]

    def renew_semaphores(self):
        self.nc.all_engine_barrier()
        self.nc.clear_and_free_semaphores(self.semaphores)
        self.nc.all_engine_barrier()
        self.semaphores = []

    def vec(self, name, c, i=0):
        r = VROWS[name] + i
        return self.vecs[:, c, r:r + 1]


def tiles_of(dram):
    return dram.rearrange("b (u p) d -> p (b u) d", p=P)


def stage_setup(chip, d, ctx_hi, ctx_lo, make_ln, prefetch):
    nc, ps = chip.nc, chip.psum
    with ExitStack() as st:
        sb = lambda n, s, t=F32: st.enter_context(nc.sbuf_tensor(n, s, t))
        sem = lambda n: chip.semaphore(n)
        vraw = sb("vecs_raw", [NV, D])
        hraw = sb("hvecs_raw", [NHV // 2, 2, K0])
        ld_ctx, ld_vec, ld_x, ld_rows = sem("ld_ctx"), sem("ld_vec"), sem("ld_x"), sem("ld_rows")
        ident_zero, ident_ok, turned, vec_turned, hi_done, lo_done, vec_done = (
            sem(n) for n in ("ident_zero", "ident_ok", "turned", "vec_turned", "ctx_hi_done", "ctx_lo_done", "vec_done"))
        ln = make_ln(st)
        with nc.Block() as block:
            @block.sync
            def _(sp):
                sp.dma_start(chip.x[:, :, :], tiles_of(d['x'])).then_inc(ld_x, 16)
                for j in range(2):
                    sp.dma_start(chip.ctx[:, j * 4:j * 4 + 4, :], tiles_of(d['ctx_2048'])[:, j * 4:j * 4 + 4, :]).then_inc(ld_ctx, 16)
                prefetch(sp)

            @block.scalar
            def _(act):
                act.dma_start(vraw[:, :], d['vecs']).then_inc(ld_vec, 16)
                act.dma_start(hraw[:, :, :], d['hvecs'].rearrange("(t r) k -> r t k", t=2)).then_inc(ld_vec, 16)
                act.dma_start(chip.rows[:, :, :].rearrange("p r d -> p (r d)"),
                              d['rows'].rearrange("(a n) -> a n", a=1).to_broadcast([P, len(ROWS) * D])).then_inc(ld_rows, 16)
                for n in range(4):
                    act.wait_ge(turned, n + 1)
                    act.activation(ctx_hi[:, n // 2, (n % 2) * HALF:(n % 2 + 1) * HALF], ps[:, n, :], ACT.Copy).then_inc(hi_done, 1)
                act.wait_ge(ld_rows, 16)
                act.wait_ge(vec_done, 1)
                ln.scalar(act)

            @block.gpsimd
            def _(pool):
                pool.memset(chip.expo[:, :], -0.5)
                pool.memset(chip.ident[:, :], 0.0).then_inc(ident_zero, 1)
                pool.wait_ge(ident_zero, 1)
                pool.affine_select(out=chip.ident[:, :], in_=chip.ident[:, :], compare_op=ALU.not_equal, fill=1.0,
                                   base=0, pattern=[[-1, P]], channel_multiplier=1).then_inc(ident_ok, 1)
                ln.gpsimd(pool)

            @block.tensor
            def _(pe):
                pe.wait_ge(ident_ok, 1)
                pe.wait_ge(ld_vec, 32)
                for c in range(NC):
                    pe.transpose(ps[:, 4, c * NV:(c + 1) * NV], vraw[:, c * P:(c + 1) * P], chip.ident[0:NV, 0:NV])
                R = NHV // 2
                for t in range(2):
                    mm = pe.transpose(ps[:, 5, t * R:(t + 1) * R], hraw[:, t, :], chip.ident[0:R, 0:R])
                mm.then_inc(vec_turned, 1)
                for n in range(4):
                    pe.wait_ge(ld_ctx, 32)
                    c, half = n // 2, n % 2
                    for t in range(4):
                        mm = pe.transpose(ps[:, n, t * P:(t + 1) * P], chip.ctx[:, half * 4 + t, c * P:(c + 1) * P], chip.ident[:, :])
                    mm.then_inc(turned, 1)
                pe.wait_ge(lo_done, 4)
                ln.tensor(pe)

            @block.vector
            def _(dve):
                dve.wait_ge(ld_x, 16)
                ln.statistics(dve, 0)
                ln.statistics(dve, 1)
                dve.wait_ge(vec_turned, 1)
                dve.tensor_copy(chip.hvecs[:, :], ps[:, 5, 0:NHV])
                dve.tensor_copy(chip.vecs[:, :, :], ps[:, 4, 0:NC * NV].rearrange("p (c v) -> p c v", c=NC)).then_inc(vec_done, 1)
                for n in range(4):
                    dve.wait_ge(hi_done, n + 1)
                    sl = slice((n % 2) * HALF, (n % 2 + 1) * HALF)
                    dve.tensor_tensor(ctx_lo[:, n // 2, sl], ps[:, n, :], ctx_hi[:, n // 2, sl].bitcast(F32), ALU.subtract).then_inc(lo_done, 1)
                ln.normalise(dve, 0)
                ln.normalise(dve, 1)
                ln.cut(dve)


class LayerNorm:

    def __init__(self, chip, stack, tag, rows, scale_of, offset_of, eps, hi=None, lo=None, plain=None, bank=0, room=None):
        sb = lambda n, s: stack.enter_context(chip.nc.sbuf_tensor(f"{tag}_{n}", s, F32))
        self.tag, self.chip, self.rows, self.scale_of, self.offset_of, self.eps = tag, chip, rows, scale_of, offset_of, float(eps)
        self.hi, self.lo, self.plain, self.bank, self.ready = hi, lo, plain, bank, None
        self.xn, self.full = room if room else (sb("normed", [P, NT, D]), sb("full", [P, 4, BANK]) if hi is not None else None)
        self.bn, self.mv, self.ve, self.rstd = sb("bn", [P, NT, 6]), sb("mean_var", [P, NT, 2]), sb("var_eps", [P, NT]), sb("rstd", [P, NT])
        self.stats, self.aggr, self.var_ok, self.rstd_ok, self.normed, self.turned, self.full_ok, self.hi_ok = (
            chip.semaphore(f"{tag}_{n}") for n in ("stats", "aggr", "var_ok", "rstd_ok", "normed", "turned", "full_ok", "hi_ok"))

    def piece(self, t, n):
        return t[:, n % 2, (n // 2) * HALF:(n // 2 + 1) * HALF]

    def gpsimd(self, pool):
        for h in range(2):
            four = slice(4 * h, 4 * h + 4)
            pool.wait_ge(self.var_ok, h + 1)
            pool.tensor_tensor(self.rstd[:, four], self.ve[:, four], self.chip.expo[:, four], ALU.pow).then_inc(self.rstd_ok, 1)
        if self.hi is not None:
            for n in (0, 2):
                pool.wait_ge(self.hi_ok, n + 1)
                pool.tensor_tensor(self.piece(self.lo, n), self.full[:, n, :], self.piece(self.hi, n).bitcast(F32), ALU.subtract)

    def statistics(self, dve, h):
        if self.ready:
            dve.wait_ge(self.ready[0], self.ready[1] + 2 * h + 2)
        for j in range(4 * h, 4 * h + 4):
            dve.bn_stats(self.bn[:, j, :], self.rows[:, j, :]).then_inc(self.stats, 1)
        for j in range(4 * h, 4 * h + 4):
            dve.wait_ge(self.stats, j + 1)
            dve.bn_aggr(self.mv[:, j, :], self.bn[:, j, :]).then_inc(self.aggr, 1)
        dve.wait_ge(self.aggr, 4 * h + 4)
        dve.tensor_scalar(self.ve[:, 4 * h:4 * h + 4], self.mv[:, 4 * h:4 * h + 4, 1], self.eps, None, ALU.add).then_inc(self.var_ok, 1)

    def normalise(self, dve, h):
        dve.wait_ge(self.rstd_ok, h + 1)
        for j in range(4 * h, 4 * h + 4):
            dve.tensor_scalar(self.xn[:, j, :], self.rows[:, j, :], self.mv[:, j, 0:1], self.rstd[:, j:j + 1], ALU.subtract, ALU.mult).then_inc(self.normed, 1)

    def cut(self, dve):
        for n in range(4 if self.hi is not None else 0):
            dve.wait_ge(self.full_ok, n + 1)
            dve.tensor_copy(self.piece(self.hi, n), self.full[:, n, :]).then_inc(self.hi_ok, 1)
            if n % 2:
                dve.wait_ge(self.hi_ok, n + 1)
                dve.tensor_tensor(self.piece(self.lo, n), self.full[:, n, :], self.piece(self.hi, n).bitcast(F32), ALU.subtract)

    def after_rows(self, dve, m):
        if m == 1:
            self.statistics(dve, 0)
        if m == 2:
            self.normalise(dve, 0)
        if m == 3:
            self.statistics(dve, 1)
            self.normalise(dve, 1)
            self.cut(dve)

    def tensor(self, pe):
        for n in range(4):
            half, c = n // 2, n % 2
            pe.wait_ge(self.normed, half * 4 + 4)
            for t in range(4):
                mm = pe.transpose(self.chip.psum[:, self.bank + n, t * P:(t + 1) * P], self.xn[:, half * 4 + t, c * P:(c + 1) * P], self.chip.ident[:, :])
            mm.then_inc(self.turned, 1)

    def scalar(self, act):
        for n in range(4):
            half, c = n // 2, n % 2
            src = self.chip.psum[:, self.bank + n, :]
            act.wait_ge(self.turned, n + 1)
            if self.hi is not None:
                act.activation(self.full[:, n, :], src, ACT.Identity, scale=self.scale_of(c), bias=self.offset_of(c)).then_inc(self.full_ok, 1)
            else:
                act.activation(self.plain(c, half), src.rearrange("p (b s) -> p b s", b=2), ACT.Identity, scale=self.scale_of(c), bias=self.offset_of(c))


def run_layernorm(chip, ln, prefetch, turns=(), vector_then=None, scalar_then=None):
    ps = chip.psum
    t_full, t_read = chip.semaphore(f"{ln.tag}_also_turned"), chip.semaphore(f"{ln.tag}_also_read")
    jobs = [(rows, out, n) for rows, out in turns for n in range(4)]
    bank = lambda k: ps[:, (4 + k) % 8, :]
    with chip.nc.Block() as block:
        block.sync(prefetch)
        block.gpsimd(ln.gpsimd)

        @block.tensor
        def _(pe):
            for k, (rows, _out, n) in enumerate(jobs):
                for t in range(4):
                    mm = pe.transpose(bank(k)[:, t * P:(t + 1) * P], rows[:, (n % 2) * 4 + t, (n // 2) * P:(n // 2 + 1) * P], chip.ident[:, :])
                mm.then_inc(t_full, 1)
            if jobs:
                pe.wait_ge(t_read, len(jobs))
            ln.tensor(pe)

        @block.scalar
        def _(act):
            for k, (_rows, out, n) in enumerate(jobs):
                act.wait_ge(t_full, k + 1)
                act.activation(out[:, n // 2, (n % 2) * HALF:(n % 2 + 1) * HALF], bank(k), ACT.Copy).then_inc(t_read, 1)
            ln.scalar(act)
            if scalar_then:
                scalar_then(act)

        @block.vector
        def _(dve):
            ln.statistics(dve, 0)
            ln.statistics(dve, 1)
            ln.normalise(dve, 0)
            ln.normalise(dve, 1)
            ln.cut(dve)
            if vector_then:
                vector_then(dve)


def attention_room(chip, stack):
    sb = lambda n, s: stack.enter_context(chip.nc.sbuf_tensor(n, s, F32))
    raw = {n: sb(f"w{n}_raw", [P, NC, HW]) for n in 'qkv'}
    raw['o'] = sb("wo_raw", [P, H0, D])
    return raw


def attention_weights(chip, d, a, raw):
    L = "L0_xattn_"
    w = {n: d[f"{L}w{n}{a}"].rearrange("(c p) n -> p c n", p=P) for n in 'qkv'}
    ld = {n: chip.semaphore(f"a{a}_ld_w{n}") for n in 'qkvo'}

    def load(sp):
        for n in 'qkv':
            sp.dma_start(raw[n][:, :, :], w[n][:, :, 0:HW]).then_inc(ld[n], 16)
        sp.dma_start(raw['o'][:, :, :], d[f"{L}wo{a}"].rearrange("(h k) n -> k h n", k=K0)).then_inc(ld['o'], 16)

    return w, ld, load


def stage_cross_attention(chip, a, raw, weights, h_hi, h_lo, ctx_hi, ctx_lo, make_ln, prefetch):
    nc, ps = chip.nc, chip.psum
    C = float(K0) ** -0.5
    at = (a - 1) * 5 * H0
    W3, ld, _load = weights
    wo_raw, ld_q, ld_k, ld_v, ld_o = raw['o'], ld['q'], ld['k'], ld['v'], ld['o']
    with ExitStack() as st:
        sb = lambda n, s, t=F32: st.enter_context(nc.sbuf_tensor(f"a{a}_{n}", s, t))
        sem = lambda n: chip.semaphore(f"a{a}_{n}")
        whi = {n: sb(f"w{n}_hi", [P, NC, HW], F32R) for n in 'qkvo'}
        wlo = {n: sb(f"w{n}_lo", [P, NC, HW], F32R) for n in 'qkvo'}
        qk_hi = {n: sb(f"{n}_hi", [P, PAIR, TOK], F32R) for n in 'qc'}
        qk_lo = {n: sb(f"{n}_lo", [P, PAIR, TOK], F32R) for n in 'qc'}
        E_LATE, M_LATE, I_LATE = 2, 1, 3
        KW = S + 2
        k_hi = sb("k_hi", [P, PAIR, B, KW], F32R)
        k_lo = sb("k_lo", [P, PAIR, B, KW], F32R)
        v_hi = sb("v_hi", [P, NT, HW], F32R)
        v_lo = sb("v_lo", [P, NT, HW], F32R)
        prob = sb("prob", [P, 4, 2, KW])
        negm = sb("neg_max", [P, 4, 2])
        tot = sb("total", [P, 4, 2])
        rtot = sb("inv_total", [P, 4, 2])
        pt_hi = sb("probT_hi", [P, 4, BANK], F32R)
        pt_lo = sb("probT_lo", [P, 4, BANK], F32R)
        one = sb("ones", [P, 2])
        pb = sb("prob_bias", [P, NT, NPAIR, PAIR])
        bcol = sb("bias_cols", [P, 3, NPAIR, PAIR])
        qk_cols = sb("qk_cols", [P, 2, PAIR])
        v_cols = sb("v_cols", [P, PAIR])
        wo_pair = sb("wo_pair", [P, PAIR, D])
        kb_hi = sb("bias_k_hi", [P, NPAIR, PAIR], F32R)
        kb_lo = sb("bias_k_lo", [P, NPAIR, PAIR], F32R)
        dvm = sb("bias_v_diag", [P, H0, H0])
        bvo = sb("bias_out", [33, D])
        pb_T = sb("prob_bias_T", [33, TOK])

        (q_split, k_split, v_split, o_split, rounded, q_rounded, cols_ok, cols_cur, ld_op, kcols,
         acc_full, acc_hi, acc_free, s_done, s_max, s_exp, s_sum, s_norm, t_done, t_hi, t_free, bias_full, bias_read, dv_ok) = (
            sem(n) for n in ("wq_split", "wk_split", "wv_split", "wo_split",
                             "w_rounded", "wq_rounded", "cols_ok", "cols_cur", "ld_wo_pair", "bias_k_cols",
                             "acc_full", "acc_hi", "acc_free", "scores_done", "max_done", "exp_done", "inv_done",
                             "norm_done", "turned", "turned_hi", "turned_free", "bias_full", "bias_read", "bias_v_ok"))
        split = {'q': q_split, 'k': k_split, 'v': v_split}
        hv = lambda k: chip.hvecs[:, at + k * H0:at + (k + 1) * H0]

        PRE = ['Q0', 'Q1', 'K0', 'K1', 'Q2', 'Q3', 'K2', 'K3']
        STEP = ("S0 S1 O0 O1 S2 O2 O3 V0 T0 V1 S3 V2 T1 S4 V3 Q0 T2 S5 Q1 K0 T3 S6 K1 A0 T4 A1 "
                "S7 T5 Q2 Q3 T6 K2 T7 K3 A2 A3").split()
        FIRST = [s for s in STEP if s[0] != 'O']
        LAST = [s for s in STEP if s[0] not in 'QK']
        TAIL = ['O0', 'O1', 'O2', 'O3']
        HIS = 16
        USES = HIS + 4
        base_of = lambda i: len(PRE) if isinstance(i, int) and i == 0 else i * USES + len(PRE) - 4
        END = base_of(NPAIR - 1) + 12 + 4
        use_of = lambda order, s: [x for x in order if x[0] in 'VAQKO'].index(s)
        ln = make_ln(st, bank=4, room=(prob[:, :, :, :].rearrange("p u q k -> p (u q k)")[:, 0:NT * D].rearrange("p (t n) -> p t n", t=NT),
                                       sb("ln_full", [P, 4, BANK])))
        ln.ready = (acc_free, END - 4)
        acc = lambda n: ps[:, n % 2, :]
        s_bank = lambda u: ps[:, 2 + 2 * (u % 2):4 + 2 * (u % 2), 0:KW]
        t_bank = lambda u: ps[:, 6 + u % 2, :]
        U = 2 * B

        def three(pe, out, l_hi, l_lo, r_hi, r_lo, first, last):
            pe.matmul(out, l_hi, r_hi, start=first, stop=False)
            pe.matmul(out, l_hi, r_lo, start=False, stop=False)
            return pe.matmul(out, l_lo, r_hi, start=False, stop=last)

        def steps(eng, body):
            body(0, FIRST)
            with eng.Fori(1, NPAIR - 1) as i:
                body(i, STEP)
            body(NPAIR - 1, LAST)
            body(NPAIR, TAIL)

        def project_out(s, h_dst, half):
            if s[0] == 'Q':
                cols = slice(half * HALF, (half + 1) * HALF)
                return qk_hi['q'][:, h_dst, cols], qk_lo['q'][:, h_dst, cols]
            return k_hi[:, h_dst, 2 * half:2 * half + 2, 0:S], k_lo[:, h_dst, 2 * half:2 * half + 2, 0:S]

        def like(s, view):
            return view.rearrange("p (b s) -> p b s", b=2) if s[0] == 'K' else view

        def later(order, what, steps):
            out, held = [], []
            for s in order:
                out.append(s)
                held = [(t, n - 1) for t, n in held]
                out += [t for t, n in held if n == 0]
                held = [(t, n) for t, n in held if n > 0]
                if s[0] == 'S':
                    held.append((what + s[1], steps))
            return out + [t for t, n in held]

        def act_order(order):
            out = [s for s in later(order, 'E', E_LATE) if s[0] in 'EVATQK' or s == 'S2']
            return [('R0' if s == 'S2' else s) for s in out]

        def dve_order(order):
            out = []
            for s in later(later(order, 'M', M_LATE), 'I', I_LATE):
                if s == 'S2':
                    out.append('R0')
                elif s[0] != 'S':
                    out.append(s)
            return out

        with nc.Block() as block:
            @block.sync
            def _(sp):
                sp.wait_ge(ld_o, 16)
                sp.dma_start(wo_pair[:, :, :], wo_raw[:, 0:PAIR, :]).then_inc(ld_op, 16)
                with sp.Fori(1, NPAIR) as i:
                    for n in 'qkv':
                        sp.wait_ge(split[n], i)
                        sp.dma_start(raw[n][:, :, :], W3[n][:, :, bass.ds(i * HW, HW)]).then_inc(ld[n], 16)
                    sp.wait_ge(o_split, i)
                    sp.dma_start(wo_pair[:, :, :], wo_raw[:, bass.ds(i * PAIR, PAIR), :]).then_inc(ld_op, 16)
                for n in 'qkv':
                    sp.wait_ge(split[n], NPAIR)
                sp.wait_ge(ld_op, 16 * NPAIR)
                prefetch(sp)

            @block.gpsimd
            def _(pool):
                ones = one[:, 0:1].to_broadcast([P, NC, HW])

                def cut(src, n, count, done):
                    pool.tensor_tensor(whi[n][:, :, :], src, ones, ALU.mult).then_inc(rounded, 1)
                    pool.wait_ge(rounded, count + 1)
                    pool.tensor_tensor(wlo[n][:, :, :], src, whi[n][:, :, :].bitcast(F32), ALU.subtract).then_inc(done, 1)

                pool.memset(one[:, :], 1.0).then_inc(rounded, 1)
                pool.wait_ge(rounded, 1)
                pool.wait_ge(ld_k, 16)
                cut(raw['k'][:, :, :], 'k', 1, k_split)
                pool.wait_ge(ld_v, 16)
                cut(raw['v'][:, :, :], 'v', 2, v_split)

                def body(i, order):
                    last = order is LAST

                    def norm(u):
                        h, b = u // B, u % B
                        pool.wait_ge(s_sum, i * U + u + 1)
                        pool.tensor_tensor(prob[:, u % 4, :, 0:S], prob[:, u % 4, :, 0:S],
                                           rtot[:, u % 4, :].unsqueeze(2).to_broadcast([P, 2, S]), ALU.mult)
                        pool.tensor_tensor(pb[:, 2 * b:2 * b + 2, i, h:h + 1], prob[:, u % 4, :, S:S + 1], rtot[:, u % 4, :].unsqueeze(2), ALU.mult).then_inc(s_norm, 1)

                    if order is TAIL:
                        return
                    norm(0)
                    norm(1)
                    if order is not FIRST:
                        pool.wait_ge(acc_full, base_of(i) + 4)
                    pool.wait_ge(ld_op, i * 16 + 16)
                    cut(wo_pair[:, :, :], 'o', i * 3 + 3, o_split)
                    norm(2)
                    if not last:
                        pool.wait_ge(ld_k, i * 16 + 32)
                        cut(raw['k'][:, :, :], 'k', i * 3 + 4, k_split)
                    for u in range(3, U):
                        norm(u)
                        if u == U - 2 and not last:
                            pool.wait_ge(ld_v, i * 16 + 32)
                            cut(raw['v'][:, :, :], 'v', i * 3 + 5, v_split)

                steps(pool, body)
                ln.gpsimd(pool)

            @block.tensor
            def _(pe):
                pe.sem_inc(t_done, 4)

                def project(s, i, n, total):
                    w, h, half = s[0].lower(), int(s[1]) // 2, int(s[1]) % 2
                    for c in range(NC):
                        cols = slice(half * HALF, (half + 1) * HALF)
                        rh, rl = (h_hi, h_lo) if w == 'q' else (ctx_hi, ctx_lo)
                        mm = three(pe, acc(n), whi[w][:, c, h * K0:(h + 1) * K0], wlo[w][:, c, h * K0:(h + 1) * K0],
                                   rh[:, c, cols], rl[:, c, cols], c == 0, c == NC - 1)
                    mm.then_inc(acc_full, 1)

                pe.wait_ge(q_split, 1)
                for n, s in enumerate(PRE):
                    if s == 'K0':
                        pe.wait_ge(k_split, 1)
                    if n >= 2:
                        pe.wait_ge(acc_free, n - 1)
                    project(s, 0, n, n)
                    if n == 1:
                        pe.wait_ge(ld_o, 16)
                        pe.wait_ge(dv_ok, 2)
                    if n:
                        for h in range(3 * (n - 1), min(3 * n, H0)):
                            mm = pe.matmul(ps[0:H0, 7, 0:D], dvm[:, h, :], wo_raw[:, h, :], start=h == 0, stop=h == H0 - 1)
                            if h == H0 - 1:
                                mm.then_inc(bias_full, 1)

                def bias_token():
                    pe.wait_ge(s_exp, 2 * U * NPAIR + 4)
                    pe.wait_ge(s_norm, U * NPAIR)
                    for j in range(NT):
                        mm = pe.transpose(ps[0:H0, 4 + j // 4, (j % 4) * P:(j % 4 + 1) * P], pb[:, j, :, :].rearrange("p i h -> p (i h)"), chip.ident[:, :])
                    mm.then_inc(bias_full, 1)

                def body(i, order):
                    base = base_of(i) if order is not TAIL else END - 4
                    if order is TAIL:
                        bias_token()
                    for s in order:
                        k, m = s[0], int(s[1])
                        if k in 'VAQKO':
                            n = use_of(order, s)
                            pe.wait_ge(acc_free, base + n - 1)
                        if k in 'QK':
                            if s in ('Q0', 'K0'):
                                pe.wait_ge(split[k.lower()], i + 2)
                            project(s, i, n, base + n)
                        if k == 'V':
                            if m == 0:
                                pe.wait_ge(v_split, i + 1)
                            for j in range(2):
                                t = 2 * m + j
                                for c in range(NC):
                                    mm = three(pe, acc(n)[:, j * HW:(j + 1) * HW], ctx_hi[:, c, t * P:(t + 1) * P], ctx_lo[:, c, t * P:(t + 1) * P],
                                               whi['v'][:, c, :], wlo['v'][:, c, :], c == 0, c == NC - 1)
                            mm.then_inc(acc_full, 1)
                        if k == 'S':
                            h, b = m // B, m % B
                            if m == 0:
                                if order is FIRST:
                                    pe.wait_ge(acc_free, PRE.index('K1') + 1)
                                else:
                                    pe.wait_ge(acc_free, base - USES + use_of(STEP, 'K1') + 1)
                                pe.wait_ge(kcols, i + 1)
                            pe.wait_ge(s_exp, 2 * (i * U + m) + 2)
                            for q in range(2):
                                cols = slice(b * S + q * P, b * S + (q + 1) * P)
                                mm = three(pe, s_bank(m)[:, q, :], qk_hi['q'][:, h, cols], qk_lo['q'][:, h, cols],
                                           k_hi[:, h, b, :], k_lo[:, h, b, :], True, True)
                            mm.then_inc(s_done, 1)
                        if k == 'T':
                            pe.wait_ge(s_norm, i * U + m + 1)
                            pe.wait_ge(t_free, i * U + m + 1)
                            for t in range(2):
                                for q in range(2):
                                    mm = pe.transpose(t_bank(m)[:, t * S + q * P:t * S + (q + 1) * P], prob[:, m % 4, q, t * P:(t + 1) * P], chip.ident[:, :])
                            mm.then_inc(t_done, 1)
                        if k == 'A':
                            pe.wait_ge(t_free, i * U + 2 * m + 4)
                            if m == 0:
                                pe.wait_ge(acc_free, base + use_of(order, 'V3') + 1)
                            for u in (2 * m, 2 * m + 1):
                                h, b = u // B, u % B
                                for t in range(2):
                                    mm = three(pe, acc(n)[:, (u % 2) * S:(u % 2 + 1) * S], v_hi[:, 2 * b + t, h * K0:(h + 1) * K0], v_lo[:, 2 * b + t, h * K0:(h + 1) * K0],
                                               pt_hi[:, u % 4, t * S:(t + 1) * S], pt_lo[:, u % 4, t * S:(t + 1) * S], t == 0, t == 1)
                            mm.then_inc(acc_full, 1)
                        if k == 'O':
                            if m == 0:
                                pe.wait_ge(o_split, i)
                                pe.wait_ge(acc_free, base)
                            for j in range(2):
                                t = 2 * m + j
                                for h in range(PAIR):
                                    mm = three(pe, acc(n)[:, j * D:(j + 1) * D], qk_hi['c'][:, h, t * P:(t + 1) * P], qk_lo['c'][:, h, t * P:(t + 1) * P],
                                               whi['o'][:, h, :], wlo['o'][:, h, :], h == 0, h == PAIR - 1 and order is not TAIL)
                                if order is TAIL:
                                    pe.wait_ge(bias_read, 1)
                                    mm = pe.matmul(acc(n)[:, j * D:(j + 1) * D], pb_T[:, t * P:(t + 1) * P], bvo[:, :], start=False, stop=True)
                            mm.then_inc(acc_full, 1)

                steps(pe, body)
                ln.tensor(pe)

            @block.scalar
            def _(act):
                act.sem_inc(s_exp, 4)
                act.wait_ge(ld_q, 16)
                act.activation(whi['q'][:, :, :], raw['q'][:, :, :], ACT.Copy, scale=C).then_inc(q_rounded, 1)
                act.wait_ge(cols_cur, 1)

                def qk(s, n, i, count):
                    h, half = int(s[1]) // 2, int(s[1]) % 2
                    act.wait_ge(acc_full, count + 1)
                    act.activation(project_out(s, h, half)[0], like(s, acc(n)), ACT.Identity,
                                   bias=qk_cols[:, 0 if s[0] == 'Q' else 1, h:h + 1]).then_inc(acc_hi, 1)

                for n, s in enumerate(PRE):
                    qk(s, n, 0, n)

                def body(i, order):
                    last = order is LAST
                    base = base_of(i) if order is not TAIL else END - 4
                    for s in act_order(order):
                        k, m = s[0], int(s[1])
                        if k == 'E':
                            act.wait_ge(s_max, i * U + m + 1)
                            act.wait_ge(t_done, i * U + m + 1)
                            for q in range(2):
                                act.activation(prob[:, m % 4, q, 0:S + 1], s_bank(m)[:, q, 0:S + 1], ACT.Exp,
                                               bias=negm[:, m % 4, q:q + 1], accum_out=tot[:, m % 4, q:q + 1]).then_inc(s_exp, 1)
                        elif k == 'T':
                            act.wait_ge(t_done, i * U + m + 5)
                            act.activation(pt_hi[:, m % 4, :], t_bank(m), ACT.Copy).then_inc(t_hi, 1)
                        elif k == 'R':
                            if not last:
                                act.wait_ge(ld_q, i * 16 + 32)
                                act.activation(whi['q'][:, :, :], raw['q'][:, :, :], ACT.Copy, scale=C).then_inc(q_rounded, 1)
                        elif k in 'QK':
                            if s == 'Q0':
                                act.wait_ge(cols_cur, 2 * i + 3)
                            qk(s, use_of(order, s), i + 1, base + use_of(order, s))
                        elif k in 'VA':
                            n = use_of(order, s)
                            act.wait_ge(acc_full, base + n + 1)
                            if s == 'A0':
                                act.wait_ge(cols_cur, 2 * i + 2)
                            if k == 'V':
                                act.activation(v_hi[:, 2 * m:2 * m + 2, :], acc(n).rearrange("p (j n) -> p j n", j=2), ACT.Copy).then_inc(acc_hi, 1)
                            else:
                                act.activation(qk_hi['c'][:, m // 2, (m % 2) * HALF:(m % 2 + 1) * HALF], acc(n), ACT.Identity,
                                               bias=v_cols[:, m // 2:m // 2 + 1]).then_inc(acc_hi, 1)

                steps(act, body)
                ln.scalar(act)

            @block.vector
            def _(dve):
                dve.sem_inc(t_free, 1)
                dve.wait_ge(q_rounded, 1)
                dve.scalar_tensor_tensor(wlo['q'][:, :, :], raw['q'][:, :, :], C, whi['q'][:, :, :].bitcast(F32), ALU.mult, ALU.subtract).then_inc(q_split, 1)
                dve.tensor_scalar(bcol[:, 0, :, :], hv(0).rearrange("p (i h) -> p i h", h=PAIR), C, None, ALU.mult)
                dve.tensor_copy(bcol[:, 1, :, :], hv(1).rearrange("p (i h) -> p i h", h=PAIR))
                dve.tensor_copy(bcol[:, 2, :, :], hv(4).rearrange("p (i h) -> p i h", h=PAIR))
                dve.memset(k_hi[:, :, :, S:KW].bitcast(F32), 0.0)
                dve.memset(k_lo[:, :, :, S:KW].bitcast(F32), 0.0)
                dve.tensor_copy(kb_hi[:, :, :], hv(2).rearrange("p (i h) -> p i h", h=PAIR)).then_inc(cols_ok, 1)
                dve.wait_ge(cols_ok, 1)
                dve.tensor_tensor(kb_lo[:, :, :], hv(2).rearrange("p (i h) -> p i h", h=PAIR), kb_hi[:, :, :].bitcast(F32), ALU.subtract).then_inc(cols_ok, 1)
                dve.wait_ge(cols_ok, 2)
                dve.tensor_copy(qk_cols[:, :, :], bcol[:, 0:2, 0, :]).then_inc(cols_cur, 1)
                dve.wait_ge(cols_cur, 1)
                dve.memset(dvm[:, :, :], 0.0).then_inc(dv_ok, 1)
                dve.wait_ge(dv_ok, 1)
                dve.tensor_tensor(dvm[:, :, :].rearrange("p a b -> p (a b)")[:, 0:H0 * H0:H0 + 1], hv(3), hv(4), ALU.subtract).then_inc(dv_ok, 1)

                def qk(s, n, i, count):
                    h, half = int(s[1]) // 2, int(s[1]) % 2
                    hi, lo = project_out(s, h, half)
                    dve.wait_ge(acc_hi, count + 1)
                    dve.scalar_tensor_tensor(lo, like(s, acc(n)), qk_cols[:, 0 if s[0] == 'Q' else 1, h:h + 1],
                                             hi.bitcast(F32), ALU.add, ALU.subtract).then_inc(acc_free, 1)

                def key_cols(i):
                    for dst, src in ((k_hi, kb_hi), (k_lo, kb_lo)):
                        ins = dve.tensor_copy(dst[:, :, :, S:S + 1], src[:, i, :].bitcast(F32).unsqueeze(2).unsqueeze(3).to_broadcast([P, PAIR, B, 1]))
                    ins.then_inc(kcols, 1)

                for n, s in enumerate(PRE):
                    qk(s, n, 0, n)
                key_cols(0)
                dve.memset(bvo[0:32, :], 0.0).then_inc(dv_ok, 1)
                dve.memset(pb_T[0:32, :], 0.0).then_inc(dv_ok, 1)
                dve.memset(pb_T[32:33, :], 1.0)
                r = ROWS.index(f"L0_xattn_bo{a}")
                dve.tensor_copy(bvo[32:33, :], chip.rows[32:33, r, :])
                dve.wait_ge(dv_ok, 4)
                dve.wait_ge(bias_full, 1)
                dve.tensor_copy(bvo[0:H0, :], ps[0:H0, 7, 0:D]).then_inc(t_free, 1)

                def body(i, order):
                    last = order is LAST
                    base = base_of(i) if order is not TAIL else END - 4
                    hi_base = i * HIS + len(PRE)
                    if order is TAIL:
                        dve.wait_ge(bias_full, 2)
                        dve.tensor_copy(pb_T[0:H0, :], ps[0:H0, 4:6, :].rearrange("p b n -> p (b n)")).then_inc(bias_read, 1)
                    his = [s for s in order if s[0] in 'VAQK']
                    for s in dve_order(order):
                        k, m = s[0], int(s[1])
                        if k == 'M':
                            dve.wait_ge(s_done, i * U + m + 1)
                            dve.tensor_reduce(negm[:, m % 4, :], s_bank(m)[:, :, 0:S + 1], AX.X, ALU.max, negate=True).then_inc(s_max, 1)
                        elif k == 'I':
                            dve.wait_ge(s_exp, 2 * (i * U + m) + 6)
                            dve.reciprocal(rtot[:, m % 4, :], tot[:, m % 4, :]).then_inc(s_sum, 1)
                        elif k == 'T':
                            dve.wait_ge(t_hi, i * U + m + 1)
                            dve.tensor_tensor(pt_lo[:, m % 4, :], t_bank(m), pt_hi[:, m % 4, :].bitcast(F32), ALU.subtract).then_inc(t_free, 1)
                        elif k == 'R':
                            dve.wait_ge(acc_free, base)
                            dve.tensor_copy(v_cols[:, :], bcol[:, 2, i, :]).then_inc(cols_cur, 1)
                            if not last:
                                dve.tensor_copy(qk_cols[:, :, :], bcol[:, 0:2, i + 1, :]).then_inc(cols_cur, 1)
                                dve.wait_ge(q_rounded, i + 2)
                                dve.scalar_tensor_tensor(wlo['q'][:, :, :], raw['q'][:, :, :], C, whi['q'][:, :, :].bitcast(F32),
                                                         ALU.mult, ALU.subtract).then_inc(q_split, 1)
                        elif k in 'QK':
                            if s == 'Q0':
                                dve.wait_ge(cols_cur, 2 * i + 3)
                            qk(s, use_of(order, s), i + 1, hi_base + his.index(s))
                            if s == 'K3':
                                key_cols(i + 1)
                        elif k == 'V':
                            dve.wait_ge(acc_hi, hi_base + his.index(s) + 1)
                            dve.tensor_tensor(v_lo[:, 2 * m:2 * m + 2, :], acc(use_of(order, s)).rearrange("p (j n) -> p j n", j=2),
                                              v_hi[:, 2 * m:2 * m + 2, :].bitcast(F32), ALU.subtract).then_inc(acc_free, 1)
                        elif k == 'A':
                            dve.wait_ge(acc_hi, hi_base + his.index(s) + 1)
                            cols = slice((m % 2) * HALF, (m % 2 + 1) * HALF)
                            dve.scalar_tensor_tensor(qk_lo['c'][:, m // 2, cols], acc(use_of(order, s)), v_cols[:, m // 2:m // 2 + 1],
                                                     qk_hi['c'][:, m // 2, cols].bitcast(F32), ALU.add, ALU.subtract).then_inc(acc_free, 1)
                        elif k == 'O':
                            n = use_of(order, s)
                            dve.wait_ge(acc_full, base + n + 1)
                            dve.tensor_tensor(chip.x[:, 2 * m:2 * m + 2, :], chip.x[:, 2 * m:2 * m + 2, :],
                                              acc(n).rearrange("p (j n) -> p j n", j=2), ALU.add).then_inc(acc_free, 1)
                            if order is TAIL:
                                ln.after_rows(dve, m)

                steps(dve, body)


def stage_mlp(chip, w1_raw, w2_raw, ld_w, h_hi, h_lo):
    nc, ps = chip.nc, chip.psum
    bias1 = lambda f: chip.hvecs[:, len(HVECS) * H0 + f:len(HVECS) * H0 + f + 1]
    with ExitStack() as st:
        sb = lambda n, s, t=F32R: st.enter_context(nc.sbuf_tensor(f"mlp_{n}", s, t))
        sem = lambda n: chip.semaphore(f"mlp_{n}")
        w1_hi, w1_lo = sb("w1_hi", [P, NC, FF]), sb("w1_lo", [P, NC, FF])
        w2_hi, w2_lo = sb("w2_hi", [P, NF, D]), sb("w2_lo", [P, NF, D])
        u = sb("u", [P, 4, BANK], F32)
        u_hi, u_lo = sb("u_hi", [P, NF, TOK]), sb("u_lo", [P, NF, TOK])
        w_hi_ok, w1_ok, w2_hi_ok, w2_ok, full, gelu, u_hi_ok, u_ok, out_full, b2_ok = (
            sem(n) for n in ("w1_hi_ok", "w1_ok", "w2_hi_ok", "w2_ok", "full", "gelu", "u_hi_ok", "u_ok", "out_full", "b2_ok"))
        part = lambda f: slice(f * P, (f + 1) * P)
        half = lambda n: slice((n % 2) * HALF, (n % 2 + 1) * HALF)
        NU = 2 * NF
        with nc.Block() as block:
            @block.scalar
            def _(act):
                act.wait_ge(ld_w, 32)
                for q in range(4):
                    act.activation(w1_hi[:, :, q * 256:(q + 1) * 256], w1_raw[:, :, q * 256:(q + 1) * 256], ACT.Copy).then_inc(w_hi_ok, 1)
                for n in range(NU):
                    act.wait_ge(full, n + 1)
                    if n >= 4:
                        act.wait_ge(u_ok, n - 3)
                    act.activation(u[:, n % 4, :], ps[:, n % 4, :], ACT.Gelu, bias=bias1(n // 2)).then_inc(gelu, 1)

            @block.gpsimd
            def _(pool):
                pool.wait_ge(ld_w, 32)
                for q in range(4):
                    pool.wait_ge(w2_hi_ok, q + 1)
                    pool.tensor_tensor(w2_lo[:, 2 * q:2 * q + 2, :], w2_raw[:, 2 * q:2 * q + 2, :],
                                       w2_hi[:, 2 * q:2 * q + 2, :].bitcast(F32), ALU.subtract).then_inc(w2_ok, 1)
                r = ROWS.index('L0_xattn_b_fc2')
                pool.tensor_tensor(chip.x[:, :, :], chip.x[:, :, :], chip.rows[:, r:r + 1, :].to_broadcast([P, NT, D]), ALU.add).then_inc(b2_ok, 1)

            @block.vector
            def _(dve):
                dve.wait_ge(ld_w, 32)
                for q in range(4):
                    dve.wait_ge(w_hi_ok, q + 1)
                    cols = slice(q * 256, (q + 1) * 256)
                    dve.tensor_tensor(w1_lo[:, :, cols], w1_raw[:, :, cols], w1_hi[:, :, cols].bitcast(F32), ALU.subtract).then_inc(w1_ok, 1)
                for q in range(4):
                    dve.tensor_copy(w2_hi[:, 2 * q:2 * q + 2, :], w2_raw[:, 2 * q:2 * q + 2, :]).then_inc(w2_hi_ok, 1)
                for n in range(NU):
                    dve.wait_ge(gelu, n + 1)
                    dve.tensor_copy(u_hi[:, n // 2, half(n)], u[:, n % 4, :]).then_inc(u_hi_ok, 1)
                    dve.wait_ge(u_hi_ok, n + 1)
                    dve.tensor_tensor(u_lo[:, n // 2, half(n)], u[:, n % 4, :], u_hi[:, n // 2, half(n)].bitcast(F32), ALU.subtract).then_inc(u_ok, 1)
                dve.wait_ge(b2_ok, 1)
                for m in range(4):
                    dve.wait_ge(out_full, m + 1)
                    dve.tensor_tensor(chip.x[:, 2 * m:2 * m + 2, :], chip.x[:, 2 * m:2 * m + 2, :],
                                      ps[:, 4 + m, :].rearrange("p (j n) -> p j n", j=2), ALU.add)

            @block.tensor
            def _(pe):
                def three(out, l_hi, l_lo, r_hi, r_lo, first, last):
                    pe.matmul(out, l_hi, r_hi, start=first, stop=False)
                    pe.matmul(out, l_hi, r_lo, start=False, stop=False)
                    return pe.matmul(out, l_lo, r_hi, start=False, stop=last)

                for n in range(NU):
                    f = n // 2
                    pe.wait_ge(w1_ok, f // 2 + 1)
                    if n >= 4:
                        pe.wait_ge(gelu, n - 3)
                    for c in range(NC):
                        mm = three(ps[:, n % 4, :], w1_hi[:, c, part(f)], w1_lo[:, c, part(f)], h_hi[:, c, half(n)], h_lo[:, c, half(n)], c == 0, c == NC - 1)
                    mm.then_inc(full, 1)
                pe.wait_ge(u_ok, NU)
                pe.wait_ge(w2_ok, 4)
                for t in range(NT):
                    for f in range(NF):
                        mm = three(ps[:, 4 + t // 2, (t % 2) * D:(t % 2 + 1) * D], u_hi[:, f, part(t)], u_lo[:, f, part(t)], w2_hi[:, f, :], w2_lo[:, f, :], f == 0, f == NF - 1)
                    if t % 2:
                        mm.then_inc(out_full, 1)


E1 = 256
H1, S1 = 32, 8
KM = 32
NMIX = 5
KD = 64
L1_WEIGHTS = ['Wr', 'Wk', 'Wv', 'Wg', 'Wo', 'ffn_Wk', 'ffn_Wr', 'ffn_Wv']
R1 = S + 1


def layer1_memory(chip, st, d):
    nc = chip.nc
    sb = lambda n, s: st.enter_context(nc.sbuf_tensor(f"r_{n}", s, F32))
    w = {n: sb(n, [P, NC, E1]) for n in L1_WEIGHTS}
    m = {'w': w, 'maa_w1': sb("maa_w1", [P, NC, NMIX * KM]), 'maa_w2': sb("maa_w2", [P, E1]), 'maa_w2e': sb("maa_w2e", [KM, E1]),
         'decay_w1': sb("decay_w1", [P, NC, KD]), 'decay_w2': sb("decay_w2", [KD, E1]),
         's0': sb("s0", [P, NC, B, S1]), 'ld': chip.semaphore("ld_layer1")}
    ld = m['ld']
    count = [0]

    def load(sp):
        def go(dst, src):
            sp.dma_start(dst, src).then_inc(ld, 16)
            count[0] += 16

        for b in range(B):
            go(m['s0'][:, :, b, :], d['ctx_2048'][b, 2:2 + S1, :].rearrange("r (q e) -> (r q) e", e=S1).rearrange("(c p) e -> p c e", p=P))
        go(m['maa_w1'][:, :, :], d['L1_xattn_maa_w1'].rearrange("(c p) n -> p c n", p=P))
        go(m['maa_w2'][:, :], d['L1_xattn_maa_w2'][0:4].rearrange("i k n -> (i k) n"))
        go(m['maa_w2e'][:, :], d['L1_xattn_maa_w2'][4])
        go(m['decay_w1'][:, :, :], d['L1_xattn_decay_w1'].rearrange("(c p) n -> p c n", p=P))
        go(m['decay_w2'][:, :], d['L1_xattn_decay_w2'])
        for n in L1_WEIGHTS:
            go(w[n][:, :, :], d[f'L1_xattn_{n}_T'].rearrange("(c p) n -> p c n", p=P))
        sp.wait_ge(ld, count[0])

    return m, load


def stage_rwkv_mix(chip, m, xe, kT, vT, rT, wT, gT):
    nc, ps = chip.nc, chip.psum
    w = m['w']
    with ExitStack() as st:
        sb = lambda n, s, t=F32: st.enter_context(nc.sbuf_tensor(f"mix_{n}", s, t))
        sem = lambda n: chip.semaphore(f"mix_{n}")
        sx = sb("shift", [P, NC, B, S])
        first = sb("first", [P, NC, B, S])
        lowA, lowB = sb("lowA", [P, TOK]), sb("lowB", [KM, TOK])
        scaled = sb("scaled", [P, 2, NC, TOK])
        mixed = sb("mixed", [P, 2, NC, TOK])
        dec = sb("dec", [KD, TOK])
        e1 = sb("e1", [P, 2, BANK])
        th = sb("th", [P, 2, BANK])
        cur = lambda c: xe[:, c, :, 1:R1]
        flat = lambda ap: ap.rearrange("p b s -> p (b s)")
        batches = lambda ap: ap.rearrange("p (b s) -> p b s", s=S)
        MIX = {'w': 1, 'k': 0, 'v': 2, 'r': 3, 'g': 4}
        ORDER = 'wkvrg'
        uses = [('low', n, 'act') for n in range(4)]
        uses += [('mw', n, 'dve') for n in range(4)] + [('mk', n, 'dve') for n in range(4)] + [('d1', n, 'act') for n in range(2)]
        uses += [('mv', n, 'dve') for n in range(4)] + [('pk', n, 'act') for n in range(4)] + [('d2', n, 'act') for n in range(4)]
        uses += [('mr', n, 'dve') for n in range(4)] + [('pv', n, 'act') for n in range(4)] + [('mg', n, 'dve') for n in range(4)]
        uses += [('pr', n, 'act') for n in range(4)] + [('pg', n, 'dve') for n in range(4)]
        num = {u[:2]: i for i, u in enumerate(uses)}
        nth = lambda i: sum(u[2] == uses[i][2] for u in uses[:i + 1])
        full, act_free, dve_free, shifted, first_ok, low_ok, mix_dve, mix_pool, dec_ok, e_ok, th_ok = (
            sem(n) for n in ("full", "act_read", "dve_read", "shifted", "first_ok", "low_ok", "mixed_dve",
                             "mixed_pool", "dec_ok", "e_ok", "th_ok"))
        ch = lambda n: (n // 2, n % 2)
        half = lambda n: slice((n % 2) * HALF, (n % 2 + 1) * HALF)
        bh = lambda n: slice(2 * (n % 2), 2 * (n % 2) + 2)

        with nc.Block() as block:
            @block.tensor
            def _(pe):
                def begin(key):
                    n = num[key]
                    if n >= 8:
                        pe.wait_ge(act_free if uses[n - 8][2] == 'act' else dve_free, nth(n - 8))
                    return ps[:, n % 8, :]

                def product(key, weight, cols, src, rows=P):
                    out = begin(key)[0:rows, :]
                    for c in range(NC):
                        mm = pe.matmul(out, weight[:, c, cols], src(c), start=c == 0, stop=c == NC - 1)
                    mm.then_inc(full, 1)

                for key in [u[:2] for u in uses]:
                    what, n = key
                    if what == 'low':
                        pe.wait_ge(first_ok, 2)
                        src = lambda c: flat(first[:, c, bh(n), :])
                        product(key, m['maa_w1'], slice(0, P) if n < 2 else slice(P, NMIX * KM), src, P if n < 2 else KM)
                    elif what[0] == 'm':
                        i, (c, _h) = MIX[what[1]], ch(n)
                        pe.wait_ge(low_ok, 4)
                        out = begin(key)
                        if i < 4:
                            lhs, rhs = m['maa_w2'][KM * i:KM * i + KM, c * P:(c + 1) * P], lowA[KM * i:KM * i + KM, half(n)]
                        else:
                            lhs, rhs = m['maa_w2e'][:, c * P:(c + 1) * P], lowB[:, half(n)]
                        tile = (KM * i, 0) if i < 4 else (0, 0)
                        pe.matmul(out, lhs, rhs, start=True, stop=True, tile_position=tile).then_inc(full, 1)
                    elif what == 'd1':
                        if n == 0:
                            pe.wait_ge(mix_dve, 1)
                            pe.wait_ge(mix_pool, 1)
                        product(key, m['decay_w1'], slice(0, KD), lambda c: mixed[:, 0, c, half(n)], KD)
                    elif what == 'd2':
                        pe.wait_ge(dec_ok, 2)
                        out = begin(key)
                        pe.matmul(out, m['decay_w2'][:, (n // 2) * P:(n // 2 + 1) * P], dec[:, half(n)], start=True, stop=True).then_inc(full, 1)
                    else:
                        i = ORDER.index(what[1])
                        if n == 0:
                            pe.wait_ge(mix_dve, i + 1)
                            pe.wait_ge(mix_pool, i + 1)
                        product(key, w['W' + what[1]], slice((n // 2) * P, (n // 2 + 1) * P), lambda c: mixed[:, i % 2, c, half(n)])

            @block.vector
            def _(dve):
                dve.tensor_copy(xe[:, :, :, 0:1], chip.vecs[:, :, PREV + B:PREV + 2 * B].unsqueeze(3)).then_inc(shifted, 1)
                dve.wait_ge(shifted, 1)
                for c in range(NC):
                    dve.tensor_tensor(sx[:, c, :, :], xe[:, c, :, 0:S], cur(c), ALU.subtract).then_inc(shifted, 1)
                for c in range(NC):
                    dve.wait_ge(shifted, c + 2)
                    dve.scalar_tensor_tensor(first[:, c, :, :], sx[:, c, :, :], chip.vec('L1_xattn_maa_x', c), cur(c), ALU.mult, ALU.add).then_inc(first_ok, 1)
                for i, x in enumerate(ORDER):
                    if i >= 2:
                        prior = ORDER[i - 2]
                        dve.wait_ge(full, num[('d1', 1) if prior == 'w' else ('p' + prior, 3)] + 1)
                        dve.wait_ge(mix_pool, i - 1)
                    for n in range(4):
                        c, h = ch(n)
                        dve.wait_ge(full, num[('m' + x, n)] + 1)
                        dve.scalar_tensor_tensor(batches(scaled[:, i % 2, c, half(n)]), batches(ps[:, num[('m' + x, n)] % 8, :]),
                                                 chip.vec('L1_xattn_maa_stack', c, MIX[x]), sx[:, c, bh(n), :], ALU.add, ALU.mult).then_inc(dve_free, 1)
                    dve.wait_ge(dve_free, nth(num[('m' + x, 3)]))
                    dve.tensor_tensor(batches(mixed[:, i % 2, 0, :]), batches(scaled[:, i % 2, 0, :]), cur(0), ALU.add).then_inc(mix_dve, 1)
                for n in range(4):
                    c, h = ch(n)
                    dve.wait_ge(th_ok, n + 1)
                    dve.scalar_tensor_tensor(gT[:, c, half(n)], th[:, n % 2, :], 1.0, ps[:, num[('pg', n)] % 8, :], ALU.add, ALU.mult).then_inc(dve_free, 1)

            @block.gpsimd
            def _(pool):
                for t in (kT, vT, wT):
                    pool.memset(t[:, :, :, 0:1], 0.0)
                for i, x in enumerate(ORDER):
                    pool.wait_ge(dve_free, nth(num[('m' + x, 3)]))
                    pool.tensor_tensor(batches(mixed[:, i % 2, 1, :]), batches(scaled[:, i % 2, 1, :]), cur(1), ALU.add).then_inc(mix_pool, 1)

            @block.scalar
            def _(act):
                for i, (what, n, reader) in enumerate(uses):
                    c, h = ch(n)
                    src = ps[:, i % 8, :]
                    if what == 'pg':
                        act.wait_ge(full, i + 1)
                        if n >= 2:
                            act.wait_ge(dve_free, nth(num[('pg', n - 2)]))
                        act.activation(th[:, n % 2, :], src, ACT.Tanh, scale=0.5).then_inc(th_ok, 1)
                        continue
                    if reader != 'act':
                        continue
                    act.wait_ge(full, i + 1)
                    if what == 'low':
                        dst, src = (lowA[:, half(n)], src) if n < 2 else (lowB[:, half(n)], src[0:KM, :])
                        act.activation(dst, src, ACT.Tanh).then_inc(act_free, 1)
                        if n == 3:
                            act.wait_ge(act_free, nth(i))
                            act.sem_inc(low_ok, 4)
                    elif what == 'd1':
                        act.activation(dec[:, half(n)], src[0:KD, :], ACT.Tanh).then_inc(act_free, 1)
                        if n == 1:
                            act.wait_ge(act_free, nth(i))
                            act.sem_inc(dec_ok, 2)
                    elif what == 'd2':
                        act.activation(e1[:, n % 2, :], src, ACT.Exp, bias=chip.vec('L1_xattn_time_decay', c)).then_inc(act_free, 1)
                        act.wait_ge(act_free, nth(i))
                        act.activation(wT[:, c, bh(n), 1:S], batches(e1[:, n % 2, :])[:, :, 0:S - 1], ACT.Exp, scale=-1.0).then_inc(e_ok, 1)
                        act.wait_ge(e_ok, n + 1)
                    elif what in ('pk', 'pv'):
                        act.activation((kT if what == 'pk' else vT)[:, c, bh(n), 1:R1], batches(src), ACT.Copy).then_inc(act_free, 1)
                    elif what == 'pr':
                        act.activation(rT[:, c, half(n)], src, ACT.Copy).then_inc(act_free, 1)


def stage_rwkv_scan(chip, m, kT, vT, rT, wT, gT, make_ln):
    nc, ps = chip.nc, chip.psum
    HP = P // S1
    with ExitStack() as st:
        sb = lambda n, s, t=F32: st.enter_context(nc.sbuf_tensor(f"scan_{n}", s, t))
        sem = lambda n: chip.semaphore(f"scan_{n}")
        same = sb("same_head", [P, P])
        dmask = sb("d_mask", [P, S1])
        spread = sb("spread", [P, S1, P], F32R)
        gather = sb("gather", [P, S1, P])
        v_hi, v_lo = sb("v_hi", [P, NC, B, R1 + 1], F32R), sb("v_lo", [P, NC, B, R1 + 1], F32R)
        ruk = sb("ruk", [P, NC, TOK])
        kv = sb("kv", [P, 2, NC, B, S])
        state = sb("state", [P, 2, NC, B, S])
        z = sb("z", [P, 2, NC, TOK])
        att = sb("att", [P, NC, TOK])
        sq = sb("sq", [P, NC, TOK])
        ru = sb("ru", [P, NC, TOK])
        LATE = 2
        SEQ = (0, 2, 1, 3)
        epsc = sb("eps", [P, 1])
        (mats, dmask_ok, spread_ok, gather_ok, vcut, ruk_ok, v_full, kv_ok, s0_ok, st_ok, z_ok, g_full, ru_full, att_ok,
         mean_full, cent_ok, sq_ok, var_full, log_ok, rstd_ok, gn_ok, gated, o_full, ru_read, x_ok) = (
            sem(n) for n in ("mats", "dmask_ok", "spread_ok", "gather_ok", "v_cut", "ruk_ok", "v_full", "kv_ok", "s0_ok",
                             "states_ok", "z_ok", "gathered", "ru_full", "att_ok", "mean_full", "centred", "squared", "var_full",
                             "log_ok", "rstd_ok", "normed", "gated", "out_full", "ru_read", "x_ok"))
        ln = make_ln(st, bank=0)
        ln.ready = (x_ok, 0)
        half = lambda n: slice((n % 2) * HALF, (n % 2 + 1) * HALF)
        bh = lambda n: slice(2 * (n % 2), 2 * (n % 2) + 2)
        batches = lambda ap: ap.rearrange("p (b s) -> p b s", s=S)
        flatb = lambda ap: ap.rearrange("p b s -> p (b s)")

        with nc.Block() as block:
            @block.gpsimd
            def _(pool):
                pool.memset(epsc[:, :], EPS0)
                pool.memset(gather[:, :, :], 0.0)
                pool.memset(same[:, :], 1.0).then_inc(mats, 1)
                v = same[:, :].rearrange("p (h e) -> p h e", e=S1)
                pool.wait_ge(mats, 1)
                pool.affine_select(out=v, in_=v, compare_op=ALU.is_ge, fill=0.0, base=0, pattern=[[-S1, HP], [0, S1]], channel_multiplier=1).then_inc(mats, 1)
                pool.wait_ge(mats, 2)
                pool.affine_select(out=v, in_=v, compare_op=ALU.is_ge, fill=0.0, base=S1 - 1, pattern=[[S1, HP], [0, S1]], channel_multiplier=-1).then_inc(mats, 1)
                for e in range(S1):
                    pool.wait_ge(st_ok, (e + 1) * NC)
                    if e >= 2:
                        pool.wait_ge(g_full, e - 1)
                    for c in range(NC):
                        pool.tensor_tensor(z[:, e % 2, c, :], rT[:, c, :], flatb(state[:, e % 2, c, :, :]), ALU.mult).then_inc(z_ok, 1)
                ln.gpsimd(pool)

            @block.vector
            def _(dve):
                dve.tensor_reduce(dmask[:, :], chip.ident[:, :].rearrange("p (h e) -> p e h", e=S1), AX.X, ALU.add).then_inc(dmask_ok, 1)
                dve.wait_ge(vcut, 1)
                dve.tensor_tensor(v_lo[:, :, :, 0:R1], vT[:, :, :, :], v_hi[:, :, :, 0:R1].bitcast(F32), ALU.subtract).then_inc(vcut, 1)
                dve.wait_ge(mats, 3)
                dve.wait_ge(dmask_ok, 1)
                for e in range(S1):
                    dve.tensor_scalar(spread[:, e, :], same[:, :], dmask[:, e:e + 1], None, ALU.mult).then_inc(spread_ok, 1)
                for e in range(S1):
                    dve.tensor_copy(gather[:, e, e:P:S1], same[:, e:P:S1]).then_inc(gather_ok, 1)
                for e in range(S1):
                    for n in range(4):
                        c = n // 2
                        u = e * 4 + n
                        dve.wait_ge(v_full, u + 1)
                        if e >= 2:
                            dve.wait_ge(st_ok, (e - 2) * NC + c + 1)
                        dve.tensor_tensor(kv[:, e % 2, c, bh(n), :], kT[:, c, bh(n), 0:S], batches(ps[:, u % 4, :]), ALU.mult).then_inc(kv_ok, 1)
                    dve.wait_ge(kv_ok, 4 * e + 4)
                    dve.tensor_copy(kv[:, e % 2, :, :, 0:1], m['s0'][:, :, :, e:e + 1]).then_inc(s0_ok, 1)
                    dve.wait_ge(s0_ok, e + 1)
                    for c in range(NC):
                        if e >= 2:
                            dve.wait_ge(z_ok, (e - 2) * NC + c + 1)
                        dve.tensor_tensor_scan(flatb(state[:, e % 2, c, :, :]), flatb(wT[:, c, :, :]), flatb(kv[:, e % 2, c, :, :]), 0.0, ALU.mult, ALU.add).then_inc(st_ok, 1)
                    if e == 0:
                        for c in range(NC):
                            dve.scalar_tensor_tensor(batches(ruk[:, c, :]), batches(rT[:, c, :]), chip.vec('L1_xattn_faaaa', c), kT[:, c, :, 1:R1], ALU.mult, ALU.mult).then_inc(ruk_ok, 1)
                for n in SEQ:
                    dve.wait_ge(ru_read, 4)
                    dve.tensor_tensor(batches(att[:, n // 2, half(n)]), batches(ru[:, n // 2, half(n)]), vT[:, n // 2, bh(n), 1:R1], ALU.mult).then_inc(att_ok, 1)

                def centre(i):
                    n = SEQ[i]
                    dve.wait_ge(mean_full, i + 1)
                    dve.scalar_tensor_tensor(att[:, n // 2, half(n)], ps[:, n, :], -1.0 / S1, att[:, n // 2, half(n)], ALU.mult, ALU.add).then_inc(cent_ok, 1)

                for i, n in enumerate(SEQ):
                    dve.wait_ge(att_ok, i + 1)
                    dve.wait_ge(g_full, S1 + i)
                    dve.tensor_tensor(att[:, n // 2, half(n)], att[:, n // 2, half(n)], ps[:, 4 + n, :], ALU.add).then_inc(att_ok, 1)
                    if i >= 2:
                        centre(i - 2)
                centre(2)
                centre(3)

                def gate(i):
                    n = SEQ[i]
                    dve.wait_ge(gn_ok, i + 1)
                    dve.scalar_tensor_tensor(z[:, 0, n // 2, half(n)], att[:, n // 2, half(n)], chip.vec('L1_xattn_gn_b', n // 2), gT[:, n // 2, half(n)],
                                             ALU.add, ALU.mult).then_inc(gated, 1)

                for i, n in enumerate(SEQ):
                    c = n // 2
                    dve.wait_ge(rstd_ok, i + 1)
                    dve.scalar_tensor_tensor(att[:, c, half(n)], att[:, c, half(n)], chip.vec('L1_xattn_gn_w', c), sq[:, c, half(n)], ALU.mult, ALU.mult).then_inc(gn_ok, 1)
                    if i:
                        gate(i - 1)
                gate(3)
                for q in range(4):
                    dve.wait_ge(o_full, q + 1)
                    dve.scalar_tensor_tensor(chip.x[:, 2 * q:2 * q + 2, :], ps[:, 4 + q, :].rearrange("p (j n) -> p j n", j=2), 0.5,
                                             chip.x[:, 2 * q:2 * q + 2, :], ALU.mult, ALU.add).then_inc(x_ok, 1)
                    ln.after_rows(dve, q)

            @block.scalar
            def _(act):
                act.activation(v_hi[:, :, :, 0:R1], vT[:, :, :, :], ACT.Copy).then_inc(vcut, 1)
                for n in range(4):
                    act.wait_ge(ru_full, n + 1)
                    act.activation(ru[:, n // 2, half(n)], ps[:, 4 + n, :], ACT.Copy).then_inc(ru_read, 1)
                for i, n in enumerate(SEQ):
                    act.wait_ge(cent_ok, i + 1)
                    act.activation(sq[:, n // 2, half(n)], att[:, n // 2, half(n)], ACT.Square).then_inc(sq_ok, 1)
                for i, n in enumerate(SEQ):
                    act.wait_ge(var_full, i + 1)
                    act.activation(sq[:, n // 2, half(n)], ps[:, 4 + n, :], ACT.Ln, scale=1.0 / S1, bias=epsc[:, :]).then_inc(log_ok, 1)
                for i, n in enumerate(SEQ):
                    act.wait_ge(log_ok, i + 1)
                    act.activation(sq[:, n // 2, half(n)], sq[:, n // 2, half(n)], ACT.Exp, scale=-0.5).then_inc(rstd_ok, 1)
                ln.scalar(act)

            @block.tensor
            def _(pe):
                pe.wait_ge(vcut, 2)
                for e in range(S1 + LATE):
                    if e < S1:
                        pe.wait_ge(spread_ok, e + 1)
                        for n in range(4):
                            u = e * 4 + n
                            if u >= 4:
                                pe.wait_ge(kv_ok, u - 3)
                            c = n // 2
                            out = batches(ps[:, u % 4, :])
                            pe.matmul(out, spread[:, e, :], v_hi[:, c, bh(n), 0:S], start=True, stop=False)
                            pe.matmul(out, spread[:, e, :], v_lo[:, c, bh(n), 0:S], start=False, stop=True).then_inc(v_full, 1)
                    if e == LATE - 1:
                        pe.wait_ge(ruk_ok, NC)
                        for n in range(4):
                            pe.matmul(ps[:, 4 + n, :], same[:, :], ruk[:, n // 2, half(n)], start=True, stop=True).then_inc(ru_full, 1)
                    if e >= LATE:
                        g = e - LATE
                        if g == 0:
                            pe.wait_ge(gather_ok, S1)
                            pe.wait_ge(ru_read, 4)
                        pe.wait_ge(z_ok, NC * g + NC)
                        for n in SEQ:
                            mm = pe.matmul(ps[:, 4 + n, :], gather[:, g, :], z[:, g % 2, n // 2, half(n)], start=g == 0, stop=g == S1 - 1)
                            if g == S1 - 1:
                                mm.then_inc(g_full, 1)
                        if g < S1 - 1:
                            mm.then_inc(g_full, 1)
                for i, n in enumerate(SEQ):
                    pe.wait_ge(att_ok, 4 + i + 1)
                    pe.matmul(ps[:, n, :], same[:, :], att[:, n // 2, half(n)], start=True, stop=True).then_inc(mean_full, 1)
                for i, n in enumerate(SEQ):
                    pe.wait_ge(sq_ok, i + 1)
                    pe.matmul(ps[:, 4 + n, :], same[:, :], sq[:, n // 2, half(n)], start=True, stop=True).then_inc(var_full, 1)
                for t in range(NT):
                    if t % 4 == 0:
                        pe.wait_ge(gated, 2 + 2 * (t // 4))
                        pe.wait_ge(log_ok, 4)
                    for c in range(NC):
                        mm = pe.matmul(ps[:, 4 + t // 2, (t % 2) * D:(t % 2 + 1) * D], z[:, 0, c, t * P:(t + 1) * P], m['w']['Wo'][:, c, :], start=c == 0, stop=c == NC - 1)
                    if t % 2:
                        mm.then_inc(o_full, 1)
                ln.tensor(pe)


def stage_channel_mix(chip, m, xe):
    nc, ps = chip.nc, chip.psum
    w = m['w']
    with ExitStack() as st:
        sb = lambda n, s, t=F32: st.enter_context(nc.sbuf_tensor(f"cm_{n}", s, t))
        sem = lambda n: chip.semaphore(f"cm_{n}")
        sx, xk, xr = sb("shift", [P, NC, B, S]), sb("xk", [P, NC, B, S]), sb("xr", [P, NC, B, S])
        relu, kk = sb("relu", [P, NC, TOK]), sb("kk", [P, NC, TOK])
        gate = sb("gate", [P, NT, D])
        t1 = sb("t1", [P, NT, D])
        shifted, mixed, k_full, r_ok, kk_ok, r_full, th_ok, g_ok, v_full, t_ok = (
            sem(n) for n in ("shifted", "mixed", "k_full", "relu_ok", "kk_ok", "r_full", "tanh_ok", "gate_ok", "v_full", "t_ok"))
        half = lambda n: slice((n % 2) * HALF, (n % 2 + 1) * HALF)
        bh = lambda n: slice(2 * (n % 2), 2 * (n % 2) + 2)
        cur = lambda c: xe[:, c, :, 1:R1]
        with nc.Block() as block:
            @block.vector
            def _(dve):
                dve.tensor_copy(xe[:, :, :, 0:1], chip.vecs[:, :, PREV:PREV + B].unsqueeze(3)).then_inc(shifted, 1)
                dve.wait_ge(shifted, 1)
                for c in range(NC):
                    dve.tensor_tensor(sx[:, c, :, :], xe[:, c, :, 0:S], cur(c), ALU.subtract).then_inc(shifted, 1)
                for dst, v in ((xk, 'L1_xattn_ffn_maa_k'), (xr, 'L1_xattn_ffn_maa_r')):
                    for c in range(NC):
                        dve.wait_ge(shifted, c + 2)
                        dve.scalar_tensor_tensor(dst[:, c, :, :], sx[:, c, :, :], chip.vec(v, c), cur(c), ALU.mult, ALU.add).then_inc(mixed, 1)
                for n in range(4):
                    dve.wait_ge(r_ok, n + 1)
                    dve.scalar_tensor_tensor(kk[:, n // 2, half(n)], ps[:, n, :], 0.0, relu[:, n // 2, half(n)], ALU.max, ALU.mult).then_inc(kk_ok, 1)
                for q in range(4):
                    dve.wait_ge(th_ok, q + 1)
                    dve.tensor_scalar(gate[:, 2 * q:2 * q + 2, :], gate[:, 2 * q:2 * q + 2, :], 0.5, 0.5, ALU.mult, ALU.add).then_inc(g_ok, 1)
                for q in range(4):
                    dve.wait_ge(v_full, q + 1)
                    dve.wait_ge(g_ok, q + 1)
                    dve.tensor_tensor(t1[:, 2 * q:2 * q + 2, :], gate[:, 2 * q:2 * q + 2, :], ps[:, q, :].rearrange("p (j n) -> p j n", j=2), ALU.mult).then_inc(t_ok, 1)
                    dve.wait_ge(t_ok, q + 1)
                    dve.tensor_tensor(chip.x[:, 2 * q:2 * q + 2, :], chip.x[:, 2 * q:2 * q + 2, :], t1[:, 2 * q:2 * q + 2, :], ALU.add)

            @block.scalar
            def _(act):
                for n in range(4):
                    act.wait_ge(k_full, n + 1)
                    act.activation(relu[:, n // 2, half(n)], ps[:, n, :], ACT.Relu).then_inc(r_ok, 1)
                for q in range(4):
                    act.wait_ge(r_full, q + 1)
                    act.activation(gate[:, 2 * q:2 * q + 2, :], ps[:, 4 + q, :].rearrange("p (j n) -> p j n", j=2), ACT.Tanh, scale=0.5).then_inc(th_ok, 1)

            @block.tensor
            def _(pe):
                for n in range(4):
                    pe.wait_ge(mixed, 2)
                    for c in range(NC):
                        mm = pe.matmul(ps[:, n, :], w['ffn_Wk'][:, c, (n // 2) * P:(n // 2 + 1) * P], xk[:, c, bh(n), :].rearrange("p b s -> p (b s)"), start=c == 0, stop=c == NC - 1)
                    mm.then_inc(k_full, 1)
                pe.wait_ge(mixed, 4)
                for t in range(NT):
                    for c in range(NC):
                        mm = pe.matmul(ps[:, 4 + t // 2, (t % 2) * D:(t % 2 + 1) * D], xr[:, c, t // 2, (t % 2) * P:(t % 2 + 1) * P], w['ffn_Wr'][:, c, :], start=c == 0, stop=c == NC - 1)
                    if t % 2:
                        mm.then_inc(r_full, 1)
                pe.wait_ge(kk_ok, 4)
                for t in range(NT):
                    for c in range(NC):
                        mm = pe.matmul(ps[:, t // 2, (t % 2) * D:(t % 2 + 1) * D], kk[:, c, t * P:(t + 1) * P], w['ffn_Wv'][:, c, :], start=c == 0, stop=c == NC - 1)
                    if t % 2:
                        mm.then_inc(v_full, 1)


class Small:

    def __init__(self, tag, heads, kv_heads, width, scale, passes):
        self.tag, self.H, self.KV, self.W, self.scale, self.passes = tag, heads, kv_heads, width, scale, passes
        self.R = 32 // width
        self.G = heads // 4
        self.kv_cols = kv_heads * width
        self.per_chunk = P // (4 * width)


L2 = Small("l2", 16, 16, 16, 16 ** -0.5, 2)
L3 = Small("l3", 32, 8, 8, 1.0 / float(np.sqrt(np.float32(8.0))), 1)
BIG = 3e38


def stage_turn_and_bias(chip, rows, out, bias, mask):
    nc, ps = chip.nc, chip.psum
    turned = chip.semaphore("t3_turned")
    with nc.Block() as block:
        @block.tensor
        def _(pe):
            for n in range(4):
                for t in range(4):
                    mm = pe.transpose(ps[:, n, t * P:(t + 1) * P], rows[:, (n % 2) * 4 + t, (n // 2) * P:(n // 2 + 1) * P], chip.ident[:, :])
                mm.then_inc(turned, 1)

        @block.scalar
        def _(act):
            for n in range(4):
                act.wait_ge(turned, n + 1)
                act.activation(out[:, n // 2, (n % 2) * HALF:(n % 2 + 1) * HALF], ps[:, n, :], ACT.Copy)

        @block.vector
        def _(dve):
            dve.tensor_scalar(mask[:, :, :], mask[:, :, :], -1.0, None, ALU.mult)
            dve.wait_ge(turned, 4)
            dve.tensor_tensor(rows[:, :, :], rows[:, :, :], bias.to_broadcast([P, NT, D]), ALU.add)


def stage_small_project(chip, sh, wq, wk, wv, q_src, k_src, q_bias, k_bias, v_bias, mem, place):
    nc, ps = chip.nc, chip.psum
    selq, selk = place
    W, G, R, NK = sh.W, sh.G, sh.R, sh.passes
    tag, KC = sh.tag, max(1, sh.kv_cols // P)
    KR = min(P, sh.kv_cols)
    q_hi, q_lo, k_hi, k_lo, v1 = mem
    with ExitStack() as st:
        sb = lambda n, s, t=F32: st.enter_context(nc.sbuf_tensor(f"{tag}_{n}", s, t))
        sem = lambda n: chip.semaphore(f"{tag}_{n}")
        full = sb("qk_full", [P, 8, BANK])
        nq = sb("neg_bq", [P, NC])
        pe_full, whole, hi_ok, v_full, nq_ok, zeroed = (sem(n) for n in ("p_full", "p_whole", "p_hi", "p_v", "p_bias", "zeroed"))
        pieces = [('q', c, h) for c in range(NC) for h in range(2)] + [('k', c, h) for c in range(KC) for h in range(2)]
        dst = lambda p, hi: ((q_hi if hi else q_lo) if p[0] == 'q' else (k_hi if hi else k_lo))[0:P if p[0] == 'q' else KR, p[1], p[2] * HALF:(p[2] + 1) * HALF]
        np_ = len(pieces)
        with nc.Block() as block:
            @block.tensor
            def _(pe):
                for i, (w, c, h) in enumerate(pieces):
                    cols = slice(h * HALF, (h + 1) * HALF)
                    rows = P if w == 'q' else KR
                    for k in range(NC):
                        mm = pe.matmul(ps[0:rows, i, :], (wq if w == 'q' else wk)[:, k, c * P:c * P + rows],
                                       (q_src if w == 'q' else k_src)[:, k, cols], start=k == 0, stop=k == NC - 1)
                    mm.then_inc(pe_full, 1)
                for t in range(NT):
                    if t % 2 == 0 and t // 2 < np_:
                        pe.wait_ge(whole, t // 2 + 1)
                    for k in range(NC):
                        mm = pe.matmul(ps[:, t // 2, (t % 2) * D:(t % 2) * D + sh.kv_cols], k_src[:, k, t * P:(t + 1) * P], wv[:, k, :],
                                       start=k == 0, stop=k == NC - 1)
                    if t % 2:
                        mm.then_inc(v_full, 1)

            @block.scalar
            def _(act):
                if q_bias:
                    act.wait_ge(nq_ok, NC)
                for i, (w, c, h) in enumerate(pieces):
                    rows = P if w == 'q' else KR
                    act.wait_ge(pe_full, i + 1)
                    bias = 0.0
                    if q_bias:
                        bias = nq[:, c:c + 1] if w == 'q' else k_bias[0:rows, :]
                    act.activation(full[0:rows, i, :], ps[0:rows, i, :], ACT.Identity, scale=-sh.scale if w == 'q' else 1.0, bias=bias).then_inc(whole, 1)

            @block.vector
            def _(dve):
                if q_bias:
                    for c in range(NC):
                        dve.tensor_scalar(nq[:, c:c + 1], q_bias(c), -sh.scale, None, ALU.mult).then_inc(nq_ok, 1)
                dve.memset(v1[:, :, :, sh.W:sh.W + 1], 1.0)
                dve.memset(v1[:, :, :, sh.W + 1:32], 0.0)
                if KR < P:
                    for half_k in (k_hi, k_lo):
                        dve.memset(half_k[KR:P, 0, :].bitcast(F32), 0.0)
                dve.wait_ge(zeroed, 2)
                ident = lambda n, k: chip.ident[:, 0:n * k * W].rearrange("p (g j w) -> p g j w", g=n, w=W)
                for r in range(R):
                    for g in range(sh.per_chunk):
                        dve.tensor_copy(selq[:, r % 2, g, :, r, :], ident(sh.per_chunk, 4)[:, g])
                if NK == 2:
                    for r in range(R):
                        for g in range(sh.per_chunk):
                            dve.tensor_copy(selk[:, 0, g, :, r, :], ident(sh.per_chunk, 4)[:, g])
                else:
                    for r in range(R):
                        for j in range(4):
                            dve.tensor_copy(selk[:, r // 2, :, j, r, :], ident(G, 1)[:, :, 0])
                for i, p in enumerate(pieces):
                    rows = P if p[0] == 'q' else KR
                    dve.wait_ge(whole, i + 1)
                    dve.tensor_copy(dst(p, True), full[0:rows, i, :]).then_inc(hi_ok, 1)
                    if i % 2:
                        dve.wait_ge(hi_ok, i + 1)
                        dve.tensor_tensor(dst(p, False), full[0:rows, i, :], dst(p, True).bitcast(F32), ALU.subtract)
                for t in range(NT):
                    dve.wait_ge(v_full, t // 2 + 1)
                    src = ps[:, t // 2, (t % 2) * D:(t % 2) * D + sh.kv_cols].rearrange("p (h e) -> p h e", e=sh.W)
                    if v_bias is None:
                        dve.tensor_copy(v1[:, t, :, 0:sh.W], src)
                    else:
                        dve.tensor_tensor(v1[:, t, :, 0:sh.W], src, v_bias.rearrange("p (h e) -> p h e", e=sh.W), ALU.add)

            @block.gpsimd
            def _(pool):
                pool.memset(selq[:].rearrange("p a g j r w -> p (a g j r w)").bitcast(F32), 0.0).then_inc(zeroed, 1)
                pool.memset(selk[:].rearrange("p a g j r w -> p (a g j r w)").bitcast(F32), 0.0).then_inc(zeroed, 1)
                for i, p in enumerate(pieces):
                    if i % 2:
                        continue
                    rows = P if p[0] == 'q' else KR
                    pool.wait_ge(hi_ok, i + 1)
                    pool.tensor_tensor(dst(p, False), full[0:rows, i, :], dst(p, True).bitcast(F32), ALU.subtract)


def stage_small_stack(chip, sh, mem, place, qs, ks):
    nc, ps = chip.nc, chip.psum
    G, NK = sh.G, sh.passes
    q_hi, q_lo, k_hi, k_lo, _v1 = mem
    selq, selk = place
    sem = lambda n: chip.semaphore(f"{sh.tag}_{n}")
    full, act_read, dve_read = sem("stack_full"), sem("stack_act"), sem("stack_dve")
    pieces = [(w, g, h) for h in range(2) for w, n in (('q', G), ('k', NK * G)) for g in range(n)]
    cols = lambda h: slice(h * HALF, (h + 1) * HALF)

    with nc.Block() as block:
        @block.tensor
        def _(pe):
            for s, (w, g, h) in enumerate(pieces):
                if s >= 8:
                    pe.wait_ge(act_read if s % 2 == 0 else dve_read, (s - 8) // 2 + 1)
                out = ps[:, s % 8, :]
                if w == 'q':
                    for part, src in enumerate((q_hi, q_lo)):
                        mm = pe.matmul(out, selq[:, part, g % sh.per_chunk].rearrange("p j r w -> p (j r w)"),
                                       src[:, g // sh.per_chunk, cols(h)], start=part == 0, stop=part == 1)
                elif NK == 2:
                    mm = pe.matmul(out, selk[:, 0, g % sh.per_chunk].rearrange("p j r w -> p (j r w)"),
                                   (k_hi if g < G else k_lo)[:, (g % G) // sh.per_chunk, cols(h)], start=True, stop=True)
                else:
                    for part, src in enumerate((k_hi, k_lo)):
                        mm = pe.matmul(out, selk[:, part, g].rearrange("p j r w -> p (j r w)"), src[:, 0, cols(h)],
                                       start=part == 0, stop=part == 1)
                mm.then_inc(full, 1)

        def evacuate(eng, mine, done, copy):
            for s, (w, g, h) in enumerate(pieces):
                if s % 2 == mine:
                    eng.wait_ge(full, s + 1)
                    copy((qs if w == 'q' else ks)[:, g, cols(h)], ps[:, s % 8, :]).then_inc(done, 1)

        @block.scalar
        def _(act):
            evacuate(act, 0, act_read, lambda o, i: act.activation(o, i, ACT.Copy))

        @block.vector
        def _(dve):
            evacuate(dve, 1, dve_read, dve.tensor_copy)


def stage_small_attention(chip, sh, qs, ks, v1, masks):
    nc, ps = chip.nc, chip.psum
    tag, H, G, NK = sh.tag, sh.H, sh.G, sh.passes
    LEAD = 3
    NM = masks.shape[1] // B
    with ExitStack() as st:
        sb = lambda n, s, t=F32: st.enter_context(nc.sbuf_tensor(f"{tag}_{n}", s, t))
        sem = lambda n: chip.semaphore(f"{tag}_{n}")
        mask = sb("mask_neg", [P, NM, S])
        sc = sb("scores", [P, 4, 2, S])
        m = sb("neg_max", [P, 4, 2])
        pr = sb("prob", [P, 4, 2, S])
        pT = sb("prob_T", [P, 4, BANK])
        vb = sb("v_batch", [P, 2, sh.KV, 32])
        qb, kb = sb("q_batch", [P, G, S], F32R), sb("k_batch", [P, NK * G, S], F32R)
        stack_in = [sem(f"stack_in{g}") for g in range(G)]
        s_full, s_begun, s_read, p_ok, turned, act_ev, dve_ev, a_done, a_read, mask_ok = (
            sem(n) for n in ("scores_full", "scores_begun", "scores_read", "exp_ok", "turned", "turned_act", "turned_dve",
                             "sum_done", "sums_read", "mask_ok"))
        v_in = [sem(f"v_in{g}") for g in range(G)]
        assert H % 4 == 0

        def batches(eng, step):
            with eng.Fori(0, B - 1) as b:
                step(b, False)
            step(B - 1, True)

        def ahead(u, lead, last):
            n, v = (u + lead) // H, (u + lead) % H
            return None if n and last else (n, v)

        with nc.Block() as block:
            @block.tensor
            def _(pe):
                pe.sem_inc(turned, 4)
                pe.sem_inc(a_done, 4)

                def scores(b, u):
                    g, j = u // 4, u % 4
                    rows = slice(32 * j, 32 * j + 32)
                    if j == 0:
                        pe.wait_ge(stack_in[g], b * 16 * (1 + NK) + 16 * (1 + NK))
                    pe.wait_ge(s_read, b * H + u + 1)
                    for q in range(2):
                        for k in range(NK):
                            mm = pe.matmul(ps[:, u % 4, q * S:(q + 1) * S], qb[rows, g, q * P:(q + 1) * P], kb[rows, k * G + g, :],
                                           start=k == 0, stop=k == NK - 1, tile_position=(32 * j, 0))
                    mm.then_inc(s_full, 1)

                def turn(b, u):
                    pe.wait_ge(p_ok, b * H + u + 5)
                    pe.wait_ge(act_ev if u % 2 == 0 else dve_ev, b * (H // 2) + u // 2 + 1)
                    for t in range(2):
                        for q in range(2):
                            mm = pe.transpose(ps[:, 4 + u % 2, t * S + q * P:t * S + (q + 1) * P], pr[:, u % 4, q, t * P:(t + 1) * P], chip.ident[:, :])
                    mm.then_inc(turned, 1)

                def sums(b, u):
                    if u % 4 == 0:
                        pe.wait_ge(v_in[u // 4], b * 16 + 16)
                        pe.wait_ge(a_read, b * G + u // 4 + 1)
                    pe.wait_ge(act_ev if u % 2 == 0 else dve_ev, b * (H // 2) + u // 2 + 2)
                    for t in range(2):
                        mm = pe.matmul(ps[32 * (u % 4):32 * (u % 4) + 32, 6 + u // 4 % 2, 0:S], vb[:, t, u * sh.KV // H, :],
                                       pT[:, u % 4, t * S:(t + 1) * S], start=t == 0, stop=t == 1, tile_position=(0, 32 * (u % 4)))
                    mm.then_inc(a_done, 1)

                for u in range(LEAD):
                    scores(0, u)

                def step(b, last):
                    for u in range(H):
                        turn(b, u)
                        nxt = ahead(u, LEAD, last)
                        if nxt:
                            scores(b + nxt[0], nxt[1])
                        if u:
                            sums(b, u - 1)
                    sums(b, H - 1)

                batches(pe, step)

            @block.scalar
            def _(act):
                act.sem_inc(act_ev, 1)
                act.sem_inc(p_ok, 4)

                def exp(b, u):
                    act.wait_ge(s_read, b * H + u + 5)
                    act.wait_ge(turned, b * H + u + 1)
                    for q in range(2):
                        e = act.activation(pr[:, u % 4, q, :], sc[:, u % 4, q, :], ACT.Exp, scale=-1.0, bias=m[:, u % 4, q:q + 1])
                    e.then_inc(p_ok, 1)

                for u in range(LEAD - 1):
                    exp(0, u)

                def step(b, last):
                    for u in range(H):
                        if u % 2 == 0:
                            act.wait_ge(turned, b * H + u + 5)
                            act.wait_ge(a_done, b * H + u + 1)
                            act.activation(pT[:, u % 4, :], ps[:, 4, :], ACT.Copy).then_inc(act_ev, 1)
                        nxt = ahead(u, LEAD - 1, last)
                        if nxt:
                            exp(b + nxt[0], nxt[1])

                batches(act, step)

            @block.vector
            def _(dve):
                dve.sem_inc(dve_ev, 1)
                dve.sem_inc(s_read, 4)
                dve.sem_inc(a_read, 2)

                def least(b, u):
                    if u == 0:
                        dve.wait_ge(s_read, b * H + 4)
                        dve.tensor_copy(mask[:, :, :], masks[:, bass.ds(b * NM, NM), :]).then_inc(mask_ok, 1)
                        dve.wait_ge(mask_ok, b + 1)
                    dve.wait_ge(s_full, b * H + u + 1)
                    dve.wait_ge(p_ok, b * H + u + 1)
                    dve.sem_inc(s_begun, 1)
                    for q in range(2):
                        e = dve.tensor_tensor_reduce(sc[:, u % 4, q, :], ps[:, u % 4, q * S:(q + 1) * S], mask[:, q % NM, :],
                                                     1.0, BIG, ALU.add, ALU.min, m[:, u % 4, q:q + 1])
                    e.then_inc(s_read, 1)

                def keep(b, g):
                    dve.wait_ge(a_done, b * H + 4 * g + 8)
                    dve.tensor_copy(qs[:, g, bass.ds(b * S, S)].bitcast(F32), ps[:, 6 + g % 2, 0:S]).then_inc(a_read, 1)

                for u in range(LEAD):
                    least(0, u)

                def step(b, last):
                    for u in range(H):
                        if u % 2:
                            dve.wait_ge(turned, b * H + u + 5)
                            dve.wait_ge(a_done, b * H + u + 1)
                            dve.tensor_copy(pT[:, u % 4, :], ps[:, 5, :]).then_inc(dve_ev, 1)
                        nxt = ahead(u, LEAD, last)
                        if nxt:
                            least(b + nxt[0], nxt[1])
                        if u % 4 == 0 and u:
                            keep(b, u // 4 - 1)
                    keep(b, G - 1)

                batches(dve, step)

            @block.sync
            def _(sp):
                def load(b, g):
                    sp.dma_start(qb[:, g, :].bitcast(F32), qs[:, g, bass.ds(b * S, S)].bitcast(F32)).then_inc(stack_in[g], 16)
                    for k in range(NK):
                        sp.dma_start(kb[:, k * G + g, :].bitcast(F32), ks[:, k * G + g, bass.ds(b * S, S)].bitcast(F32)).then_inc(stack_in[g], 16)

                def load_v(b, g):
                    n = sh.KV // G * 32
                    sp.dma_start(vb[:].rearrange("p t h w -> p t (h w)")[:, :, g * n:(g + 1) * n],
                                 v1[:].rearrange("p t h w -> p t (h w)")[:, bass.ds(2 * b, 2), g * n:(g + 1) * n]).then_inc(v_in[g], 16)

                for g in range(G):
                    load(0, g)
                    load_v(0, g)
                with sp.Fori(0, B - 1) as b:
                    for g in range(G):
                        sp.wait_ge(s_full, b * H + 4 * g + 4)
                        load(b + 1, g)
                        if g:
                            sp.wait_ge(a_done, b * H + 4 * g + 4)
                            load_v(b + 1, g - 1)
                    sp.wait_ge(a_done, b * H + H + 4)
                    load_v(b + 1, G - 1)


def stage_small_output(chip, sh, qs, wo, finish):
    nc, ps = chip.nc, chip.psum
    W, G = sh.W, sh.G
    with ExitStack() as st:
        sb = lambda n, s: st.enter_context(nc.sbuf_tensor(f"{sh.tag}_{n}", s, F32))
        turned, read, inv_ok, back, att_T_ok, full, added = (
            chip.semaphore(f"{sh.tag}_{n}") for n in ("sums_turned", "turned_read", "inv_ok", "turned_back", "att_T_ok", "out_full", "out_added"))
        Q = G // 4
        rec, att, att_T = sb("inv_total", [P, 4, BANK // 32]), sb("att_rows", [P, NT, D]), sb("att_T", [P, NT, D])
        bank = lambda k: ps[:, k % 4, :]
        with nc.Block() as block:
            @block.tensor
            def _(pe):
                def sums(t):
                    for q in range(Q):
                        k = t * Q + q
                        if k >= 4:
                            pe.wait_ge(read, k - 3)
                        for i in range(4):
                            mm = pe.transpose(bank(k)[:, i * P:(i + 1) * P], qs[:, 4 * q + i, t * P:(t + 1) * P].bitcast(F32), chip.ident[:, :])
                        mm.then_inc(turned, 1)

                def turn_back(t):
                    pe.wait_ge(read, (t + 1) * Q)
                    if t >= 2:
                        pe.wait_ge(att_T_ok, t - 1)
                    for c in range(NC):
                        mm = pe.transpose(ps[:, 4 + t % 2, c * P:(c + 1) * P], att[:, t, c * P:(c + 1) * P], chip.ident[:, :])
                    mm.then_inc(back, 1)

                def project(t):
                    pe.wait_ge(att_T_ok, t + 1)
                    if t >= 4 and t % 2 == 0:
                        pe.wait_ge(added, t // 2 - 1)
                    for c in range(NC):
                        mm = pe.matmul(ps[:, 6 + t // 2 % 2, (t % 2) * D:(t % 2 + 1) * D], att_T[:, t, c * P:(c + 1) * P], wo[:, c, :], start=c == 0, stop=c == NC - 1)
                    if t % 2:
                        mm.then_inc(full, 1)

                for t in range(NT + 2):
                    if t < NT:
                        sums(t)
                    if 1 <= t <= NT:
                        turn_back(t - 1)
                    if t >= 2:
                        project(t - 2)

            @block.scalar
            def _(act):
                for t in range(NT):
                    act.wait_ge(back, t + 1)
                    act.activation(att_T[:, t, :], ps[:, 4 + t % 2, 0:D], ACT.Copy).then_inc(att_T_ok, 1)

            @block.vector
            def _(dve):
                heads = lambda k: bank(k).rearrange("p (h w) -> p h w", w=32)

                def add(n):
                    dve.wait_ge(full, n + 1)
                    finish(dve, slice(2 * n, 2 * n + 2), ps[:, 6 + n % 2, :].rearrange("p (t n) -> p t n", t=2)).then_inc(added, 1)

                for k in range(NT * Q):
                    t, q = k // Q, k % Q
                    dve.wait_ge(turned, k + 1)
                    dve.reciprocal(rec[:, k % 4, :].unsqueeze(2), heads(k)[:, :, W:W + 1]).then_inc(inv_ok, 1)
                    dve.wait_ge(inv_ok, k + 1)
                    dve.tensor_tensor(att[:, t, q * 16 * W:(q + 1) * 16 * W].rearrange("p (h w) -> p h w", w=W), heads(k)[:, :, 0:W],
                                      rec[:, k % 4, :].unsqueeze(2).to_broadcast([P, 16, W]), ALU.mult).then_inc(read, 1)
                    if q == Q - 1 and t >= 3 and t % 2:
                        add((t - 3) // 2)
                add(NT // 2 - 1)


def stage_final_norm(chip, out):
    nc = chip.nc
    with ExitStack() as st:
        sb = lambda n, s: st.enter_context(nc.sbuf_tensor(f"fin_{n}", s, F32))
        sem = lambda n: chip.semaphore(f"fin_{n}")
        bn, mv, ve, rstd = sb("bn", [P, NT, 6]), sb("mean_var", [P, NT, 2]), sb("var_eps", [P, NT]), sb("rstd", [P, NT])
        y, z = sb("y", [P, NT, D]), sb("z", [P, NT, D])
        stats, aggr, var_ok, rstd_ok, y_ok, z_ok, o_ok, stored = (sem(n) for n in ("stats", "aggr", "var_ok", "rstd_ok", "y_ok", "z_ok", "o_ok", "stored"))
        R = ROWS.index('L3_xattn_gamma')
        with nc.Block() as block:
            @block.gpsimd
            def _(pool):
                pool.wait_ge(var_ok, 1)
                pool.tensor_tensor(rstd[:, :], ve[:, :], chip.expo[:, :], ALU.pow).then_inc(rstd_ok, 1)

            @block.vector
            def _(dve):
                for j in range(NT):
                    dve.bn_stats(bn[:, j, :], chip.x[:, j, :]).then_inc(stats, 1)
                for j in range(NT):
                    dve.wait_ge(stats, j + 1)
                    dve.bn_aggr(mv[:, j, :], bn[:, j, :]).then_inc(aggr, 1)
                dve.wait_ge(aggr, NT)
                dve.tensor_scalar(ve[:, :], mv[:, :, 1], 1e-6, None, ALU.add).then_inc(var_ok, 1)
                dve.wait_ge(rstd_ok, 1)
                for j in range(NT):
                    dve.tensor_scalar(y[:, j, :], chip.x[:, j, :], mv[:, j, 0:1], rstd[:, j:j + 1], ALU.subtract, ALU.mult).then_inc(y_ok, 1)
                    if j % 2:
                        q = j // 2
                        two = slice(2 * q, 2 * q + 2)
                        dve.wait_ge(y_ok, j + 1)
                        dve.tensor_tensor(z[:, two, :], y[:, two, :], chip.rows[:, R:R + 1, :].to_broadcast([P, 2, D]), ALU.mult).then_inc(z_ok, 1)
                        dve.wait_ge(z_ok, q + 1)
                        dve.tensor_tensor(y[:, two, :], z[:, two, :], chip.rows[:, R + 1:R + 2, :].to_broadcast([P, 2, D]), ALU.add).then_inc(o_ok, 1)

            @block.sync
            def _(sp):
                for q in range(4):
                    sp.wait_ge(o_ok, q + 1)
                    sp.dma_start(tiles_of(out)[:, 2 * q:2 * q + 2, :], y[:, 2 * q:2 * q + 2, :]).then_inc(stored, 16)
                sp.wait_ge(stored, 64)


def layers_2_and_3(chip, d, out):
    nc = chip.nc
    with ExitStack() as both:
        sb = lambda n, s, t=F32: both.enter_context(nc.sbuf_tensor(n, s, t))
        ld = chip.semaphore("ld_layers23")
        w2 = {n: sb(f"l2_w{n}", [P, NC, D]) for n in 'qkvo'}
        w3 = {n: sb(f"l3_w{n}", [P, NC, L3.kv_cols if n in 'kv' else D]) for n in 'qkvo'}
        mask8 = sb("mask_bytes", [P, B * S], U8)
        gate = sb("gate", [P, 1])
        bk3, bv3 = sb("l3_bk", [L3.kv_cols, 1]), sb("l3_bv", [P, L3.kv_cols])
        aT, cT, xT = sb("ctx_normed_T", [P, NC, TOK]), sb("ctx_T", [P, NC, TOK]), sb("x_T", [P, NC, TOK])
        mask3 = sb("mask3", [P, NT, S])
        maskf, masks2 = sb("mask_f", [P, B, S]), sb("mask2", [P, B, S])

        def load(sp):
            for n in 'qkvo':
                sp.dma_start(w2[n][:, :, :], d[f'L2_xattn_W{n}_T'].rearrange("(c p) n -> p c n", p=P)).then_inc(ld, 16)
                sp.dma_start(w3[n][:, :, :], d[f'L3_xattn_W{n}'].rearrange("(c p) n -> p c n", p=P)).then_inc(ld, 16)
            sp.dma_start(mask8[:, :], d['mask_BxS2_bf1'].rearrange("(a b) s -> a (b s)", a=1).to_broadcast([P, B * S])).then_inc(ld, 16)
            sp.dma_start(gate[:, :], d['L2_xattn_gate'].rearrange("(a n) -> a n", a=1).to_broadcast([P, 1])).then_inc(ld, 16)
            sp.dma_start(bk3[:, :], d['L3_xattn_bk'].rearrange("(n a) -> n a", a=1)).then_inc(ld, 16)
            sp.dma_start(bv3[:, :], d['L3_xattn_bv'].rearrange("(a n) -> a n", a=1).to_broadcast([P, L3.kv_cols])).then_inc(ld, 16)
            sp.dma_start(mask3[:, :, :], d['mask_Bx1xSxS2_ff0'].rearrange("b a (u p) t -> p (b a u) t", p=P)).then_inc(ld, 16)
            sp.wait_ge(ld, 16 * 13)

        flat = lambda c, half: aT[:, c, half * HALF:(half + 1) * HALF].rearrange("p (b s) -> p b s", b=2)
        steps = chip.semaphore("mask_steps")

        def make_mask(dve):
            dve.wait_ge(ld, 16 * 13)
            mf = maskf[:, :, :].rearrange("p b s -> p (b s)")
            dve.tensor_copy(mf, mask8[:, :]).then_inc(steps, 1)
            dve.wait_ge(steps, 1)
            dve.tensor_scalar(mf, mf, 1.0, -BIG, ALU.subtract, ALU.mult).then_inc(steps, 1)
            dve.wait_ge(steps, 2)
            dve.tensor_scalar(masks2[:, :, :].rearrange("p b s -> p (b s)"), mf, BIG, None, ALU.mult)

        def make_gate(act):
            act.wait_ge(ld, 16 * 13)
            act.activation(gate[:, :], gate[:, :], ACT.Tanh)

        with ExitStack() as st:
            ln = LayerNorm(chip, st, "ln_ctx", chip.ctx, lambda c: chip.vec('L2_xattn_ln_gamma', c),
                           lambda c: chip.vec('L2_xattn_ln_beta', c), EPS0, plain=flat)
            run_layernorm(chip, ln, load, turns=((chip.x, xT), (chip.ctx, cT)), vector_then=make_mask, scalar_then=make_gate)

        def attend(sh, w, q_src, k_src, biases, masks, finish):
            with ExitStack() as layer:
                t = lambda n, s, dt=F32R: layer.enter_context(nc.sbuf_tensor(f"{sh.tag}_{n}", s, dt))
                qs, ks = t("q_stack", [P, sh.G, TOK]), t("k_stack", [P, sh.passes * sh.G, TOK])
                v1 = t("v_ones", [P, NT, sh.KV, 32], F32)
                with ExitStack() as compact:
                    t = lambda n, s: compact.enter_context(nc.sbuf_tensor(f"{sh.tag}_{n}", s, F32R))
                    KC = max(1, sh.kv_cols // P)
                    mem = (t("q_hi", [P, NC, TOK]), t("q_lo", [P, NC, TOK]), t("k_hi", [P, KC, TOK]), t("k_lo", [P, KC, TOK]), v1)
                    place = (compact.enter_context(nc.sbuf_tensor(f"{sh.tag}_place_q", [P, 2, sh.per_chunk, 4, sh.R, sh.W], F32R)),
                             compact.enter_context(nc.sbuf_tensor(f"{sh.tag}_place_k", [P, 3 - sh.passes, sh.per_chunk if sh.passes == 2 else sh.G, 4, sh.R, sh.W], F32R)))
                    stage_small_project(chip, sh, w['q'], w['k'], w['v'], q_src, k_src, *biases, mem, place)
                    stage_small_stack(chip, sh, mem, place, qs, ks)
                stage_small_attention(chip, sh, qs, ks, v1, masks)
                stage_small_output(chip, sh, qs, w['o'], finish)

        def gated(dve, two, o):
            return dve.scalar_tensor_tensor(chip.x[:, two, :], o, gate[:, :], chip.x[:, two, :], ALU.mult, ALU.add)

        attend(L2, w2, xT, aT, (None, None, None), masks2, gated)

        r = ROWS.index('L3_xattn_bo')
        stage_turn_and_bias(chip, chip.x, xT, chip.rows[:, r:r + 1, :], mask3)
        attend(L3, w3, xT, cT, (lambda c: chip.vec('L3_xattn_bq', c), bk3, bv3[:, :]), mask3,
               lambda dve, two, o: dve.tensor_tensor(chip.x[:, two, :], o, chip.x[:, two, :], ALU.add))
        stage_final_norm(chip, out)


def build(nc, d, out):
    with ExitStack() as stack:
        chip = Chip(nc, stack)
        with ExitStack() as l0:
            sb = lambda n, s, t=F32R: l0.enter_context(nc.sbuf_tensor(n, s, t))
            ctx_hi, ctx_lo = sb("ctxT_hi", [P, NC, TOK]), sb("ctxT_lo", [P, NC, TOK])
            h_hi, h_lo = sb("hT_hi", [P, NC, TOK]), sb("hT_lo", [P, NC, TOK])

            def ln_l0(which):
                L = f"L0_xattn_ln{which}_"
                return lambda stack, **place: LayerNorm(chip, stack, f"ln{which}", chip.x, lambda c: chip.vec(L + "scale", c),
                                                        lambda c: chip.vec(L + "offset", c), EPS0, hi=h_hi, lo=h_lo, **place)

            raw = attention_room(chip, l0)
            weights = {a: attention_weights(chip, d, a, raw) for a in (1, 2)}
            w1_raw = raw['o'][:, 0:NT, :].rearrange("p (c a) d -> p c (a d)", c=NC)
            w2_raw = raw['o'][:, NT:2 * NT, :]
            ld_w = chip.semaphore("ld_mlp")

            def load_mlp(sp):
                sp.dma_start(w1_raw, d['L0_xattn_w_fc1'].rearrange("(c p) n -> p c n", p=P)).then_inc(ld_w, 16)
                sp.dma_start(w2_raw, d['L0_xattn_w_fc2'].rearrange("(f p) n -> p f n", p=P)).then_inc(ld_w, 16)

            stage_setup(chip, d, ctx_hi, ctx_lo, ln_l0("1"), weights[1][2])
            stage_cross_attention(chip, 1, raw, weights[1], h_hi, h_lo, ctx_hi, ctx_lo, ln_l0("2"), weights[2][2])
            stage_cross_attention(chip, 2, raw, weights[2], h_hi, h_lo, ctx_hi, ctx_lo, ln_l0("_mlp"), load_mlp)
            stage_mlp(chip, w1_raw, w2_raw, ld_w, h_hi, h_lo)
        chip.renew_semaphores()
        with ExitStack() as l1:
            sb = lambda n, s: l1.enter_context(nc.sbuf_tensor(n, s, F32))
            m, load = layer1_memory(chip, l1, d)
            xe = sb("xn_T", [P, NC, B, R1])

            def ln_l1(i):
                return lambda stack, **place: LayerNorm(chip, stack, f"ln_r{i}", chip.x, lambda c: chip.vec(f'L1_xattn_ln{i}_w', c),
                                                        lambda c: chip.vec(f'L1_xattn_ln{i}_b', c), EPS0,
                                                        plain=lambda c, half: xe[:, c, 2 * half:2 * half + 2, 1:R1], **place)

            with ExitStack() as st:
                run_layernorm(chip, ln_l1(1)(st), load)
            with ExitStack() as seq:
                sq = lambda n, s: seq.enter_context(nc.sbuf_tensor(n, s, F32))
                kT, vT = sq("k_T", [P, NC, B, R1]), sq("v_T", [P, NC, B, R1])
                wT = sq("w_T", [P, NC, B, S])
                rT, gT = sq("r_T", [P, NC, TOK]), sq("g_T", [P, NC, TOK])
                stage_rwkv_mix(chip, m, xe, kT, vT, rT, wT, gT)
                stage_rwkv_scan(chip, m, kT, vT, rT, wT, gT, ln_l1(2))
            stage_channel_mix(chip, m, xe)
        chip.renew_semaphores()
        layers_2_and_3(chip, d, out)


_DIRECT = ['x', 'ctx_2048'] + [f'L0_xattn_w{n}{a}' for a in (1, 2) for n in 'qkvo'] + ['L0_xattn_w_fc1', 'L0_xattn_w_fc2']
_DIRECT += [f'L1_xattn_{n}' for n in ('maa_w1', 'maa_w2', 'decay_w1', 'decay_w2')]
_DIRECT += ['mask_BxS2_bf1', 'mask_Bx1xSxS2_ff0', 'L2_xattn_gate', 'L3_xattn_bk', 'L3_xattn_bv'] + [f'L3_xattn_W{n}' for n in 'qkvo']
_TURNED = [f'L1_xattn_{n}' for n in L1_WEIGHTS] + [f'L2_xattn_W{n}' for n in 'qkvo']


def kernel(**inputs):
    import numpy as _np
    import concourse.bacc as _bacc
    from concourse import mybir as _mybir
    from concourse.bass_utils import run_bass_kernel_spmd as _run

    laid = {n: _np.ascontiguousarray(inputs[n]) for n in _DIRECT}
    laid.update({n + '_T': _np.ascontiguousarray(_np.transpose(inputs[n])) for n in _TURNED})
    laid['vecs'] = _np.concatenate([_np.reshape(inputs[n], (-1, D)) for n in VECS]
                                   + [_np.reshape(inputs['ctx_2048'][:, i], (-1, D)) for i in range(2)], 0)
    laid['hvecs'] = _np.concatenate([_np.reshape(inputs[n], (-1, K0)) for n in HVECS + ['L0_xattn_b_fc1']], 0)
    laid['rows'] = _np.concatenate([_np.reshape(inputs[n], (-1,)) for n in ROWS], 0)
    nc = _bacc.Bacc("TRN2", target_bir_lowering=False, num_devices=1)
    arrays, d = {}, {}
    for name, a in laid.items():
        arrays[f"in_{name}"] = a
        d[name] = nc.dram_tensor(f"in_{name}", a.shape, _mybir.dt.from_np(a.dtype), kind="ExternalInput").ap()
    out = nc.dram_tensor("out_0_dram", (B, S, D), F32, kind="ExternalOutput").ap()
    build(nc, d, out)
    r = _run(nc, [arrays], core_ids=[0])
    return r.results[0]["out_0_dram"]
```
